# Optimizing a Trainium2 kernel written in Bass

```python
import numpy as np
import jax
import jax.numpy as jnp

def _softmax(x, axis=-1):
    return jax.nn.softmax(x, axis=axis)

def _gelu(x):
    return jax.nn.gelu(x, approximate=True)

def _silu(x):
    return jax.nn.silu(x)

def _sigmoid(x):
    return jax.nn.sigmoid(x)

def _layernorm(x, axis=-1, eps=1e-05):
    m = jnp.mean(x, axis=axis, keepdims=True)
    v = jnp.var(x, axis=axis, keepdims=True)
    return (x - m) / jnp.sqrt(v + eps)

def _scatter_add(tgt, idx, src, axis=0):
    return tgt.at[idx].add(src)

def _segment_sum(src, seg, n):
    return jax.ops.segment_sum(src, seg, n)
kernel_name = 'mk_vit_tower_cls_d1_tok_img256_r4_8f4661'

def setup_inputs(seed: int=0):
    np.random.seed(seed)
    _w = jnp.asarray

    def _rec_inputs():
        import jax
        import jax.numpy as jnp
        _rk = jax.random.key(seed)
        x = 7.22013e-05 + 1.00017 * jax.random.normal(jax.random.fold_in(_rk, 1), (2, 64, 64, 64), jnp.float32)
        cls_tok = 0.02 * jax.random.normal(jax.random.fold_in(_rk, 5), (1, 1, 64), jnp.float32)
        return (x, cls_tok)
    x, cls_tok = _rec_inputs()

    def _L0_tok_setup():
        import jax, jax.numpy as jnp
        import numpy as np
        B, C, H, W = (8, 64, 64, 64)
        NB = 3
        E = 64
        key = jax.random.key(seed)
        ks = jax.random.split(key, 6)
        x = jax.random.normal(ks[0], (B, C, H, W), dtype=jnp.float32)
        bases = jax.random.normal(ks[1], (C, NB), dtype=jnp.float32)
        W_spline = jax.random.normal(ks[2], (E, C * NB), dtype=jnp.float32) * (1.0 / np.sqrt(C * NB))
        b_spline = jax.random.normal(ks[3], (E,), dtype=jnp.float32) * 0.01
        W_base = jax.random.normal(ks[4], (E, C), dtype=jnp.float32) * (1.0 / np.sqrt(C))
        b_base = jax.random.normal(ks[5], (E,), dtype=jnp.float32) * 0.01
        return {'x': x, 'bases': bases, 'W_spline': W_spline, 'b_spline': b_spline, 'W_base': W_base, 'b_base': b_base}
    _L0_tok_all = _L0_tok_setup()
    _L0_tok_in = {k: v for k, v in _L0_tok_all.items() if k in ('bases', 'W_spline', 'b_spline', 'W_base', 'b_base')}
    del _L0_tok_all

    def _L0_attn_setup():
        import jax, jax.numpy as jnp
        import numpy as np
        WS = 7
        CT = 2
        H = 8
        C = 64
        B = 1024
        WS2 = WS * WS
        N = WS2 + CT * CT
        HD = C // H

        def _relative_position_index():
            coords = np.arange(WS)
            cc = np.stack(np.meshgrid(coords, coords, indexing='ij'))
            cc = cc.reshape(2, -1)
            rel = cc[:, :, None] - cc[:, None, :]
            rel = rel.transpose(1, 2, 0).copy()
            rel[:, :, 0] += WS - 1
            rel[:, :, 1] += WS - 1
            rel[:, :, 0] *= 2 * WS - 1
            return jnp.asarray(rel.sum(-1).reshape(-1), dtype=jnp.int32)
        key = jax.random.key(seed)
        k1, k2, k3, k4, k5 = jax.random.split(key, 5)
        s = 0.02
        return {'x': jax.random.normal(k1, (B, N, C), dtype=jnp.float32), 'w_qkv': jax.random.normal(k2, (3 * C, C), dtype=jnp.float32) * s, 'w_proj': jax.random.normal(k3, (C, C), dtype=jnp.float32) * s, 'b_proj': jax.random.normal(k4, (C,), dtype=jnp.float32) * s, 'rel_table': jax.random.normal(k5, ((2 * WS - 1) ** 2, H), dtype=jnp.float32) * s, 'rel_index': _relative_position_index()}
    _L0_attn_all = _L0_attn_setup()
    _L0_attn_in = {k: v for k, v in _L0_attn_all.items() if k in ('w_qkv', 'w_proj', 'b_proj', 'rel_table', 'rel_index')}
    del _L0_attn_all

    def _L0_ffn_setup():
        import jax, jax.numpy as jnp
        import numpy as np
        D_IN, D_HID, D_OUT = (64, 128, 64)
        N_EXPERTS, TOP_K = (64, 2)
        B, S = (8, 1024)
        key = jax.random.key(seed)
        ks = jax.random.split(key, 8)
        scale_in = 1.0 / np.sqrt(D_IN)
        scale_hid = 1.0 / np.sqrt(D_HID)
        return {'x': jax.random.normal(ks[0], (B, S, D_IN), dtype=jnp.float32), 'Wr': jax.random.uniform(ks[1], (D_IN, N_EXPERTS), jnp.float32, -scale_in, scale_in), 'br': jax.random.uniform(ks[2], (N_EXPERTS,), jnp.float32, -scale_in, scale_in), 'W1': jax.random.uniform(ks[3], (N_EXPERTS, D_IN, D_HID), jnp.float32, -scale_in, scale_in), 'b1': jax.random.uniform(ks[4], (N_EXPERTS, D_HID), jnp.float32, -scale_in, scale_in), 'W2': jax.random.uniform(ks[5], (N_EXPERTS, D_HID, D_OUT), jnp.float32, -scale_hid, scale_hid), 'b2': jax.random.uniform(ks[6], (N_EXPERTS, D_OUT), jnp.float32, -scale_hid, scale_hid)}
    _L0_ffn_all = _L0_ffn_setup()
    _L0_ffn_in = {k: v for k, v in _L0_ffn_all.items() if k in ('Wr', 'br', 'W1', 'b1', 'W2', 'b2')}
    del _L0_ffn_all
    return {'x': x, 'cls_tok': cls_tok, 'L0_tok_bases': _L0_tok_in['bases'], 'L0_tok_W_spline': _L0_tok_in['W_spline'], 'L0_tok_b_spline': _L0_tok_in['b_spline'], 'L0_tok_W_base': _L0_tok_in['W_base'], 'L0_tok_b_base': _L0_tok_in['b_base'], 'L0_attn_w_qkv': _L0_attn_in['w_qkv'], 'L0_attn_w_proj': _L0_attn_in['w_proj'], 'L0_attn_b_proj': _L0_attn_in['b_proj'], 'L0_attn_rel_table': _L0_attn_in['rel_table'], 'L0_attn_rel_index': _L0_attn_in['rel_index'], 'L0_ffn_Wr': _L0_ffn_in['Wr'], 'L0_ffn_br': _L0_ffn_in['br'], 'L0_ffn_W1': _L0_ffn_in['W1'], 'L0_ffn_b1': _L0_ffn_in['b1'], 'L0_ffn_W2': _L0_ffn_in['W2'], 'L0_ffn_b2': _L0_ffn_in['b2']}

def reference(x, cls_tok, L0_tok_bases, L0_tok_W_spline, L0_tok_b_spline, L0_tok_W_base, L0_tok_b_base, L0_attn_w_qkv, L0_attn_w_proj, L0_attn_b_proj, L0_attn_rel_table, L0_attn_rel_index, L0_ffn_Wr, L0_ffn_br, L0_ffn_W1, L0_ffn_b1, L0_ffn_W2, L0_ffn_b2):
    import jax
    import jax.numpy as jnp

    def _L0_tok_ref(x, bases, W_spline, b_spline, W_base, b_base):
        import jax, jax.numpy as jnp
        import numpy as np
        B, C, H, W = (8, 64, 64, 64)
        NB = 3
        E = 64
        b, c, h, w = x.shape
        x_flat = jnp.transpose(x.reshape(b, c, h * w), (0, 2, 1))
        base_out = jnp.einsum('blc,ec->ble', jax.nn.silu(x_flat), W_base) + b_base
        spline = jax.nn.sigmoid(x_flat[..., None] * bases[None, None, :, :])
        spline_flat = spline.reshape(b, h * w, c * bases.shape[1])
        spline_proj = jnp.einsum('blk,ek->ble', spline_flat, W_spline) + b_spline
        return base_out + spline_proj

    def _L0_attn_ref(x, w_qkv, w_proj, b_proj, rel_table, rel_index):
        import jax, jax.numpy as jnp
        import numpy as np
        WS = 7
        CT = 2
        H = 8
        C = 64
        B = 1024
        WS2 = WS * WS
        N = WS2 + CT * CT
        HD = C // H

        def _relative_position_index():
            coords = np.arange(WS)
            cc = np.stack(np.meshgrid(coords, coords, indexing='ij'))
            cc = cc.reshape(2, -1)
            rel = cc[:, :, None] - cc[:, None, :]
            rel = rel.transpose(1, 2, 0).copy()
            rel[:, :, 0] += WS - 1
            rel[:, :, 1] += WS - 1
            rel[:, :, 0] *= 2 * WS - 1
            return jnp.asarray(rel.sum(-1).reshape(-1), dtype=jnp.int32)
        b, n, c = x.shape
        scale = HD ** (-0.5)
        qkv = jnp.einsum('bnc,dc->bnd', x, w_qkv).reshape(b, n, 3, H, HD)
        qkv = jnp.moveaxis(qkv, 2, 0)
        q, k, v = (qkv[0], qkv[1], qkv[2])
        attn = jnp.einsum('bnhd,bmhd->bhnm', q, k) * scale
        bias = rel_table[rel_index].reshape(WS2, WS2, H).transpose(2, 0, 1)
        pad = n - WS2
        bias = jnp.pad(bias, ((0, 0), (pad, 0), (pad, 0)))
        attn = jax.nn.softmax(attn + bias[None], axis=-1)
        out = jnp.einsum('bhnm,bmhd->bnhd', attn, v).reshape(b, n, c)
        return jnp.einsum('bnc,dc->bnd', out, w_proj) + b_proj

    def _L0_ffn_ref(x, Wr, br, W1, b1, W2, b2):
        import jax, jax.numpy as jnp
        import numpy as np
        D_IN, D_HID, D_OUT = (64, 128, 64)
        N_EXPERTS, TOP_K = (64, 2)
        B, S = (8, 1024)
        Bx, Sx, D = x.shape
        xf = x.reshape(-1, D)
        T = xf.shape[0]
        E = Wr.shape[1]
        logits = xf @ Wr + br
        topk_logits, topk_idx = jax.lax.top_k(logits, TOP_K)
        gates = jax.nn.softmax(topk_logits, axis=1)
        combine = jnp.zeros((T, E), xf.dtype).at[jnp.arange(T)[:, None], topk_idx].add(gates)
        out = jnp.zeros((T, W2.shape[-1]), xf.dtype)
        for e in range(E):
            h = jax.nn.relu(xf @ W1[e] + b1[e])
            y = h @ W2[e] + b2[e]
            out = out + combine[:, e:e + 1] * y
        return out.reshape(Bx, Sx, -1)
    h = _L0_tok_ref(x, L0_tok_bases, L0_tok_W_spline, L0_tok_b_spline, L0_tok_W_base, L0_tok_b_base)
    h = jnp.concatenate([jnp.broadcast_to(cls_tok, (h.shape[0], 1, h.shape[2])), h], axis=1)
    h = h + _L0_attn_ref(_layernorm(h, axis=-1), L0_attn_w_qkv, L0_attn_w_proj, L0_attn_b_proj, L0_attn_rel_table, L0_attn_rel_index)
    h = h + _L0_ffn_ref(_layernorm(h, axis=-1), L0_ffn_Wr, L0_ffn_br, L0_ffn_W1, L0_ffn_b1, L0_ffn_W2, L0_ffn_b2)
    return h

_drawn_inputs = setup_inputs


def setup_inputs(seed=0):
    import zlib

    import numpy as np

    out = dict(_drawn_inputs(seed))
    spreads = {}
    factors = {'cls_tok': 64.0, 'L0_attn_rel_table': 64.0}
    for name, (base, spread) in spreads.items():
        noise = np.random.default_rng([zlib.crc32(name.encode()), seed]).standard_normal(out[name].shape)
        drawn = base * np.exp(spread * noise) if base else spread * noise
        out[name] = jnp.asarray(drawn.astype(out[name].dtype))
    for name, factor in factors.items():
        out[name] = (out[name] * factor).astype(out[name].dtype)
    return out
```

```python
import struct
from contextlib import ExitStack

import concourse.bass as bass
from concourse import mybir

ALU = mybir.AluOpType
ACT = mybir.ActivationFunctionType
AX = mybir.AxisListType
F32 = mybir.dt.float32
BF16 = mybir.dt.bfloat16
I32 = mybir.dt.int32
U32 = mybir.dt.uint32
RMAX = bass.bass_isa.ReduceOp.max

P = 128
C = 64
H = 8
HD = C // H
NB = 3
B = 2
PATCHES = 64 * 64
N = PATCHES + 1
TQ = 114
CT = 4
CH = TQ * CT
NCH = 9
NT = NCH * CT
NP = NCH * CH
LASTX = PATCHES - (NCH - 1) * CH
KB = 33
KP = KB * P
KG = 3
NG = KB // KG
WS2 = 49
WIN0 = PATCHES - WS2
TABLE = 169
WIN_COLS = -(-WS2 * WS2 // P)
PARTS = 3
SROWS = PARTS * PARTS * HD
STACK = SROWS + PARTS
EPS = 1e-5
TWO_ONES = struct.unpack('<f', struct.pack('<I', 0x3F803F80))[0]
EXPERTS = 64
TOP = 2
HID = 128
B1_ROW = C
B2_ROW = 96
PACK = HID + C
BLOCKS = (B * NT * TQ * TOP + EXPERTS * (P - 1)) // P + 1
BLOCKS += -BLOCKS % 8
EXPERT_STEPS = 36
SAFE = 30.0



def after(c):
    return c + 2


def before(c):
    return c + 1


def vit_layer(nc, ins, out):
    ctx = ExitStack()
    with ctx:
        def keep(name, shape, dt=F32):
            return ctx.enter_context(nc.sbuf_tensor(name, shape, dt))

        def dram(name, shape, dt=F32):
            return nc.dram_tensor(name, shape, dt).ap()

        t = {}
        t["h"] = keep("h", [P, B * NT, C])
        t["identity"] = keep("identity", [P, P])
        t["wprojT"] = keep("wprojT", [C, C])
        t["window"] = keep("window", [WS2, H, WS2])
        t["qk_parts"] = dram("qk_parts", (B, PARTS, P, NP), BF16)
        t["v_rows"] = dram("v_rows", (B, KP, C))
        t["q_squares"] = dram("q_squares", (B * H, NP))
        t["head_tops"] = dram("head_tops", (2, B * H))
        t["window_rows"] = dram("window_rows", (P * WIN_COLS, H))
        t["shift_parts"] = dram("shift_parts", (B * H, PARTS, NP), BF16)
        t["row_max"] = dram("row_max", (B * H, KP))
        t["slot_x"] = dram("slot_x", (P, BLOCKS, C))
        t["slot_y"] = dram("slot_y", (P, BLOCKS, C))
        t["weights"] = dram("weights", (EXPERTS, P, PACK))
        embed_and_project(nc, ins, t)
        settle_shifts(nc, ins, t)
        t["attn"] = keep("attn", [P, B * NT, C])
        attend(nc, ins, t)
        t["normed"] = keep("normed", [P, B * NT, C])
        t["rows"] = keep("rows", [P, B * NT, TOP], I32)
        t["gates"] = keep("gates", [P, B * NT, TOP])
        t["expert_of"] = dram("expert_of", (BLOCKS,), I32)
        route(nc, ins, t)
        run_experts(nc, ins, t)
        combine(nc, t, out)


def embed_and_project(nc, ins, t):
    ctx = ExitStack()
    with ctx:
        ctx.enter_context(nc.cleanup_on_exit())
        def sb(name, shape, dt=F32):
            return ctx.enter_context(nc.sbuf_tensor(name, shape, dt))

        def ps(name, shape, dt=F32):
            return ctx.enter_context(nc.psum_tensor(name, shape, dt))

        def sem(name):
            return nc.alloc_semaphore(name)

        def pair(name):
            return [sem(f"{name}{b}") for b in range(B)]

        h, identity, wprojT, window = (t[k] for k in ("h", "identity", "wprojT", "window"))

        spl_raw = sb("spl_raw", [C, C, NB])
        base_raw = sb("base_raw", [C, C])
        mix_raw = sb("mix_raw", [C, 2, 2, C])
        qkv_raw = sb("qkv_raw", [C, 3, C])
        proj_raw = sb("proj_raw", [C, C])
        mixT = sb("mixT", [P, 2, C])
        qkvT = sb("qkvT", [C, 3 * C])
        bases = sb("bases", [P, NB])
        slope = sb("slope", [P, 2])
        bias_spline = sb("bias_spline", [P, C])
        bias_base = sb("bias_base", [P, C])
        bias_e = sb("bias_e", [P, C])
        table = sb("table", [H, TABLE])
        table_max = sb("table_max", [H, 1])
        heads_f = sb("heads_f", [P, 2, H])
        heads_of = sb("heads_of", [P, 2, H], BF16)
        qscale = sb("qscale", [P, 1])
        power = sb("power", [P, CT])
        x2 = sb("x2", [P, B, PATCHES])
        feat = sb("feat", [P, B, 2, CH])
        total = sb("total", [P, B, CT])
        neg_mean = sb("neg_mean", [P, B, CT])
        centred = sb("centred", [P, B, CT, C])
        square = sb("square", [P, B, CT, C])
        variance = sb("variance", [P, B, CT])
        var_eps = sb("var_eps", [P, B, CT])
        rstd = sb("rstd", [P, B, CT])
        xn = sb("xn", [P, B, CT, C])
        xnT = sb("xnT", [C, B, CH])
        qk = sb("qk", [P, B, CH])
        rest1 = sb("rest1", [P, B, CH])
        rest2 = sb("rest2", [P, B, CH])
        qksq = sb("qksq", [P, B, CH], BF16)
        qkp = sb("qkp", [P, B, PARTS, CH], BF16)
        vout = sb("vout", [P, B, CT, C])
        zeros = sb("zeros", [P, C])
        kn = sb("kn", [H, B, NCH])
        kmax = sb("kmax", [H, B])
        qn = sb("qn", [H, B, CH])
        win_index = sb("win_index", [P, WIN_COLS], I32)
        win_bias = sb("win_bias", [P, WIN_COLS, H])
        win_raw = sb("win_raw", [WS2, WS2, H])

        ps_h = ps("ps_h", [P, B, 512])
        ps_qk = ps("ps_qk", [P, B, 512])
        ps_n = ps("ps_n", [H, 2, 512])
        ps_t = ps("ps_t", [P, 512])
        ps_v = ps("ps_v", [P, 512])

        w_in, ident, turned, turned_out, consts = (sem(n) for n in ("w_in", "ident", "turned", "turned_out", "consts"))
        packed = sem("packed")
        x_in = pair("x_in")
        feat_done, silu_done, mixed, h_done = pair("feat_done"), pair("silu_done"), pair("mixed"), pair("h_done")
        sum_done, mean_done, centre_done, square_done = (pair(n) for n in ("sum_done", "mean_done", "centre_done", "square_done"))
        var_done, eps_done, rstd_done, norm_done = (pair(n) for n in ("var_done", "eps_done", "rstd_done", "norm_done"))
        xnT_ps, xnT_done, qk_ps, v_ps, n_ps = (pair(n) for n in ("xnT_ps", "xnT_done", "qk_ps", "v_ps", "n_ps"))
        qk_done, qksq_done, v_done, qn_done, kn_done = (pair(n) for n in ("qk_done", "qksq_done", "v_done", "qn_done", "kn_done"))
        hi_done, rest1_done, mid_done, rest2_done, parts_done = (pair(n) for n in ("hi_done", "rest1_done", "mid_done", "rest2_done", "parts_done"))
        parts_out, v_out = pair("parts_out"), pair("v_out")
        padded, cls_in, zeroed, v_pad, held, packed_raw = (
            sem(n) for n in ("padded", "cls_in", "zeroed", "v_pad", "held", "packed_raw"))
        kmax_done, table_done, tops_out = (sem(n) for n in ("kmax_done", "table_done", "tops_out"))
        qn_out = pair("qn_out")
        index_clear, index_in, gathered, rows_out, window_in = (
            sem(n) for n in ("index_clear", "index_in", "gathered", "rows_out", "window_in"))

        xflat = ins["x"].rearrange("b c a w -> b c (a w)")
        cls_row = ins["cls_tok"].rearrange("a b c -> (a b) c")
        LOADS = 9
        TURNS = 6
        CLS_ROW = PATCHES - (NT - 1) * TQ

        block = ctx.enter_context(nc.Block())

        def chunks(eng, body):
            with eng.Fori(0, NCH - 1) as c:
                body(c, CH)
            body(NCH - 1, LASTX)

        @block.sync
        def _(sp):
            def load(dst, src):
                sp.dma_start(dst, src).then_inc(w_in, 16)

            for b in range(B):
                for s in (parts_out, v_out, qn_out):
                    sp.sem_inc(s[b], 16)
            load(spl_raw[:], ins["L0_tok_W_spline"].rearrange("e (c k) -> e c k", k=NB))
            load(base_raw[:], ins["L0_tok_W_base"])
            for half in range(2):
                load(bases[C * half:C * half + C, :], ins["L0_tok_bases"])
            for half in range(2):
                sp.dma_start(x2[C * half:C * half + C, 0, :], xflat[0]).then_inc(x_in[0], 16)
            load(qkv_raw[:], ins["L0_attn_w_qkv"].rearrange("(s e) c -> e s c", s=3))
            load(proj_raw[:], ins["L0_attn_w_proj"])
            load(bias_spline[:], ins["L0_tok_b_spline"].partition_broadcast(P))
            load(bias_base[:], ins["L0_tok_b_base"].partition_broadcast(P))
            for half in range(2):
                sp.dma_start(x2[C * half:C * half + C, 1, :], xflat[1]).then_inc(x_in[1], 16)
            with nc.allow_non_contiguous_dma(reason="a table of 169 x 8, once"):
                load(table[:], ins["L0_attn_rel_table"].rearrange("r h -> h r"))
            sp.wait_ge(padded, 1)
            for b in range(B):
                sp.dma_start(h[CLS_ROW:CLS_ROW + 1, b * NT + NT - 1, :], cls_row).then_inc(cls_in, 16)
            sp.wait_ge(zeroed, 1)
            for b in range(B):
                sp.dma_start(t["v_rows"][b, NP:KP, :], zeros[0:KP - NP, :]).then_inc(v_pad, 16)

            def store(c, n):
                for b in range(B):
                    sp.wait_ge(parts_done[b], after(c))
                    sp.sem_inc(held, 1)
                    sp.dma_start(t["qk_parts"][b][:, :, bass.ds(c * CH, CH)].rearrange("s p n -> p s n"),
                                 qkp[:, b]).then_inc(parts_out[b], 16)
                    sp.wait_ge(v_done[b], after(c))
                    sp.sem_inc(held, 1)
                    sp.dma_start(t["v_rows"][b][bass.ds(c * CH, CH), :].rearrange("(i p) e -> p i e", p=TQ),
                                 vout[0:TQ, b]).then_inc(v_out[b], 16)
                    sp.wait_ge(qn_done[b], after(c))
                    sp.sem_inc(held, 1)
                    sp.dma_start(t["q_squares"][b * H:b * H + H, bass.ds(c * CH, CH)], qn[:, b]).then_inc(qn_out[b], 16)
            chunks(sp, store)
            sp.wait_ge(kmax_done, B)
            for b in range(B):
                sp.dma_start(t["head_tops"][0:1, b * H:b * H + H].rearrange("a h -> h a"), kmax[:, b:b + 1]).then_inc(tops_out, 16)
            sp.wait_ge(table_done, 1)
            for b in range(B):
                sp.dma_start(t["head_tops"][1:2, b * H:b * H + H].rearrange("a h -> h a"), table_max[:]).then_inc(tops_out, 16)
            sp.wait_ge(gathered, 16 * WIN_COLS)
            sp.dma_start(t["window_rows"].rearrange("(p r) h -> p (r h)", p=P),
                         win_bias[:].rearrange("p r h -> p (r h)")).then_inc(rows_out, 16)
            sp.wait_ge(rows_out, 16)
            sp.dma_start(win_raw[:].rearrange("n m h -> n (m h)"),
                         t["window_rows"][0:WS2 * WS2, :].rearrange("(n m) h -> n (m h)", m=WS2)).then_inc(window_in, 16)
            sp.wait_ge(v_pad, 16 * B)
            for b in range(B):
                sp.wait_ge(parts_out[b], 16 * (NCH + 1))
                sp.wait_ge(v_out[b], 16 * (NCH + 1))
                sp.wait_ge(qn_out[b], 16 * (NCH + 1))
            sp.wait_ge(tops_out, 16 * 2 * B)

        @block.gpsimd
        def _(pool):
            for b in range(B):
                for s in (eps_done, rstd_done):
                    pool.sem_inc(s[b], 1)
            nc.gpsimd.memset(identity[:], 0.0).then_inc(ident, 1)
            pool.wait_ge(ident, 1)
            nc.gpsimd.affine_select(out=identity[:], in_=identity[:], compare_op=ALU.not_equal, fill=1.0, base=0,
                                    pattern=[[-1, P]], channel_multiplier=1).then_inc(ident, 1)
            nc.gpsimd.memset(power[:], -0.5).then_inc(consts, 1)
            nc.gpsimd.memset(win_index[:], 0).then_inc(index_clear, 1)
            pool.wait_ge(index_clear, 1)
            whole = WS2 * WS2 // WIN_COLS
            index = ins["L0_attn_rel_index"]
            pool.dma_start(win_index[0:whole, :], index[0:whole * WIN_COLS].rearrange("(p r) -> p r", r=WIN_COLS)).then_inc(index_in, 16)
            pool.dma_start(win_index[whole:whole + 1, 0:WS2 * WS2 - whole * WIN_COLS],
                           index[whole * WIN_COLS:WS2 * WS2].rearrange("(p r) -> p r", p=1)).then_inc(index_in, 16)
            pool.wait_ge(index_in, 32)
            for r in range(WIN_COLS):
                nc.gpsimd.indirect_dma_start(out=win_bias[:, r, :], out_offset=None, in_=ins["L0_attn_rel_table"],
                                             in_offset=bass.IndirectOffsetOnAxis(ap=win_index[:, r:r + 1], axis=0)).then_inc(gathered, 16)
            nc.gpsimd.memset(heads_f[:], 1.0).then_inc(consts, 1)
            pool.wait_ge(consts, 2)
            nc.gpsimd.affine_select(out=heads_f[:], in_=heads_f[:], compare_op=ALU.is_ge, fill=0.0, base=0,
                                    pattern=[[-C, 2], [-HD, H]], channel_multiplier=1).then_inc(consts, 1)
            pool.wait_ge(consts, 3)
            nc.gpsimd.affine_select(out=heads_f[:], in_=heads_f[:], compare_op=ALU.is_ge, fill=0.0, base=HD - 1,
                                    pattern=[[C, 2], [HD, H]], channel_multiplier=-1).then_inc(consts, 1)

            def step(c, n):
                for b in range(B):
                    pool.wait_ge(var_done[b], after(c))
                    pool.sem_inc(held, 1)
                    nc.gpsimd.tensor_scalar(var_eps[0:TQ, b], variance[0:TQ, b], 1.0 / C, EPS, ALU.mult,
                                            ALU.add).then_inc(eps_done[b], 1)
                    pool.wait_ge(eps_done[b], after(c))
                    nc.gpsimd.tensor_tensor(out=rstd[0:TQ, b], in0=var_eps[0:TQ, b], in1=power[0:TQ],
                                            op=ALU.pow).then_inc(rstd_done[b], 1)
            chunks(pool, step)

        @block.scalar
        def _(act):
            for b in range(B):
                for s in (feat_done, xnT_done, qk_done, qksq_done, v_done, qn_done):
                    act.sem_inc(s[b], 1)
            act.wait_ge(packed, 2)
            for b in range(B):
                act.wait_ge(x_in[b], 32)

            def step(c, n):
                for b in range(B):
                    act.wait_ge(mixed[b], before(c))
                    act.wait_ge(silu_done[b], before(c))
                    for f in range(2):
                        last = nc.scalar.activation(feat[:, b, f, 0:n], x2[:, b, bass.ds(c * CH, n)], ACT.Sigmoid,
                                                    scale=slope[:, f:f + 1])
                    last.then_inc(feat_done[b], 1)
                for b in range(B):
                    act.wait_ge(xnT_ps[b], after(c))
                    act.wait_ge(v_ps[b], before(c))
                    nc.scalar.copy(xnT[:, b], ps_t[0:C, 0:CH]).then_inc(xnT_done[b], 1)
                    act.wait_ge(qk_ps[b], after(c))
                    act.wait_ge(parts_done[b], before(c))
                    act.wait_ge(qksq_done[b], before(c))
                    nc.scalar.activation(qk[:, b], ps_qk[:, b, 0:CH], ACT.Copy, scale=qscale[:]).then_inc(qk_done[b], 1)
                    act.wait_ge(qk_done[b], after(c))
                    act.wait_ge(n_ps[b], before(c))
                    nc.scalar.activation(qksq[:, b], qk[:, b], ACT.Square).then_inc(qksq_done[b], 1)
                    act.wait_ge(v_ps[b], after(c))
                    act.wait_ge(v_out[b], 16 * before(c))
                    nc.scalar.copy(vout[0:TQ, b].rearrange("p i e -> p (i e)"), ps_v[0:TQ, 0:CT * C]).then_inc(v_done[b], 1)
                    act.wait_ge(n_ps[b], after(c))
                    act.wait_ge(qn_out[b], 16 * before(c))
                    nc.scalar.copy(qn[:, b], ps_n[:, 0, 0:CH]).then_inc(qn_done[b], 1)
            chunks(act, step)

        @block.vector
        def _(dve):
            for b in range(B):
                for s in (silu_done, h_done, sum_done, mean_done, centre_done, square_done, var_done, norm_done, hi_done,
                          rest1_done, mid_done, rest2_done, parts_done, kn_done):
                    dve.sem_inc(s[b], 1)
            nc.vector.memset(zeros[:], 0.0).then_inc(zeroed, 1)
            for b in range(B):
                last = nc.vector.memset(h[96:TQ, b * NT + NT - 1, :], 0.0)
            last.then_inc(padded, 1)
            dve.wait_ge(w_in, 16 * LOADS)
            for f, half, src in ((0, 0, spl_raw[:, :, 0]), (0, 1, spl_raw[:, :, 1]), (1, 0, spl_raw[:, :, 2]),
                                 (1, 1, base_raw[:])):
                nc.vector.tensor_copy(mix_raw[:, f, half, :], src).then_inc(packed_raw, 1)
            nc.vector.tensor_copy(slope[0:C, 0:1], bases[0:C, 0:1])
            nc.vector.tensor_copy(slope[C:P, 0:1], bases[C:P, 1:2])
            nc.vector.tensor_copy(slope[0:C, 1:2], bases[0:C, 2:3])
            nc.vector.memset(slope[C:P, 1:2], 1.0).then_inc(packed, 1)
            nc.vector.memset(qscale[C:P, :], 1.0)
            nc.vector.memset(qscale[0:C, :], float(HD) ** -0.5).then_inc(packed, 1)
            nc.vector.tensor_tensor(bias_e[:], bias_spline[:], bias_base[:], ALU.add).then_inc(packed, 1)
            nc.vector.tensor_reduce(table_max[:], table[:], AX.X, ALU.max).then_inc(packed, 1)
            dve.wait_ge(consts, 4)
            nc.vector.tensor_copy(heads_of[:], heads_f[:]).then_inc(packed, 1)
            for n, (dst, src) in enumerate(((mixT[:, 0, :], ps_t[:, 0:C]), (mixT[:, 1, :], ps_t[:, C:2 * C]),
                                            (qkvT[:, 0:C], ps_t[0:C, 2 * C:3 * C]), (qkvT[:, C:2 * C], ps_t[0:C, 3 * C:4 * C]),
                                            (qkvT[:, 2 * C:], ps_t[0:C, 4 * C:5 * C]), (wprojT[:], ps_t[0:C, 5 * C:6 * C]))):
                dve.wait_ge(turned, 1)
                nc.vector.tensor_copy(dst, src).then_inc(turned_out, 1)
            dve.wait_ge(padded, 1)
            dve.wait_ge(packed, 5)

            def step(c, n):
                for b in range(B):
                    dve.wait_ge(feat_done[b], after(c))
                    nc.vector.tensor_tensor(feat[C:P, b, 1, 0:n], feat[C:P, b, 1, 0:n], x2[C:P, b, bass.ds(c * CH, n)],
                                            ALU.mult).then_inc(silu_done[b], 1)
                for b in range(B):
                    tile = b * NT + c * CT
                    full = n // TQ
                    dve.wait_ge(mixed[b], after(c))
                    dst = h[0:TQ, bass.ds(tile, full), :]
                    psv = ps_h[:, b, 0:CT * C].rearrange("p (i e) -> p i e", e=C)
                    over = bias_e[0:TQ].unsqueeze(1).to_broadcast([TQ, full, C])
                    last = nc.vector.tensor_tensor(dst, psv[0:TQ, 0:full], over, ALU.add)
                    if full < CT:
                        rows = n - full * TQ
                        last = nc.vector.tensor_tensor(h[0:rows, tile + full, :], psv[0:rows, full], bias_e[0:rows], ALU.add)
                        dve.wait_ge(cls_in, 16 * B)
                    last.then_inc(h_done[b], 1)
                    tok = h[0:TQ, bass.ds(tile, CT), :]
                    dve.wait_ge(h_done[b], after(c))
                    dve.sem_inc(held, 1)
                    nc.vector.tensor_reduce(total[0:TQ, b], tok, AX.X, ALU.add).then_inc(sum_done[b], 1)
                    dve.wait_ge(sum_done[b], after(c))
                    nc.vector.tensor_scalar(neg_mean[0:TQ, b], total[0:TQ, b], -1.0 / C, None, ALU.mult).then_inc(mean_done[b], 1)
                    dve.wait_ge(mean_done[b], after(c))
                    nc.vector.tensor_tensor(centred[0:TQ, b], tok, neg_mean[0:TQ, b].unsqueeze(2).to_broadcast([TQ, CT, C]),
                                            ALU.add).then_inc(centre_done[b], 1)
                    dve.wait_ge(centre_done[b], after(c))
                    nc.vector.tensor_tensor(square[0:TQ, b], centred[0:TQ, b], centred[0:TQ, b], ALU.mult).then_inc(square_done[b], 1)
                    dve.wait_ge(square_done[b], after(c))
                    nc.vector.tensor_reduce(variance[0:TQ, b], square[0:TQ, b], AX.X, ALU.add).then_inc(var_done[b], 1)
                for b in range(B):
                    dve.wait_ge(rstd_done[b], after(c))
                    dve.wait_ge(xnT_ps[b], before(c))
                    nc.vector.tensor_tensor(xn[0:TQ, b], centred[0:TQ, b], rstd[0:TQ, b].unsqueeze(2).to_broadcast([TQ, CT, C]),
                                            ALU.mult).then_inc(norm_done[b], 1)
                for b in range(B):
                    dve.wait_ge(qk_done[b], after(c))
                    dve.wait_ge(parts_out[b], 16 * before(c))
                    nc.vector.tensor_copy(qkp[:, b, 0], qk[:, b]).then_inc(hi_done[b], 1)
                    dve.wait_ge(hi_done[b], after(c))
                    nc.vector.tensor_tensor(rest1[:, b], qk[:, b], qkp[:, b, 0], ALU.subtract).then_inc(rest1_done[b], 1)
                    dve.wait_ge(rest1_done[b], after(c))
                    nc.vector.tensor_copy(qkp[:, b, 1], rest1[:, b]).then_inc(mid_done[b], 1)
                    dve.wait_ge(mid_done[b], after(c))
                    nc.vector.tensor_tensor(qkp[:, b, 2], rest1[:, b], qkp[:, b, 1], ALU.subtract).then_inc(parts_done[b], 1)
                    dve.wait_ge(n_ps[b], after(c))
                    dve.sem_inc(held, 1)
                    nc.vector.tensor_reduce(kn[:, b, bass.ds(c, 1)], ps_n[:, 1, 0:CH], AX.X, ALU.max).then_inc(kn_done[b], 1)
            chunks(dve, step)
            for b in range(B):
                dve.wait_ge(kn_done[b], after(NCH - 1))
                nc.vector.tensor_reduce(kmax[:, b:b + 1], kn[:, b], AX.X, ALU.max).then_inc(kmax_done, 1)
            nc.vector.tensor_scalar(table_max[:], table_max[:], 0.0, None, ALU.max).then_inc(table_done, 1)
            dve.wait_ge(window_in, 16)
            nc.vector.tensor_copy(window[:], win_raw[:].rearrange("n m h -> n h m")).then_inc(table_done, 1)

        @block.tensor
        def _(pe):
            for b in range(B):
                for s in (mixed, xnT_ps, qk_ps, v_ps, n_ps):
                    pe.sem_inc(s[b], 1)
            pe.wait_ge(ident, 2)
            pe.wait_ge(w_in, 16 * LOADS)
            pe.wait_ge(packed_raw, 4)
            eye = identity[0:C, 0:C]
            for f in range(2):
                nc.tensor.transpose(ps_t[:, C * f:C * f + C], mix_raw[:, f].rearrange("e a c -> e (a c)"), eye)
            for s in range(3):
                nc.tensor.transpose(ps_t[0:C, C * (2 + s):C * (3 + s)], qkv_raw[:, s, :], eye)
            nc.tensor.transpose(ps_t[0:C, 5 * C:6 * C], proj_raw[:], eye).then_inc(turned, 1)
            pe.wait_ge(turned_out, TURNS)
            pe.wait_ge(packed, 5)

            def step(c, n):
                for b in range(B):
                    pe.wait_ge(silu_done[b], after(c))
                    pe.wait_ge(h_done[b], before(c))
                    for i in range(CT):
                        rows = min(TQ, n - i * TQ)
                        for f in range(2):
                            last = nc.tensor.matmul(ps_h[0:rows, b, C * i:C * i + C], feat[:, b, f, TQ * i:TQ * i + rows],
                                                    mixT[:, f, :], start=(f == 0), stop=(f == 1))
                    last.then_inc(mixed[b], 1)
                for b in range(B):
                    pe.wait_ge(norm_done[b], after(c))
                    pe.wait_ge(xnT_done[1 - b], after(c) if b else before(c))
                    pe.sem_inc(held, 1)
                    for i in range(CT):
                        last = nc.tensor.transpose(ps_t[0:C, TQ * i:TQ * i + TQ], xn[0:TQ, b, i, :], identity[0:TQ, 0:TQ])
                    last.then_inc(xnT_ps[b], 1)
                    pe.wait_ge(xnT_done[b], after(c))
                    pe.wait_ge(qk_done[b], before(c))
                    nc.tensor.matmul(ps_qk[:, b, 0:CH], qkvT[:, 0:2 * C], xnT[:, b], start=True, stop=True).then_inc(qk_ps[b], 1)
                    pe.wait_ge(v_done[1 - b], after(c) if b else before(c))
                    for i in range(CT):
                        last = nc.tensor.matmul(ps_v[0:TQ, C * i:C * i + C], xnT[:, b, TQ * i:TQ * i + TQ], qkvT[:, 2 * C:],
                                                start=True, stop=True)
                    last.then_inc(v_ps[b], 1)
                    pe.wait_ge(qksq_done[b], after(c))
                    pe.wait_ge(qn_done[1 - b], after(c) if b else before(c))
                    pe.wait_ge(kn_done[1 - b], after(c) if b else before(c))
                    for w in range(2):
                        last = nc.tensor.matmul(ps_n[:, w, 0:CH], heads_of[:, w, :], qksq[:, b], start=True, stop=True)
                    last.then_inc(n_ps[b], 1)
            chunks(pe, step)


def load_stack(sp, t, b, head, q_stack, k_stack, with_shift, done):
    parts = t["qk_parts"][b] if isinstance(b, int) else t["qk_parts"][bass.ds(b, 1)].rearrange("a s r n -> (a s) r n")
    for j in range(PARTS):
        rows = slice(j * PARTS * HD, (j + 1) * PARTS * HD)
        of_q = parts[j:j + 1, bass.ds(head * HD, HD), :].to_broadcast([PARTS, HD, NP])
        sp.dma_start(q_stack[rows, 0:NP], of_q).then_inc(done, 16)
        of_k = parts[:, bass.ds(head * HD + C, HD), :]
        sp.dma_start(k_stack[rows, 0:NP], of_k).then_inc(done, 16)
    if with_shift:
        of_shift = t["shift_parts"][bass.ds(b * H + head, 1)].rearrange("a s n -> (a s) n")
        sp.dma_start(q_stack[SROWS:STACK, 0:NP], of_shift).then_inc(done, 16)


def settle_shifts(nc, ins, t):
    ctx = ExitStack()
    with ctx:
        ctx.enter_context(nc.cleanup_on_exit())
        def sb(name, shape, dt=F32):
            return ctx.enter_context(nc.sbuf_tensor(name, shape, dt))

        def sem(name):
            return nc.alloc_semaphore(name)

        COLS = B * H * NP // P
        shift = sb("shift", [P, COLS])
        k_top = sb("k_top", [P, 1])
        k_scale = sb("k_scale", [P, 1])
        bias_top = sb("bias_top", [P, 1])
        top = sb("top", [P, 1])
        top_all = sb("top_all", [P, 1])
        wide = sb("wide", [1, 1])
        general = sb("general", [1, 1], I32)
        rest1 = sb("s_rest1", [P, COLS])
        parts = sb("s_parts", [P, PARTS, COLS], BF16)
        q_stack = sb("m_q_stack", [SROWS, KP], BF16)
        k_stack = sb("m_k_stack", [SROWS, NP], BF16)
        row_top = sb("row_top", [P, NCH])
        row_tops = sb("row_tops", [P, KB])
        place = sb("place", [WS2, P])
        ps_s = ctx.enter_context(nc.psum_tensor("ps_s", [P, PARTS, 512], F32))

        loaded, scaled, rooted, raised, top_done, top_shared, wide_done, flagged = (sem(n) for n in (
            "loaded", "scaled", "rooted", "raised", "top_done", "top_shared", "wide_done", "flagged"))
        split, parts_out = sem("split"), sem("s_parts_out")
        prepared, placed, stack_in, piece_done, piece_read, tile_done, head_out, max_in = (sem(n) for n in (
            "prepared", "placed", "m_stack_in", "piece_done", "piece_read", "tile_done", "head_out", "max_in"))
        held = sem("s_held")
        PIECES = NCH
        BANKS = 3
        PER_HEAD = KB * PIECES
        WINDOW_TILE = (WIN0 + WS2) // P - 1

        block = ctx.enter_context(nc.Block())

        @block.sync
        def _(sp):
            sp.dma_start(shift[:], t["q_squares"].rearrange("g (s n) -> (g s) n", n=COLS)).then_inc(loaded, 16)
            per = P // (B * H)
            for n, dst in enumerate((k_top, bias_top)):
                sp.dma_start(dst[:], t["head_tops"][n].unsqueeze(1).unsqueeze(2).to_broadcast([B * H, per, 1])).then_inc(loaded, 16)
            sp.wait_ge(flagged, 1)
            wide_bound = sp.value_load(general[0:1, 0:1], min_val=0, max_val=1)
            with sp.If(wide_bound > 0):
                sp.sem_inc(head_out, 16)
                sp.wait_ge(prepared, 1)
                with sp.Fori(0, B) as b:
                    with sp.Fori(0, H) as n:
                        sp.wait_ge(tile_done, (b * H + n) * KB + 1)
                        sp.sem_inc(held, 1)
                        load_stack(sp, t, b, n, q_stack, k_stack, False, stack_in)
                        sp.wait_ge(tile_done, (b * H + n) * KB + KB + 1)
                        sp.sem_inc(held, 1)
                        with nc.allow_non_contiguous_dma(reason="4097 maxima of a head"):
                            sp.dma_start(t["row_max"][bass.ds(b * H + n, 1), :].rearrange("a (i p) -> p (a i)", p=P),
                                         row_tops[:]).then_inc(head_out, 16)
                sp.wait_ge(head_out, 16 * B * H + 16)
                sp.dma_start(shift[:], t["row_max"][:, 0:NP].rearrange("g (s n) -> g s n", n=COLS)).then_inc(max_in, 16)
            with sp.Else():
                sp.sem_inc(held, 1)
            sp.wait_ge(split, 4)
            for j in range(PARTS):
                sp.dma_start(t["shift_parts"][:, j, :].rearrange("g (s n) -> g s n", n=COLS), parts[:, j, :]).then_inc(parts_out, 16)
            sp.wait_ge(parts_out, 16 * PARTS)

        @block.gpsimd
        def _(pool):
            nc.gpsimd.memset(place[:], 0.0).then_inc(placed, 1)
            pool.wait_ge(placed, 1)
            nc.gpsimd.affine_select(out=place[:], in_=place[:], compare_op=ALU.not_equal, fill=1.0, base=P - WS2,
                                    pattern=[[-1, P]], channel_multiplier=1).then_inc(placed, 1)
            pool.wait_ge(placed, 2)
            pool.wait_ge(top_done, 1)
            nc.gpsimd.partition_all_reduce(top_all[:], top[:], P, RMAX).then_inc(top_shared, 1)

        @block.scalar
        def _(act):
            act.wait_ge(scaled, 1)
            nc.scalar.activation(shift[:], shift[:], ACT.Sqrt, scale=k_scale[:]).then_inc(rooted, 1)

        @block.vector
        def _(dve):
            dve.wait_ge(loaded, 48)
            nc.vector.tensor_scalar(k_scale[:], k_top[:], 1.03, None, ALU.mult).then_inc(scaled, 1)
            dve.wait_ge(rooted, 1)
            nc.vector.tensor_scalar(shift[:], shift[:], bias_top[:], None, ALU.add).then_inc(raised, 1)
            dve.wait_ge(raised, 1)
            nc.vector.tensor_reduce(top[:], shift[:], AX.X, ALU.max).then_inc(top_done, 1)
            dve.wait_ge(top_shared, 1)
            nc.vector.tensor_scalar(wide[:], top_all[0:1, :], SAFE, None, ALU.is_gt).then_inc(wide_done, 1)
            dve.wait_ge(wide_done, 1)
            nc.vector.tensor_copy(general[:], wide[:]).then_inc(flagged, 1)
            dve.wait_ge(flagged, 1)
            wide_bound = dve.value_load(general[0:1, 0:1], min_val=0, max_val=1)
            with dve.If(wide_bound > 0):
                dve.sem_inc(tile_done, 1)
                dve.sem_inc(piece_read, BANKS)
                nc.vector.memset(q_stack[:, NP:KP], 0.0).then_inc(prepared, 1)
                with dve.Fori(0, B * H) as n:
                    with dve.Fori(0, KB) as i:
                        dve.wait_ge(tile_done, n * KB + i + 1)
                        for k in range(PIECES):
                            keys = CH if k < PIECES - 1 else N - (PIECES - 1) * CH
                            dve.wait_ge(piece_done, (n * KB + i) * PIECES + k + 1)
                            nc.vector.tensor_reduce(row_top[:, k:k + 1], ps_s[:, k % BANKS, 0:keys], AX.X, ALU.max).then_inc(piece_read, 1)
                        dve.wait_ge(piece_read, (n * KB + i) * PIECES + PIECES + BANKS)
                        dve.wait_ge(head_out, 16 * n + 16)
                        dve.sem_inc(held, 1)
                        nc.vector.tensor_reduce(row_tops[:, bass.ds(i, 1)], row_top[:], AX.X, ALU.max).then_inc(tile_done, 1)
                dve.wait_ge(max_in, 16)
                dve.sem_inc(held, 1)
            with dve.Else():
                dve.sem_inc(held, 1)
            nc.vector.tensor_scalar(parts[:, 0, :], shift[:], -1.0, None, ALU.mult).then_inc(split, 1)
            dve.wait_ge(split, 1)
            nc.vector.scalar_tensor_tensor(out=rest1[:], in0=shift[:], scalar=-1.0, in1=parts[:, 0, :], op0=ALU.mult,
                                           op1=ALU.subtract).then_inc(split, 1)
            dve.wait_ge(split, 2)
            nc.vector.tensor_copy(parts[:, 1, :], rest1[:]).then_inc(split, 1)
            dve.wait_ge(split, 3)
            nc.vector.tensor_tensor(parts[:, 2, :], rest1[:], parts[:, 1, :], ALU.subtract).then_inc(split, 1)

        @block.tensor
        def _(pe):
            pe.wait_ge(flagged, 1)
            wide_bound = pe.value_load(general[0:1, 0:1], min_val=0, max_val=1)
            with pe.If(wide_bound > 0):
                pe.wait_ge(prepared, 1)
                pe.wait_ge(placed, 2)
                pe.sem_inc(held, 1)

                def tile(n, i, windowed):
                    for k in range(PIECES):
                        keys = CH if k < PIECES - 1 else N - (PIECES - 1) * CH
                        pe.wait_ge(piece_read, (n * KB + i) * PIECES + k + 1)
                        pe.sem_inc(held, 1)
                        over = windowed and k == PIECES - 1
                        last = nc.tensor.matmul(ps_s[:, k % BANKS, 0:keys], q_stack[:, bass.ds(i * P, P)],
                                                k_stack[:, k * CH:k * CH + keys], start=True, stop=not over)
                        if over:
                            at = WIN0 - k * CH
                            last = nc.tensor.matmul(ps_s[:, k % BANKS, at:at + WS2], place[:],
                                                    windowed[0], start=False, stop=True)
                        last.then_inc(piece_done, 1)

                with pe.Fori(0, B) as b:
                    with pe.Fori(0, H) as hd:
                        n = pe.snap(b * H + hd)
                        pe.wait_ge(stack_in, n * (16 * 2 * PARTS) + 16 * 2 * PARTS)
                        pe.sem_inc(held, 1)
                        with pe.Fori(0, WINDOW_TILE) as i:
                            tile(n, i, None)
                        bias = t["window"][:, bass.ds(hd, 1), :].rearrange("n a m -> n (a m)")
                        tile(n, WINDOW_TILE, [bias])
                        tile(n, WINDOW_TILE + 1, None)
            with pe.Else():
                pe.sem_inc(held, 1)


def attend(nc, ins, t):
    ctx = ExitStack()
    with ctx:
        ctx.enter_context(nc.cleanup_on_exit())
        def sb(name, shape, dt=F32):
            return ctx.enter_context(nc.sbuf_tensor(name, shape, dt))

        def sem(name):
            return nc.alloc_semaphore(name)

        def pair(name):
            return [sem(f"{name}{n}") for n in range(2)]

        SLOTS = 2
        GROUPS = 2 * NG
        PAIRS = B * H // 2
        PER_IMAGE = H // 2 // SLOTS
        V = HD + 1
        RING = 4
        ring_at = [g % 3 for g in range(GROUPS - RING)] + list(range(RING))
        back = [next(d for d in range(1, GROUPS + 1) if ring_at[(g - d) % GROUPS] == ring_at[g]) for g in range(GROUPS)]
        AHEAD = 2
        FINISH = (6, 17)

        q_stack = [[sb(f"q_stack{u}{p}", [STACK, NP], BF16) for p in range(2)] for u in range(SLOTS)]
        k_stack = [[sb(f"k_stack{u}{p}", [STACK, KP], BF16) for p in range(2)] for u in range(SLOTS)]
        v_all = sb("v_all", [P, B, KB, C])
        v_head = [[sb(f"v_head{u}{p}", [P, KB, V]) for p in range(2)] for u in range(SLOTS)]
        win_head = [[sb(f"win_head{u}{p}", [WS2, P]) for p in range(2)] for u in range(SLOTS)]
        probs = sb("probs", [P, RING, KG, CH])
        o_rest = sb("o_rest", [P, 2, CH])
        o_parts = sb("o_parts", [P, 2, PARTS, CH], BF16)
        inverse = sb("inverse", [P, 2, CT, 1])
        gather_f = sb("gather_f", [P, V])
        gather = sb("gather", [P, V], BF16)
        identity, attn = t["identity"], t["attn"]

        ps_s = ctx.enter_context(nc.psum_tensor("ps_scores", [P, 2, KG, 512], F32))
        ps_o = ctx.enter_context(nc.psum_tensor("ps_out", [P, 2, 512], F32))

        stacks_set, v_in, ones_set, win_set, gather_set = (sem(n) for n in (
            "stacks_set", "v_in", "ones_set", "win_set", "gather_set"))
        stack_in, v_ready = pair("stack_in"), pair("v_ready")
        scored, exped, valued = sem("scored"), sem("exped"), sem("valued")
        parts_ready, turned, split, inverted, normed = (pair(n) for n in (
            "parts_ready", "o_turned", "o_split", "o_inverted", "normed"))
        cleared = sem("cleared")
        a_held = sem("a_held")
        LOADS = 16 * 2 * (2 * PARTS + 1)
        STAGED = 4
        PAIR_GROUPS = NCH * GROUPS
        TURNS = PAIRS // SLOTS
        START = PAIR_GROUPS + RING

        void = sb("void", [P, 16 * C])
        b2_in = sb("b2_in", [EXPERTS, C])
        b2_rest = sb("b2_rest", [EXPERTS, C])
        b2_parts = sb("b2_parts", [EXPERTS, PARTS, C], BF16)
        void_set, b2_loaded, b2_split, voided, packed = (sem(n) for n in ("void_set", "b2_loaded", "b2_split", "voided", "packed_w"))
        VOIDS = BLOCKS // 16 + -(-(P - B1_ROW - 1) // 8)

        block = ctx.enter_context(nc.Block())

        @block.sync
        def _(sp):
            sp.wait_ge(stacks_set, 8)
            with sp.Fori(0, B) as b:
                with sp.Fori(0, PER_IMAGE) as j:
                    for u in range(SLOTS):
                        sp.wait_ge(scored, (((b * PER_IMAGE + j) * SLOTS + u) - 1) * PAIR_GROUPS + START)
                        sp.sem_inc(a_held, 1)
                        for p in range(2):
                            load_stack(sp, t, b, j * 2 * SLOTS + 2 * u + p, q_stack[u][p], k_stack[u][p], True, stack_in[u])
            sp.wait_ge(packed, 16 * 4)
            sp.wait_ge(voided, 16 * VOIDS)

        @block.gpsimd
        def _(pool):
            for b in range(B):
                pool.dma_start(v_all[:, b], t["v_rows"][b].rearrange("(k p) e -> p k e", p=P)).then_inc(v_in, 16)
            nc.gpsimd.memset(gather_f[:], 0.0).then_inc(gather_set, 1)
            for j in range(4):
                pool.wait_ge(gather_set, j + 1)
                nc.gpsimd.affine_select(out=gather_f[:], in_=gather_f[:], compare_op=ALU.not_equal, fill=1.0, base=-32 * j,
                                        pattern=[[-1, V]], channel_multiplier=1).then_inc(gather_set, 1)
            pool.wait_ge(gather_set, 5)
            nc.gpsimd.tensor_copy(gather[:], gather_f[:]).then_inc(gather_set, 1)
            pool.dma_start(b2_in[:], ins["L0_ffn_b2"]).then_inc(b2_loaded, 16)
            pool.wait_ge(void_set, 1)
            for v in range(BLOCKS // 16):
                pool.dma_start(t["slot_x"][:, 16 * v:16 * v + 16, :], void[:].rearrange("p (k c) -> p k c", c=C)).then_inc(voided, 16)
            packs = t["weights"]
            for at in range(B1_ROW + 1, P, 8):
                n = min(8, P - at)
                pool.dma_start(packs[:, at:at + n, 0:HID],
                               void[0:EXPERTS, 0:n * HID].rearrange("e (r c) -> e r c", c=HID)).then_inc(voided, 16)
            pool.dma_start(packs[:, 0:C, 0:HID], ins["L0_ffn_W1"]).then_inc(packed, 16)
            pool.dma_start(packs[:, B1_ROW:B1_ROW + 1, 0:HID], ins["L0_ffn_b1"].unsqueeze(1)).then_inc(packed, 16)
            pool.dma_start(packs[:, :, HID:PACK], ins["L0_ffn_W2"]).then_inc(packed, 16)
            pool.wait_ge(voided, 16 * VOIDS)
            pool.wait_ge(b2_split, 4)
            pool.dma_start(packs[:, B2_ROW:B2_ROW + PARTS, 0:C // 2], b2_parts[:].bitcast(F32)).then_inc(packed, 16)
            pool.wait_ge(v_in, 16 * B)
            pool.wait_ge(ones_set, 12)
            pool.sem_inc(a_held, 1)
            with pool.Fori(0, B) as b:
                with pool.Fori(0, PER_IMAGE) as j:
                    for u in range(SLOTS):
                        pool.wait_ge(valued, (((b * PER_IMAGE + j) * SLOTS + u) - 1) * PAIR_GROUPS + START)
                        pool.sem_inc(a_held, 1)
                        for p in range(2):
                            head = j * 2 * SLOTS + 2 * u + p
                            nc.gpsimd.tensor_copy(v_head[u][p][:, :, 0:HD],
                                                  v_all[:, bass.ds(b, 1), :, bass.ds(head * HD, HD)].rearrange("p a k e -> p (a k) e")
                                                  ).then_inc(v_ready[u], 1)
                            nc.gpsimd.tensor_copy(win_head[u][p][:, P - WS2:P],
                                                  t["window"][:, bass.ds(head, 1), :].rearrange("n a m -> n (a m)")
                                                  ).then_inc(v_ready[u], 1)

        @block.scalar
        def _(act):
            nc.scalar.preload_act_table(ACT.Exp)
            with act.Fori(0, PAIRS * NCH) as k:
                for g in range(GROUPS):
                    act.wait_ge(scored, k * GROUPS + g + 1 + START)
                    act.wait_ge(valued, k * GROUPS + g - back[g] + 1 + START)
                    nc.scalar.activation(probs[:, ring_at[g]], ps_s[:, g % 2, :, 0:CH], ACT.Exp).then_inc(exped, 1)

        @block.vector
        def _(dve):
            for p in range(2):
                dve.sem_inc(normed[p], 1)
            for u in range(SLOTS):
                for p in range(2):
                    nc.vector.memset(k_stack[u][p][C:STACK, 0:NP].bitcast(F32), TWO_ONES).then_inc(stacks_set, 1)
                    nc.vector.memset(k_stack[u][p][:, NP:KP], 0.0).then_inc(stacks_set, 1)
            for u in range(SLOTS):
                for p in range(2):
                    nc.vector.memset(v_head[u][p][:, 0:KB - 1, HD:V], 1.0).then_inc(ones_set, 1)
                    nc.vector.memset(v_head[u][p][:, KB - 1, HD:V], 0.0).then_inc(ones_set, 1)
                    nc.vector.memset(win_head[u][p][:], 0.0).then_inc(ones_set, 1)
            dve.wait_ge(ones_set, 12)
            for u in range(SLOTS):
                for p in range(2):
                    nc.vector.memset(v_head[u][p][0:1, KB - 1, HD:V], 1.0).then_inc(win_set, 1)
            nc.vector.memset(void[:], 0.0).then_inc(void_set, 1)
            dve.wait_ge(b2_loaded, 16)
            nc.vector.tensor_copy(b2_parts[:, 0], b2_in[:]).then_inc(b2_split, 1)
            dve.wait_ge(b2_split, 1)
            nc.vector.tensor_tensor(b2_rest[:], b2_in[:], b2_parts[:, 0], ALU.subtract).then_inc(b2_split, 1)
            dve.wait_ge(b2_split, 2)
            nc.vector.tensor_copy(b2_parts[:, 1], b2_rest[:]).then_inc(b2_split, 1)
            dve.wait_ge(b2_split, 3)
            nc.vector.tensor_tensor(b2_parts[:, 2], b2_rest[:], b2_parts[:, 1], ALU.subtract).then_inc(b2_split, 1)
            nc.vector.memset(ps_o[:], 0.0).then_inc(cleared, 1)
            nc.vector.memset(o_parts[:, 1], 0.0).then_inc(parts_ready[1], 1)
            with dve.Fori(0, B) as b:
                with dve.Fori(0, PER_IMAGE) as j:
                    for u in range(SLOTS):
                        with dve.Fori(0, NCH) as c:
                            k = dve.snap(((b * PER_IMAGE + j) * SLOTS + u) * NCH + c)
                            for p in range(2):
                                dve.wait_ge(valued, k * GROUPS + (p + 1) * NG + START)
                                nc.vector.tensor_copy(o_parts[:, p, 0], ps_o[:, p, 0:CH]).then_inc(split[p], 1)
                                dve.wait_ge(split[p], k * 3 + 1)
                                nc.vector.tensor_tensor(o_rest[:, p], ps_o[:, p, 0:CH], o_parts[:, p, 0], ALU.subtract).then_inc(split[p], 1)
                                dve.wait_ge(split[p], k * 3 + 2)
                                nc.vector.tensor_copy(o_parts[:, p, 1], o_rest[:, p]).then_inc(split[p], 1)
                                dve.wait_ge(split[p], k * 3 + 3)
                                nc.vector.tensor_tensor(o_parts[:, p, 2], o_rest[:, p], o_parts[:, p, 1], ALU.subtract).then_inc(parts_ready[p], 1)
                                dve.wait_ge(turned[p], k + 1 + p)
                                sums = ps_o[0:TQ, p, CH:CH + CT * V].rearrange("q (i v) -> q i v", v=V)
                                dve.wait_ge(normed[p], k + 1)
                                nc.vector.reciprocal(inverse[0:TQ, p], sums[:, :, HD:V]).then_inc(inverted[p], 1)
                                dve.wait_ge(inverted[p], k + 1)
                                dst = attn[0:TQ, bass.ds(b * NT + c * CT, CT), bass.ds((j * 2 * SLOTS + 2 * u + p) * HD, HD)]
                                nc.vector.tensor_tensor(dst, sums[:, :, 0:HD], inverse[0:TQ, p].to_broadcast([TQ, CT, HD]),
                                                        ALU.mult).then_inc(normed[p], 1)

        @block.tensor
        def _(pe):
            pe.sem_inc(exped, AHEAD)
            pe.sem_inc(scored, START)
            pe.sem_inc(valued, START)

            def scores(u, c, g, windowed):
                p, first = g // NG, g % NG * KG
                for s in range(KG):
                    over = windowed and first + s == (WIN0 + WS2) // P - 1
                    last = nc.tensor.matmul(ps_s[:, g % 2, s, 0:CH], k_stack[u][p][:, (first + s) * P:(first + s + 1) * P],
                                            q_stack[u][p][:, bass.ds(c * CH, CH)], start=True, stop=not over)
                    if over:
                        at = WIN0 - (NCH - 1) * CH
                        last = nc.tensor.matmul(ps_s[:, g % 2, s, at:at + WS2], win_head[u][p][:], identity[0:WS2, 0:WS2],
                                                start=False, stop=True)
                last.then_inc(scored, 1)

            def values(u, g):
                p, first = g // NG, g % NG * KG
                for s in range(KG):
                    kb = first + s
                    at = 32 * (kb % 4)
                    last = nc.tensor.matmul(ps_o[at:at + V, p, 0:CH], v_head[u][p][:, kb, :], probs[:, ring_at[g], s],
                                            start=kb < 4, stop=kb >= KB - 4)
                last.then_inc(valued, 1)

            def turn(p):
                for i in range(CT):
                    for part in range(PARTS):
                        last = nc.tensor.matmul(ps_o[0:TQ, p, CH + V * i:CH + V * i + V], o_parts[:, p, part, TQ * i:TQ * i + TQ],
                                                gather[:], start=part == 0, stop=part == PARTS - 1)
                last.then_inc(turned[p], 1)

            def body(turn_no, u, c, last_pair):
                k = (turn_no * SLOTS + u) * NCH + c
                ends = isinstance(c, int)
                for g in range(AHEAD, GROUPS + AHEAD):
                    pe.wait_ge(exped, k * GROUPS + g + 1)
                    if g < GROUPS:
                        scores(u, c, g, ends)
                    elif not ends:
                        scores(u, c + 1, g - GROUPS, False)
                    elif not last_pair:
                        if g == GROUPS:
                            pe.wait_ge(stack_in[1 - u], (turn_no + 1 + u) * LOADS)
                        scores(1 - u, 0, g - GROUPS, False)
                    if (g - AHEAD) % NG == 0:
                        pe.wait_ge(normed[(g - AHEAD) // NG], k + 1)
                    values(u, g - AHEAD)
                    if g in FINISH:
                        p = 1 - FINISH.index(g)
                        pe.wait_ge(parts_ready[p], k + 1)
                        turn(p)

            def head_pair(turn_no, u, last_pair=False):
                pe.wait_ge(v_ready[u], (turn_no + 1) * STAGED)
                pe.sem_inc(a_held, 1)
                with pe.Fori(0, NCH - 1) as c:
                    body(turn_no, u, c, last_pair)
                body(turn_no, u, NCH - 1, last_pair)

            pe.wait_ge(gather_set, 6)
            pe.wait_ge(win_set, 2 * SLOTS)
            pe.wait_ge(cleared, 1)
            pe.wait_ge(stack_in[0], LOADS)
            for g in range(AHEAD):
                scores(0, 0, g, False)
            with pe.Fori(0, TURNS - 1) as turn_no:
                for u in range(SLOTS):
                    head_pair(turn_no, u)
            head_pair(TURNS - 1, 0)
            head_pair(TURNS - 1, 1, last_pair=True)
            pe.wait_ge(parts_ready[1], PAIRS * NCH + 1)
            turn(1)


def tile_sems(sem, names):
    return [[sem(f"{n}{s}") for s in range(2)] for n in names]


def route(nc, ins, t):
    ctx = ExitStack()
    with ctx:
        ctx.enter_context(nc.cleanup_on_exit())
        def sb(name, shape, dt=F32):
            return ctx.enter_context(nc.sbuf_tensor(name, shape, dt))

        def ps(name, shape, dt=F32):
            return ctx.enter_context(nc.psum_tensor(name, shape, dt))

        def sem(name):
            return nc.alloc_semaphore(name)

        h, attn, normed, identity, wprojT = (t[k] for k in ("h", "attn", "normed", "identity", "wprojT"))
        TILES = B * NT
        STEPS = TILES // CT // 2
        router = sb("router", [C, EXPERTS])
        router_bias = sb("router_bias", [P, EXPERTS])
        proj_bias = sb("proj_bias", [P, C])
        r_power = sb("r_power", [P, CT])
        aT = sb("aT", [C, 2, CH])
        xT = sb("xT", [C, 2, CH])
        raised = sb("raised", [P, 2, CT, C])
        total = sb("r_total", [P, 2, CT])
        neg_mean = sb("r_neg_mean", [P, 2, CT])
        centred = sb("r_centred", [P, 2, CT, C])
        square = sb("r_square", [P, 2, CT, C])
        variance = sb("r_variance", [P, 2, CT])
        var_eps = sb("r_var_eps", [P, 2, CT])
        rstd = sb("r_rstd", [P, 2, CT])
        logits = sb("logits", [P, 2, CT, EXPERTS])
        attn_c = sb("attn_c", [P, 2, CT, C])
        xn_c = sb("xn_c", [P, 2, CT, C])
        best_c = sb("best_c", [P, 2, CT, 8])
        best_at_c = sb("best_at_c", [P, 2, CT, 8], U32)
        best = sb("best", [P, TILES, 8])
        best_at = sb("best_at", [P, TILES, 8], U32)
        at_f = sb("at_f", [P, TOP, TILES])
        ids = sb("ids", [P, EXPERTS])
        block_ids = sb("block_ids", [P, 2])
        chosen = sb("chosen", [P, TOP, TILES, EXPERTS], BF16)
        either = sb("either", [P, TILES, EXPERTS], BF16)
        ones_f = sb("ones_f", [P, P])
        before_f = sb("before_f", [P, P])
        ones_b = sb("ones_b", [P, P], BF16)
        before_b = sb("before_b", [P, P], BF16)
        rank = sb("rank", [P, TILES, EXPERTS])
        in_tile = sb("in_tile", [P, TILES, EXPERTS])
        start = sb("start", [P, TILES, EXPERTS])
        product = sb("product", [P, TILES, EXPERTS])
        count = sb("count", [P, EXPERTS])
        count_i = sb("count_i", [P, 3, EXPERTS], I32)
        ends = sb("ends", [P, 2, EXPERTS])
        n_blocks = sb("n_blocks", [P, EXPERTS])
        slot = sb("slot", [P, TILES, TOP])
        slot_i = sb("slot_i", [P, 3, TILES * TOP], I32)
        slot_f = sb("slot_f", [P, 2, TILES * TOP])
        over = sb("over", [P, 2, EXPERTS])
        expert_f = sb("expert_f", [P, 2])
        expert_i = sb("expert_i", [P, 2], I32)
        gap = sb("gap", [P, TILES])
        weight2 = sb("weight2", [P, TILES])
        weight_sum = sb("weight_sum", [P, TILES])

        ps_a = ps("ps_a", [C, 2, 512])
        ps_x = ps("ps_x", [C, 2, 512])
        ps_p = ps("ps_p", [P, 2, 512])
        ps_l = ps("ps_l", [P, 2, 512])

        w_in, consts, held = sem("r_w_in"), sem("r_consts"), sem("r_held")
        aT_ps, aT_done, p_ps, raise_done, h_done, sum_done, mean_done, centre_done, square_done, var_done = tile_sems(sem, (
            "aT_ps", "aT_done", "p_ps", "raise_done", "r_h_done", "r_sum_done", "r_mean_done", "r_centre_done", "r_square_done", "r_var_done"))
        eps_done, rstd_done, norm_done, xT_ps, xT_done, l_ps, logits_done, best_done = tile_sems(sem, (
            "r_eps_done", "r_rstd_done", "r_norm_done", "xT_ps", "xT_done", "l_ps", "logits_done", "best_done"))
        staged, spread, best_found, kept = tile_sems(sem, ("staged", "spread", "best_found", "kept"))
        step = sem("step")
        either_done, counted, copied = sem("either_done"), sem("counted"), sem("copied")
        gap_done, weight_done, expert_out = sem("gap_done"), sem("weight_done"), sem("expert_out")

        block = ctx.enter_context(nc.Block())

        def chunk_steps(eng, body):
            with eng.Fori(0, STEPS) as i:
                body(i)

        @block.sync
        def _(sp):
            sp.dma_start(router[:], ins["L0_ffn_Wr"]).then_inc(w_in, 16)
            sp.dma_start(router_bias[:], ins["L0_ffn_br"].partition_broadcast(P)).then_inc(w_in, 16)
            sp.dma_start(proj_bias[:], ins["L0_attn_b_proj"].partition_broadcast(P)).then_inc(w_in, 16)
            sp.wait_ge(step, EXPERT_STEPS)
            half = BLOCKS // 2
            with nc.allow_non_contiguous_dma(reason="an expert number for each block, once"):
                sp.dma_start(t["expert_of"].rearrange("(a p) -> p a", p=half), expert_i[0:half, :]).then_inc(expert_out, 16)
            sp.wait_ge(expert_out, 16)

        @block.gpsimd
        def _(pool):
            for s in range(2):
                pool.sem_inc(spread[s], 1)
                pool.sem_inc(eps_done[s], 1)
                pool.sem_inc(rstd_done[s], 1)
            nc.gpsimd.memset(r_power[:], -0.5).then_inc(consts, 1)
            nc.gpsimd.iota(ids[:], [[1, EXPERTS]], base=0, channel_multiplier=0, allow_small_or_imprecise_dtypes=True).then_inc(consts, 1)
            nc.gpsimd.iota(block_ids[:], [[BLOCKS // 2, 2]], base=0, channel_multiplier=1, allow_small_or_imprecise_dtypes=True).then_inc(consts, 1)
            nc.gpsimd.memset(ones_f[:], 1.0).then_inc(consts, 1)
            pool.wait_ge(consts, 4)
            nc.gpsimd.affine_select(out=before_f[:], in_=ones_f[:], compare_op=ALU.is_gt, fill=0.0, base=0,
                                    pattern=[[1, P]], channel_multiplier=-1).then_inc(consts, 1)

            def body(i):
                for s in range(2):
                    pool.wait_ge(var_done[s], after(i))
                    pool.sem_inc(held, 1)
                    nc.gpsimd.tensor_scalar(var_eps[0:TQ, s], variance[0:TQ, s], 1.0 / C, EPS, ALU.mult,
                                            ALU.add).then_inc(eps_done[s], 1)
                    pool.wait_ge(eps_done[s], after(i))
                    nc.gpsimd.tensor_tensor(out=rstd[0:TQ, s], in0=var_eps[0:TQ, s], in1=r_power[0:TQ],
                                            op=ALU.pow).then_inc(rstd_done[s], 1)
                for s in range(2):
                    pool.wait_ge(norm_done[s], after(i))
                    pool.sem_inc(held, 1)
                    nc.gpsimd.tensor_copy(normed[0:TQ, bass.ds((i * 2 + s) * CT, CT), :], xn_c[0:TQ, s]).then_inc(spread[s], 1)
            chunk_steps(pool, body)

        @block.scalar
        def _(act):
            for s in range(2):
                act.sem_inc(staged[s], 1)
                act.sem_inc(aT_done[s], 1)
                act.sem_inc(xT_done[s], 1)
            nc.scalar.preload_act_table(ACT.Exp)

            def body(i):
                for s in range(2):
                    act.wait_ge(aT_ps[s], before(i))
                    nc.scalar.copy(attn_c[0:TQ, s], attn[0:TQ, bass.ds((i * 2 + s) * CT, CT), :]).then_inc(staged[s], 1)
                for s in range(2):
                    act.wait_ge(aT_ps[s], after(i))
                    nc.scalar.copy(aT[:, s], ps_a[:, s, 0:CH]).then_inc(aT_done[s], 1)
                for s in range(2):
                    act.wait_ge(xT_ps[s], after(i))
                    nc.scalar.copy(xT[:, s], ps_x[:, s, 0:CH]).then_inc(xT_done[s], 1)
            chunk_steps(act, body)
            act.wait_ge(gap_done, 1)
            nc.scalar.activation(weight2[0:TQ], gap[0:TQ], ACT.Exp).then_inc(weight_done, 1)
            for g in range(TILES * EXPERTS // 512):
                act.wait_ge(counted, 2 * g + 2)
                for dst, src in ((rank, ps_p), (in_tile, ps_l)):
                    last = nc.scalar.copy(dst[0:TQ, 8 * g:8 * g + 8].rearrange("p i e -> p (i e)"), src[0:TQ, g % 2])
                last.then_inc(copied, 1)

        @block.vector
        def _(dve):
            for s in range(2):
                for w in (raise_done, h_done, sum_done, mean_done, centre_done, square_done, var_done, norm_done, logits_done, best_done, best_found, kept):
                    dve.sem_inc(w[s], 1)
            dve.wait_ge(w_in, 48)

            def wide(x):
                return x.unsqueeze(2).to_broadcast([TQ, CT, C])

            def body(i):
                for s in range(2):
                    tok = h[0:TQ, bass.ds((i * 2 + s) * CT, CT), :]
                    dve.wait_ge(h_done[s], before(i))
                    nc.vector.tensor_tensor(raised[0:TQ, s], tok, proj_bias[0:TQ].unsqueeze(1).to_broadcast([TQ, CT, C]),
                                            ALU.add).then_inc(raise_done[s], 1)
                    dve.wait_ge(raise_done[s], after(i))
                    dve.wait_ge(p_ps[s], after(i))
                    nc.vector.tensor_tensor(tok, raised[0:TQ, s], ps_p[0:TQ, s, 0:CT * C].rearrange("p (i e) -> p i e", e=C),
                                            ALU.add).then_inc(h_done[s], 1)
                    dve.wait_ge(h_done[s], after(i))
                    dve.sem_inc(held, 1)
                    nc.vector.tensor_reduce(total[0:TQ, s], tok, AX.X, ALU.add).then_inc(sum_done[s], 1)
                    dve.wait_ge(sum_done[s], after(i))
                    nc.vector.tensor_scalar(neg_mean[0:TQ, s], total[0:TQ, s], -1.0 / C, None, ALU.mult).then_inc(mean_done[s], 1)
                    dve.wait_ge(mean_done[s], after(i))
                    nc.vector.tensor_tensor(centred[0:TQ, s], tok, wide(neg_mean[0:TQ, s]), ALU.add).then_inc(centre_done[s], 1)
                    dve.wait_ge(centre_done[s], after(i))
                    nc.vector.tensor_tensor(square[0:TQ, s], centred[0:TQ, s], centred[0:TQ, s], ALU.mult).then_inc(square_done[s], 1)
                    dve.wait_ge(square_done[s], after(i))
                    nc.vector.tensor_reduce(variance[0:TQ, s], square[0:TQ, s], AX.X, ALU.add).then_inc(var_done[s], 1)
                for s in range(2):
                    dve.wait_ge(rstd_done[s], after(i))
                    dve.wait_ge(xT_ps[s], before(i))
                    dve.wait_ge(spread[s], before(i))
                    nc.vector.tensor_tensor(xn_c[0:TQ, s], centred[0:TQ, s], wide(rstd[0:TQ, s]), ALU.mult).then_inc(norm_done[s], 1)
                for s in range(2):
                    dve.wait_ge(l_ps[s], after(i))
                    dve.wait_ge(best_done[s], before(i))
                    nc.vector.tensor_tensor(logits[0:TQ, s], ps_l[0:TQ, s, 0:CT * EXPERTS].rearrange("p (i e) -> p i e", e=EXPERTS),
                                            router_bias[0:TQ].unsqueeze(1).to_broadcast([TQ, CT, EXPERTS]), ALU.add).then_inc(logits_done[s], 1)
                    dve.wait_ge(logits_done[s], after(i))
                    dve.wait_ge(kept[s], i * 2 + 1)
                    dve.sem_inc(held, 1)
                    for x in range(CT):
                        last = nc.vector.max(best_c[0:TQ, s, x, :], logits[0:TQ, s, x, :])
                    last.then_inc(best_found[s], 1)
                    dve.wait_ge(best_found[s], after(i))
                    dve.sem_inc(held, 1)
                    for x in range(CT):
                        last = nc.vector.max_index(best_at_c[0:TQ, s, x, :], best_c[0:TQ, s, x, :], logits[0:TQ, s, x, :])
                    last.then_inc(best_done[s], 1)
                    dve.wait_ge(best_done[s], after(i))
                    first = (i * 2 + s) * CT
                    nc.vector.tensor_copy(best[0:TQ, bass.ds(first, CT), :], best_c[0:TQ, s]).then_inc(kept[s], 1)
                    nc.vector.tensor_copy(best_at[0:TQ, bass.ds(first, CT), :], best_at_c[0:TQ, s]).then_inc(kept[s], 1)
            chunk_steps(dve, body)
            done = [0]

            def then(instruction):
                done[0] += 1
                instruction.then_inc(step, 1)
                dve.wait_ge(step, done[0])

            R = slice(0, TQ)
            for s in range(2):
                dve.wait_ge(kept[s], 2 * STEPS + 1)
            then(nc.vector.tensor_tensor(gap[R], best[R, :, 1], best[R, :, 0], ALU.subtract))
            dve.sem_inc(gap_done, 1)
            for k in range(TOP):
                then(nc.vector.tensor_copy(at_f[R, k], best_at[R, :, k]))
            dve.wait_ge(consts, 5)
            then(nc.vector.tensor_copy(ones_b[:], ones_f[:]))
            then(nc.vector.tensor_copy(before_b[:], before_f[:]))
            whole = [TQ, TILES, EXPERTS]
            for k in range(TOP):
                then(nc.vector.tensor_tensor(chosen[R, k], ids[R].unsqueeze(1).to_broadcast(whole),
                                             at_f[R, k].unsqueeze(2).to_broadcast(whole), ALU.is_equal))
            then(nc.vector.tensor_tensor(either[R], chosen[R, 0], chosen[R, 1], ALU.add))
            dve.sem_inc(either_done, 1)
            gates = t["gates"]
            dve.wait_ge(weight_done, 1)
            then(nc.vector.tensor_scalar(weight_sum[R], weight2[R], 1.0, None, ALU.add))
            then(nc.vector.reciprocal(gates[R, :, 0], weight_sum[R]))
            then(nc.vector.tensor_tensor(gates[R, :, 1], weight2[R], gates[R, :, 0], ALU.mult))
            dve.wait_ge(copied, TILES // 8)
            then(nc.vector.tensor_reduce(count[R], in_tile[R].rearrange("p i e -> p e i"), AX.X, ALU.add))
            then(nc.vector.tensor_scalar(count[R], count[R], float(P - 1), None, ALU.add))
            then(nc.vector.tensor_copy(count_i[R, 0], count[R]))
            then(nc.vector.tensor_scalar(count_i[R, 1], count_i[R, 0], 7, None, ALU.arith_shift_right))
            then(nc.vector.tensor_copy(n_blocks[R], count_i[R, 1]))
            then(nc.vector.tensor_copy(ends[R, 0], n_blocks[R]))
            src, width = 0, 1
            while width < EXPERTS:
                then(nc.vector.tensor_copy(ends[R, 1 - src, 0:width], ends[R, src, 0:width]))
                then(nc.vector.tensor_tensor(ends[R, 1 - src, width:], ends[R, src, width:], ends[R, src, 0:EXPERTS - width], ALU.add))
                src, width = 1 - src, 2 * width
            last_block = ends[R, src]
            then(nc.vector.tensor_tensor(start[R, 0], last_block, n_blocks[R], ALU.subtract))
            then(nc.vector.tensor_scalar(start[R, 0], start[R, 0], float(P), None, ALU.mult))
            half = BLOCKS // 2
            for a in range(2):
                then(nc.vector.tensor_scalar(over[0:half, a], ends[0:half, src], block_ids[0:half, a:a + 1], None, ALU.is_le))
            then(nc.vector.tensor_reduce(expert_f[0:half], over[0:half], AX.X, ALU.add))
            then(nc.vector.tensor_scalar(expert_f[0:half], expert_f[0:half], float(EXPERTS - 1), None, ALU.min))
            then(nc.vector.tensor_copy(expert_i[0:half], expert_f[0:half]))
            assert done[0] == EXPERT_STEPS, done[0]
            for i in range(TILES - 1):
                then(nc.vector.tensor_tensor(start[R, i + 1], start[R, i], in_tile[R, i], ALU.add))
            then(nc.vector.tensor_tensor(rank[R], rank[R], start[R], ALU.add))
            for k in range(TOP):
                then(nc.vector.tensor_tensor(product[R], rank[R], chosen[R, k], ALU.mult))
                then(nc.vector.tensor_reduce(slot[R, :, k], product[R], AX.X, ALU.add))
            flat = slot[R].rearrange("p i k -> p (i k)")
            then(nc.vector.tensor_copy(slot_i[R, 0], flat))
            then(nc.vector.tensor_scalar(slot_i[R, 1], slot_i[R, 0], P - 1, None, ALU.bitwise_and))
            then(nc.vector.tensor_scalar(slot_i[R, 2], slot_i[R, 0], 7, None, ALU.arith_shift_right))
            for k in range(2):
                then(nc.vector.tensor_copy(slot_f[R, k], slot_i[R, 1 + k]))
            then(nc.vector.scalar_tensor_tensor(out=slot_f[R, 0], in0=slot_f[R, 0], scalar=float(BLOCKS), in1=slot_f[R, 1],
                                                op0=ALU.mult, op1=ALU.add))
            then(nc.vector.tensor_copy(t["rows"][R].rearrange("p i k -> p (i k)"), slot_f[R, 0]))

        @block.tensor
        def _(pe):
            for s in range(2):
                for w in (aT_ps, p_ps, xT_ps, l_ps):
                    pe.sem_inc(w[s], 1)
            pe.wait_ge(w_in, 48)

            def body(i):
                for s in range(2):
                    pe.wait_ge(staged[s], after(i))
                    pe.wait_ge(aT_done[s], before(i))
                    pe.sem_inc(held, 1)
                    for x in range(CT):
                        last = nc.tensor.transpose(ps_a[:, s, TQ * x:TQ * x + TQ], attn_c[0:TQ, s, x, :], identity[0:TQ, 0:TQ])
                    last.then_inc(aT_ps[s], 1)
                for s in range(2):
                    pe.wait_ge(aT_done[s], after(i))
                    pe.wait_ge(h_done[s], before(i))
                    pe.sem_inc(held, 1)
                    for x in range(CT):
                        last = nc.tensor.matmul(ps_p[0:TQ, s, C * x:C * x + C], aT[:, s, TQ * x:TQ * x + TQ], wprojT[:],
                                                start=True, stop=True)
                    last.then_inc(p_ps[s], 1)
                for s in range(2):
                    pe.wait_ge(norm_done[s], after(i))
                    pe.wait_ge(xT_done[s], before(i))
                    pe.sem_inc(held, 1)
                    for x in range(CT):
                        last = nc.tensor.transpose(ps_x[:, s, TQ * x:TQ * x + TQ], xn_c[0:TQ, s, x, :], identity[0:TQ, 0:TQ])
                    last.then_inc(xT_ps[s], 1)
                for s in range(2):
                    pe.wait_ge(xT_done[s], after(i))
                    pe.wait_ge(logits_done[s], before(i))
                    pe.sem_inc(held, 1)
                    for x in range(CT):
                        last = nc.tensor.matmul(ps_l[0:TQ, s, EXPERTS * x:EXPERTS * x + EXPERTS], xT[:, s, TQ * x:TQ * x + TQ], router[:],
                                                start=True, stop=True)
                    last.then_inc(l_ps[s], 1)
            chunk_steps(pe, body)
            pe.wait_ge(either_done, 1)
            for g in range(TILES * EXPERTS // 512):
                rhs = either[0:TQ, 8 * g:8 * g + 8].rearrange("p i e -> p (i e)")
                if g >= 2:
                    pe.wait_ge(copied, g - 1)
                nc.tensor.matmul(ps_p[0:TQ, g % 2], before_b[0:TQ, 0:TQ], rhs, start=True, stop=True).then_inc(counted, 1)
                nc.tensor.matmul(ps_l[0:TQ, g % 2], ones_b[0:TQ, 0:TQ], rhs, start=True, stop=True).then_inc(counted, 1)


def run_experts(nc, ins, t):
    ctx = ExitStack()
    with ctx:
        ctx.enter_context(nc.cleanup_on_exit())
        def sb(name, shape, dt=F32):
            return ctx.enter_context(nc.sbuf_tensor(name, shape, dt))

        def ps(name, shape, dt=F32):
            return ctx.enter_context(nc.psum_tensor(name, shape, dt))

        def sem(name):
            return nc.alloc_semaphore(name)

        G = 4
        TURNS = BLOCKS // G // 2
        expert_row = sb("expert_row", [1, BLOCKS], I32)
        xs = sb("xs", [P, 2, G, C])
        pack = sb("pack", [P, 2, G, PACK])
        xsT = sb("xsT", [C + 1, 2, G * P])
        hidT = sb("hidT", [P, 2, G * P])
        ys = sb("ys", [P, 2, G, C])
        ones3 = sb("ones3", [P, P], BF16)
        identity = t["identity"]
        ps_x = ps("e_ps_x", [C, 2, 512])
        ps_h = ps("e_ps_h", [P, 2, 512])
        ps_y = ps("e_ps_y", [P, 2, 512])

        row_in, scattered, ones_done, held = (sem(n) for n in ("row_in", "scattered", "ones_done", "e_held"))
        x_in, pack_in, y_out, xT_ps, xT_done, h_ps, h_done, y_ps, y_done = tile_sems(sem, (
            "e_x_in", "pack_in", "y_out", "e_xT_ps", "e_xT_done", "h_ps", "e_h_done", "y_ps", "y_done"))
        SCATTERS = 16 * B * NT * TOP

        block = ctx.enter_context(nc.Block())

        @block.gpsimd
        def _(pool):
            rows_x = t["slot_x"].rearrange("p k c -> (p k) c")
            for i in range(B * NT):
                for k in range(TOP):
                    nc.gpsimd.indirect_dma_start(
                        out=rows_x, out_offset=bass.IndirectOffsetOnAxis(ap=t["rows"][0:TQ, i, k:k + 1], axis=0),
                        in_=t["normed"][0:TQ, i, :], in_offset=None).then_inc(scattered, 16)

        @block.sync
        def _(sp):
            for s in range(2):
                sp.sem_inc(y_out[s], 16)
            sp.dma_start(expert_row[:], t["expert_of"].rearrange("(a k) -> a k", a=1)).then_inc(row_in, 16)
            sp.wait_ge(row_in, 16)
            sp.sem_inc(held, 1)

            with sp.Fori(0, TURNS) as i:
                for s in range(2):
                    group = i * 2 + s
                    sp.wait_ge(y_ps[s], before(i))
                    sp.sem_inc(held, 1)
                    for x in range(G):
                        expert = sp.value_load(expert_row[0:1, bass.ds(group * G + x, 1)], min_val=0, max_val=EXPERTS - 1)
                        sp.dma_start(pack[:, s, x], t["weights"][bass.ds(expert, 1)].rearrange("a p n -> p (a n)")).then_inc(pack_in[s], 16)
                    sp.wait_ge(scattered, SCATTERS)
                    sp.dma_start(xs[:, s], t["slot_x"][:, bass.ds(group * G, G), :]).then_inc(x_in[s], 16)
            for s in range(2):
                sp.wait_ge(y_out[s], 16 * (TURNS + 1))

        @block.scalar
        def _(act):
            for s in range(2):
                act.sem_inc(xT_done[s], 1)
                act.sem_inc(y_done[s], 1)
            with act.Fori(0, TURNS) as i:
                for s in range(2):
                    act.wait_ge(xT_ps[s], after(i))
                    act.wait_ge(h_ps[s], before(i))
                    nc.scalar.copy(xsT[0:C, s], ps_x[:, s]).then_inc(xT_done[s], 1)
                for s in range(2):
                    act.wait_ge(y_ps[s], after(i))
                    act.wait_ge(y_out[s], 16 * before(i))
                    nc.scalar.copy(ys[:, s].rearrange("p g c -> p (g c)"), ps_y[:, s, 0:G * C]).then_inc(y_done[s], 1)
                    act.wait_ge(y_done[s], after(i))
                    act.dma_start(t["slot_y"][:, bass.ds((i * 2 + s) * G, G), :], ys[:, s]).then_inc(y_out[s], 16)

        @block.vector
        def _(dve):
            for s in range(2):
                dve.sem_inc(h_done[s], 1)
            nc.vector.memset(ones3[:], 1.0).then_inc(ones_done, 1)
            nc.vector.memset(xsT[B1_ROW:B1_ROW + 1], 1.0).then_inc(ones_done, 1)
            with dve.Fori(0, TURNS) as i:
                for s in range(2):
                    dve.wait_ge(h_ps[s], after(i))
                    dve.wait_ge(y_ps[s], before(i))
                    nc.vector.tensor_scalar(hidT[:, s], ps_h[:, s], 0.0, None, ALU.max).then_inc(h_done[s], 1)

        @block.tensor
        def _(pe):
            for s in range(2):
                for w in (xT_ps, h_ps, y_ps):
                    pe.sem_inc(w[s], 1)
            pe.wait_ge(ones_done, 2)
            with pe.Fori(0, TURNS) as i:
                for s in range(2):
                    pe.wait_ge(x_in[s], 16 * i + 16)
                    pe.wait_ge(xT_done[s], before(i))
                    pe.sem_inc(held, 1)
                    for x in range(G):
                        last = nc.tensor.transpose(ps_x[:, s, P * x:P * x + P], xs[:, s, x, :], identity[:])
                    last.then_inc(xT_ps[s], 1)
                for s in range(2):
                    pe.wait_ge(pack_in[s], 16 * G * i + 16 * G)
                    pe.wait_ge(xT_done[s], after(i))
                    pe.wait_ge(h_done[s], before(i))
                    pe.sem_inc(held, 1)
                    for x in range(G):
                        last = nc.tensor.matmul(ps_h[:, s, P * x:P * x + P], pack[0:C + 1, s, x, 0:HID], xsT[:, s, P * x:P * x + P],
                                                start=True, stop=True)
                    last.then_inc(h_ps[s], 1)
                for s in range(2):
                    pe.wait_ge(h_done[s], after(i))
                    pe.wait_ge(y_done[s], before(i))
                    pe.sem_inc(held, 1)
                    for x in range(G):
                        y = ps_y[:, s, C * x:C * x + C]
                        nc.tensor.matmul(y, hidT[:, s, P * x:P * x + P], pack[:, s, x, HID:PACK], start=True, stop=False)
                        b2 = pack[B2_ROW:B2_ROW + PARTS, s, x, 0:C // 2].bitcast(BF16)
                        last = nc.tensor.matmul(y, ones3[B2_ROW:B2_ROW + PARTS, :], b2, start=False, stop=True)
                    last.then_inc(y_ps[s], 1)


def combine(nc, t, out):
    ctx = ExitStack()
    with ctx:
        ctx.enter_context(nc.cleanup_on_exit())
        def sb(name, shape, dt=F32):
            return ctx.enter_context(nc.sbuf_tensor(name, shape, dt))

        def sem(name):
            return nc.alloc_semaphore(name)

        TILES = B * NT
        CHUNKS = TILES // CT
        got = sb("got", [P, TILES, TOP, C])
        part = sb("part", [P, CHUNKS, TOP, CT, C])
        h, gates = t["h"], t["gates"]
        got_in = [sem(f"got_in{n}") for n in range(CHUNKS)]
        scaled, summed, h_ready, stored = (sem(n) for n in ("c_scaled", "c_summed", "h_ready", "stored"))
        CLS_ROW = PATCHES - (NT - 1) * TQ

        block = ctx.enter_context(nc.Block())

        @block.gpsimd
        def _(pool):
            rows_y = t["slot_y"].rearrange("p k c -> (p k) c")
            for i in range(TILES):
                for k in range(TOP):
                    nc.gpsimd.indirect_dma_start(
                        out=got[0:TQ, i, k, :], out_offset=None, in_=rows_y,
                        in_offset=bass.IndirectOffsetOnAxis(ap=t["rows"][0:TQ, i, k:k + 1], axis=0)).then_inc(got_in[i // CT], 16)

        @block.vector
        def _(dve):
            for n in range(CHUNKS):
                dve.wait_ge(got_in[n], 16 * TOP * CT)
                for k in range(TOP):
                    nc.vector.tensor_tensor(part[0:TQ, n, k], got[0:TQ, n * CT:n * CT + CT, k, :],
                                            gates[0:TQ, n * CT:n * CT + CT, k:k + 1].to_broadcast([TQ, CT, C]), ALU.mult).then_inc(scaled, 1)
                dve.wait_ge(scaled, 2 * n + 2)
                nc.vector.tensor_tensor(part[0:TQ, n, 0], part[0:TQ, n, 0], part[0:TQ, n, 1], ALU.add).then_inc(summed, 1)
                dve.wait_ge(summed, n + 1)
                tok = h[0:TQ, n * CT:n * CT + CT, :]
                nc.vector.tensor_tensor(tok, tok, part[0:TQ, n, 0], ALU.add).then_inc(h_ready, 1)

        @block.sync
        def _(sp):
            stores = 0
            for n in range(CHUNKS):
                b, c = divmod(n, NCH)
                sp.wait_ge(h_ready, n + 1)
                full = CT if c < NCH - 1 else CT - 1
                at = 1 + c * CH
                sp.dma_start(out[b, at:at + full * TQ, :].rearrange("(i p) e -> p i e", p=TQ),
                             h[0:TQ, n * CT:n * CT + full, :]).then_inc(stored, 16)
                stores += 1
                if full < CT:
                    sp.dma_start(out[b, at + full * TQ:N, :], h[0:CLS_ROW, n * CT + full, :]).then_inc(stored, 16)
                    sp.dma_start(out[b, 0:1, :], h[CLS_ROW:CLS_ROW + 1, n * CT + full, :]).then_inc(stored, 16)
                    stores += 2
            sp.wait_ge(stored, 16 * stores)


_INS = ["x", "cls_tok", "L0_tok_bases", "L0_tok_W_spline", "L0_tok_b_spline", "L0_tok_W_base", "L0_tok_b_base",
        "L0_attn_w_qkv", "L0_attn_w_proj", "L0_attn_b_proj", "L0_attn_rel_table", "L0_attn_rel_index",
        "L0_ffn_Wr", "L0_ffn_br", "L0_ffn_W1", "L0_ffn_b1", "L0_ffn_W2", "L0_ffn_b2"]


def kernel(**inputs):
    import numpy as np
    import concourse.bacc as bacc
    from concourse.bass_utils import run_bass_kernel_spmd

    nc = bacc.Bacc("TRN2", target_bir_lowering=False, num_devices=1)
    arrays, aps = {}, {}
    for name in _INS:
        a = np.ascontiguousarray(inputs[name])
        arrays[f"in_{name}"] = a
        aps[name] = nc.dram_tensor(f"in_{name}", a.shape, mybir.dt.from_np(a.dtype), kind="ExternalInput").ap()
    out = nc.dram_tensor("out_tokens", (B, N, C), F32, kind="ExternalOutput").ap()
    vit_layer(nc, aps, out)
    r = run_bass_kernel_spmd(nc, [arrays], core_ids=[0])
    return r.results[0]["out_tokens"]
```

```python
import struct
from contextlib import ExitStack

import concourse.bass as bass
from concourse import mybir

ALU = mybir.AluOpType
ACT = mybir.ActivationFunctionType
AX = mybir.AxisListType
F32 = mybir.dt.float32
BF16 = mybir.dt.bfloat16
I32 = mybir.dt.int32
U32 = mybir.dt.uint32
RMAX = bass.bass_isa.ReduceOp.max

P = 128
C = 64
H = 8
HD = C // H
NB = 3
B = 2
PATCHES = 64 * 64
N = PATCHES + 1
TQ = 114
CT = 4
CH = TQ * CT
NCH = 9
NT = NCH * CT
NP = NCH * CH
LASTX = PATCHES - (NCH - 1) * CH
KB = 33
KP = KB * P
KG = 3
NG = KB // KG
WS2 = 49
WIN0 = PATCHES - WS2
TABLE = 169
WIN_COLS = -(-WS2 * WS2 // P)
PARTS = 3
SROWS = PARTS * PARTS * HD
STACK = SROWS + PARTS
EPS = 1e-5
TWO_ONES = struct.unpack('<f', struct.pack('<I', 0x3F803F80))[0]
SLOTS = 2
HEAD_AT = 16
VW = HEAD_AT + HD + 1
EXPERTS = 64
TOP = 2
HID = 128
B1_ROW = C
B2_ROW = 96
PACK = HID + C
BLOCKS = (B * NT * TQ * TOP + EXPERTS * (P - 1)) // P + 1
BLOCKS += -BLOCKS % 8
CAP_BLOCKS = -(-(B * NT * TQ + P) // P)
VOID = EXPERTS * CAP_BLOCKS
BLOCK_STEPS = 27
SAFE = 30.0



def after(c):
    return c + 2


def before(c):
    return c + 1


def vit_layer(nc, ins, out):
    ctx = ExitStack()
    with ctx:
        def keep(name, shape, dt=F32):
            return ctx.enter_context(nc.sbuf_tensor(name, shape, dt))

        def dram(name, shape, dt=F32):
            return nc.dram_tensor(name, shape, dt).ap()

        t = {}
        t["h"] = keep("h", [P, B * NT, C])
        t["identity"] = keep("identity", [P, P])
        t["wprojT"] = keep("wprojT", [C + 1, C])
        t["window"] = keep("window", [WS2, H, WS2])
        t["qk_parts"] = dram("qk_parts", (B, PARTS, P, NP), BF16)
        t["v_rows"] = dram("v_rows", (B, KP, C))
        t["q_squares"] = dram("q_squares", (B * H, NP))
        t["head_tops"] = dram("head_tops", (2, B * H))
        t["window_rows"] = dram("window_rows", (P * WIN_COLS, H))
        t["shift_parts"] = dram("shift_parts", (B * H, PARTS, NP), BF16)
        t["row_max"] = dram("row_max", (B * H, KP))
        t["slot_x"] = dram("slot_x", (VOID + BLOCKS, P, C))
        t["slot_y"] = dram("slot_y", (P, BLOCKS, C))
        t["weights"] = dram("weights", (EXPERTS, P, PACK))
        t["attn"] = keep("attn", [P, B * NT, C])
        t["voided"] = nc.alloc_semaphore("voided")
        t["packed"] = nc.alloc_semaphore("packed_w")
        with ExitStack() as stacks:
            def pairs(name, shape, dt=F32):
                return [[stacks.enter_context(nc.sbuf_tensor(f"{name}{u}{p}", shape, dt)) for p in range(2)] for u in range(SLOTS)]

            t["q_stack"] = pairs("q_stack", [STACK, NP], BF16)
            t["k_stack"] = pairs("k_stack", [STACK, KP], BF16)
            t["v_head"] = pairs("v_head", [P, KB, VW])
            t["win_head"] = pairs("win_head", [WS2, P])
            embed_and_project(nc, ins, t)
            settle_shifts(nc, ins, t)
            attend(nc, ins, t)
        t["at_f"] = keep("at_f", [P, B * NT, TOP])
        t["slots"] = keep("slots", [P, B * NT, TOP], I32)
        t["rows"] = keep("rows", [P, B * NT, TOP], I32)
        t["gates"] = keep("gates", [P, B * NT, TOP])
        t["ids"] = keep("ids", [P, EXPERTS])
        t["moved"] = keep("moved", [P, EXPERTS])
        t["blocks"] = dram("blocks", (2, BLOCKS), I32)
        route(nc, ins, t)
        run_experts(nc, ins, t)
        combine(nc, t, out)


def embed_and_project(nc, ins, t):
    ctx = ExitStack()
    with ctx:
        ctx.enter_context(nc.cleanup_on_exit())
        def sb(name, shape, dt=F32):
            return ctx.enter_context(nc.sbuf_tensor(name, shape, dt))

        def ps(name, shape, dt=F32):
            return ctx.enter_context(nc.psum_tensor(name, shape, dt))

        def sem(name):
            return nc.alloc_semaphore(name)

        def pair(name):
            return [sem(f"{name}{b}") for b in range(B)]

        h, identity, wprojT, window = (t[k] for k in ("h", "identity", "wprojT", "window"))
        k_stack, v_head, win_head = (t[k] for k in ("k_stack", "v_head", "win_head"))

        spl_raw = sb("spl_raw", [C, C, NB])
        base_raw = sb("base_raw", [C, C])
        mix_raw = sb("mix_raw", [C, 2, 2, C])
        qkv_raw = sb("qkv_raw", [C, 3, C])
        proj_raw = sb("proj_raw", [C, C])
        mixT = sb("mixT", [P, 2, C])
        qkvT = sb("qkvT", [C, 3 * C])
        bases = sb("bases", [P, NB])
        slope = sb("slope", [P, 2])
        bias_spline = sb("bias_spline", [P, C])
        bias_base = sb("bias_base", [P, C])
        bias_e = sb("bias_e", [P, C])
        table = sb("table", [H, TABLE])
        table_max = sb("table_max", [H, 1])
        heads_f = sb("heads_f", [P, 2, H])
        heads_of = sb("heads_of", [P, 2, H], BF16)
        qscale = sb("qscale", [P, 1])
        power = sb("power", [P, CT])
        x2 = sb("x2", [P, B, PATCHES])
        feat = sb("feat", [P, B, 2, CH])
        total = sb("total", [P, B, CT])
        neg_mean = sb("neg_mean", [P, B, CT])
        centred = sb("centred", [P, B, CT, C])
        square = sb("square", [P, B, CT, C])
        variance = sb("variance", [P, B, CT])
        var_eps = sb("var_eps", [P, B, CT])
        rstd = sb("rstd", [P, B, CT])
        xn = sb("xn", [P, B, CT, C])
        xnT = sb("xnT", [C, B, CH])
        qk = sb("qk", [P, B, CH])
        rest1 = sb("rest1", [P, B, CH])
        qksq = sb("qksq", [P, B, CH], BF16)
        qkp = sb("qkp", [P, B, PARTS, CH], BF16)
        vout = sb("vout", [P, B, CT, C])
        zeros = sb("zeros", [P, C])
        kn = sb("kn", [H, B, NCH])
        kmax = sb("kmax", [H, B])
        qn = sb("qn", [H, B, CH])
        win_index = sb("win_index", [P, WIN_COLS], I32)
        win_bias = sb("win_bias", [P, WIN_COLS, H])
        win_raw = sb("win_raw", [WS2, WS2, H])
        VOIDS = BLOCKS // (NCH - 1)
        assert VOIDS * (NCH - 1) == BLOCKS and EXPERTS % (NCH - 1) == 0
        void = sb("void", [P, VOIDS * C])
        b2_in = sb("b2_in", [EXPERTS, C])
        b2_rest = sb("b2_rest", [EXPERTS, C])
        b2_parts = sb("b2_parts", [EXPERTS, PARTS, C], BF16)

        ps_h = ps("ps_h", [P, B, 512])
        ps_qk = ps("ps_qk", [P, B, 512])
        ps_n = ps("ps_n", [H, 2, 512])
        ps_t = ps("ps_t", [P, 512])
        ps_v = ps("ps_v", [P, 512])

        w_in, ident, turned, turned_out, consts = (sem(n) for n in ("w_in", "ident", "turned", "turned_out", "consts"))
        packed = sem("packed")
        x_in = pair("x_in")
        feat_done, silu_done, mixed, h_done = pair("feat_done"), pair("silu_done"), pair("mixed"), pair("h_done")
        sum_done, mean_done, centre_done, square_done = (pair(n) for n in ("sum_done", "mean_done", "centre_done", "square_done"))
        var_done, eps_done, rstd_done, norm_done = (pair(n) for n in ("var_done", "eps_done", "rstd_done", "norm_done"))
        xnT_ps, xnT_done, qk_ps, v_ps, n_ps = (pair(n) for n in ("xnT_ps", "xnT_done", "qk_ps", "v_ps", "n_ps"))
        qk_done, qksq_done, v_done, qn_done, kn_done = (pair(n) for n in ("qk_done", "qksq_done", "v_done", "qn_done", "kn_done"))
        hi_done, rest1_done, mid_done, rest2_done, parts_done = (pair(n) for n in ("hi_done", "rest1_done", "mid_done", "rest2_done", "parts_done"))
        parts_out, v_out = pair("parts_out"), pair("v_out")
        padded, cls_in, zeroed, v_pad, held, packed_raw = (
            sem(n) for n in ("padded", "cls_in", "zeroed", "v_pad", "held", "packed_raw"))
        kmax_done, table_done, tops_out = (sem(n) for n in ("kmax_done", "table_done", "tops_out"))
        qn_out = pair("qn_out")
        ones_set, attn_set, void_set, b2_loaded, b2_split = (sem(n) for n in ("ones_set", "attn_set", "void_set", "b2_loaded", "b2_split"))
        index_clear, index_in, gathered, rows_out, window_in = (
            sem(n) for n in ("index_clear", "index_in", "gathered", "rows_out", "window_in"))

        xflat = ins["x"].rearrange("b c a w -> b c (a w)")
        cls_row = ins["cls_tok"].rearrange("a b c -> (a b) c")
        LOADS = 9
        TURNS = 6
        CLS_ROW = PATCHES - (NT - 1) * TQ

        block = ctx.enter_context(nc.Block())

        def chunks(eng, body):
            with eng.Fori(0, NCH - 1) as c:
                body(c, CH)
            body(NCH - 1, LASTX)

        def pipelined(eng, head, turn, tail):
            head(0, CH)
            with eng.Fori(0, NCH - 2) as c:
                turn(c, CH)
            turn(NCH - 2, LASTX)
            tail(NCH - 1)

        @block.sync
        def _(sp):
            def load(dst, src):
                sp.dma_start(dst, src).then_inc(w_in, 16)

            for b in range(B):
                for s in (parts_out, v_out, qn_out):
                    sp.sem_inc(s[b], 16)
            load(spl_raw[:], ins["L0_tok_W_spline"].rearrange("e (c k) -> e c k", k=NB))
            load(base_raw[:], ins["L0_tok_W_base"])
            for half in range(2):
                load(bases[C * half:C * half + C, :], ins["L0_tok_bases"])
            for half in range(2):
                sp.dma_start(x2[C * half:C * half + C, 0, :], xflat[0]).then_inc(x_in[0], 16)
            load(qkv_raw[:], ins["L0_attn_w_qkv"].rearrange("(s e) c -> e s c", s=3))
            load(proj_raw[:], ins["L0_attn_w_proj"])
            load(bias_spline[:], ins["L0_tok_b_spline"].partition_broadcast(P))
            load(bias_base[:], ins["L0_tok_b_base"].partition_broadcast(P))
            for half in range(2):
                sp.dma_start(x2[C * half:C * half + C, 1, :], xflat[1]).then_inc(x_in[1], 16)
            with nc.allow_non_contiguous_dma(reason="a table of 169 x 8, once"):
                load(table[:], ins["L0_attn_rel_table"].rearrange("r h -> h r"))
            sp.dma_start(b2_in[:], ins["L0_ffn_b2"]).then_inc(b2_loaded, 16)
            sp.wait_ge(padded, 1)
            for b in range(B):
                sp.dma_start(h[CLS_ROW:CLS_ROW + 1, b * NT + NT - 1, :], cls_row).then_inc(cls_in, 16)
            sp.wait_ge(zeroed, 1)
            for b in range(B):
                sp.dma_start(t["v_rows"][b, NP:KP, :], zeros[0:KP - NP, :]).then_inc(v_pad, 16)

            def store(c, n):
                for b in range(B):
                    sp.wait_ge(parts_done[b], after(c))
                    sp.sem_inc(held, 1)
                    sp.dma_start(t["qk_parts"][b][:, :, bass.ds(c * CH, CH)].rearrange("s p n -> p s n"),
                                 qkp[:, b]).then_inc(parts_out[b], 16)
                    sp.wait_ge(v_done[b], after(c))
                    sp.sem_inc(held, 1)
                    sp.dma_start(t["v_rows"][b][bass.ds(c * CH, CH), :].rearrange("(i p) e -> p i e", p=TQ),
                                 vout[0:TQ, b]).then_inc(v_out[b], 16)
                    sp.wait_ge(qn_done[b], after(c))
                    sp.sem_inc(held, 1)
                    sp.dma_start(t["q_squares"][b * H:b * H + H, bass.ds(c * CH, CH)], qn[:, b]).then_inc(qn_out[b], 16)
            sp.wait_ge(gathered, 16 * WIN_COLS)
            sp.dma_start(t["window_rows"].rearrange("(p r) h -> p (r h)", p=P),
                         win_bias[:].rearrange("p r h -> p (r h)")).then_inc(rows_out, 16)
            sp.wait_ge(rows_out, 16)
            sp.dma_start(win_raw[:].rearrange("n m h -> n (m h)"),
                         t["window_rows"][0:WS2 * WS2, :].rearrange("(n m) h -> n (m h)", m=WS2)).then_inc(window_in, 16)
            chunks(sp, store)
            sp.wait_ge(kmax_done, B)
            for b in range(B):
                sp.dma_start(t["head_tops"][0:1, b * H:b * H + H].rearrange("a h -> h a"), kmax[:, b:b + 1]).then_inc(tops_out, 16)
            sp.wait_ge(table_done, 1)
            for b in range(B):
                sp.dma_start(t["head_tops"][1:2, b * H:b * H + H].rearrange("a h -> h a"), table_max[:]).then_inc(tops_out, 16)
            sp.wait_ge(v_pad, 16 * B)
            for b in range(B):
                sp.wait_ge(parts_out[b], 16 * (NCH + 1))
                sp.wait_ge(v_out[b], 16 * (NCH + 1))
                sp.wait_ge(qn_out[b], 16 * (NCH + 1))
            sp.wait_ge(tops_out, 16 * 2 * B)
            sp.wait_ge(attn_set, 4 * SLOTS)

        @block.gpsimd
        def _(pool):
            for b in range(B):
                for s in (eps_done, rstd_done):
                    pool.sem_inc(s[b], 1)
            nc.gpsimd.memset(identity[:], 0.0).then_inc(ident, 1)
            pool.wait_ge(ident, 1)
            nc.gpsimd.affine_select(out=identity[:], in_=identity[:], compare_op=ALU.not_equal, fill=1.0, base=0,
                                    pattern=[[-1, P]], channel_multiplier=1).then_inc(ident, 1)
            nc.gpsimd.memset(power[:], -0.5).then_inc(consts, 1)
            nc.gpsimd.memset(win_index[:], 0).then_inc(index_clear, 1)
            pool.wait_ge(index_clear, 1)
            whole = WS2 * WS2 // WIN_COLS
            index = ins["L0_attn_rel_index"]
            pool.dma_start(win_index[0:whole, :], index[0:whole * WIN_COLS].rearrange("(p r) -> p r", r=WIN_COLS)).then_inc(index_in, 16)
            pool.dma_start(win_index[whole:whole + 1, 0:WS2 * WS2 - whole * WIN_COLS],
                           index[whole * WIN_COLS:WS2 * WS2].rearrange("(p r) -> p r", p=1)).then_inc(index_in, 16)
            pool.wait_ge(index_in, 32)
            for r in range(WIN_COLS):
                nc.gpsimd.indirect_dma_start(out=win_bias[:, r, :], out_offset=None, in_=ins["L0_attn_rel_table"],
                                             in_offset=bass.IndirectOffsetOnAxis(ap=win_index[:, r:r + 1], axis=0)).then_inc(gathered, 16)
            nc.gpsimd.memset(heads_f[:], 1.0).then_inc(consts, 1)
            pool.wait_ge(consts, 2)
            nc.gpsimd.affine_select(out=heads_f[:], in_=heads_f[:], compare_op=ALU.is_ge, fill=0.0, base=0,
                                    pattern=[[-C, 2], [-HD, H]], channel_multiplier=1).then_inc(consts, 1)
            pool.wait_ge(consts, 3)
            nc.gpsimd.affine_select(out=heads_f[:], in_=heads_f[:], compare_op=ALU.is_ge, fill=0.0, base=HD - 1,
                                    pattern=[[C, 2], [HD, H]], channel_multiplier=-1).then_inc(consts, 1)

            def step(c, n):
                for b in range(B):
                    pool.wait_ge(var_done[b], after(c))
                    pool.sem_inc(held, 1)
                    nc.gpsimd.tensor_scalar(var_eps[0:TQ, b], variance[0:TQ, b], 1.0 / C, EPS, ALU.mult,
                                            ALU.add).then_inc(eps_done[b], 1)
                    pool.wait_ge(eps_done[b], after(c))
                    nc.gpsimd.tensor_tensor(out=rstd[0:TQ, b], in0=var_eps[0:TQ, b], in1=power[0:TQ],
                                            op=ALU.pow).then_inc(rstd_done[b], 1)

            packs, packed_w, voided = t["weights"], t["packed"], t["voided"]
            each = EXPERTS // (NCH - 1)

            def prepare(c):
                blocks = t["slot_x"][bass.ds(c * VOIDS + VOID, VOIDS)]
                pool.dma_start(blocks.rearrange("k p c -> p k c"), void[:].rearrange("p (k c) -> p k c", c=C)).then_inc(voided, 16)
                pool.dma_start(packs[bass.ds(c * each, each), B1_ROW:P, 0:HID].rearrange("e r c -> r e c"),
                               void[0:P - B1_ROW, 0:each * HID].rearrange("r (e c) -> r e c", c=HID)).then_inc(voided, 16)
                for columns, rows, name in ((slice(0, HID), slice(0, C), "L0_ffn_W1"), (slice(HID, PACK), slice(0, P), "L0_ffn_W2")):
                    pool.dma_start(packs[bass.ds(c * each, each), rows, columns], ins[name][bass.ds(c * each, each)]).then_inc(packed_w, 16)

            pool.wait_ge(void_set, 1)
            with pool.Fori(0, NCH - 1) as c:
                step(c, CH)
                prepare(c)
            step(NCH - 1, LASTX)
            pool.wait_ge(voided, 16 * 2 * (NCH - 1))
            pool.wait_ge(b2_split, 4)
            pool.dma_start(packs[:, B1_ROW:B1_ROW + 1, 0:HID], ins["L0_ffn_b1"].unsqueeze(1)).then_inc(packed_w, 16)
            pool.dma_start(packs[:, B2_ROW:B2_ROW + PARTS, 0:C // 2], b2_parts[:].bitcast(F32)).then_inc(packed_w, 16)

        @block.scalar
        def _(act):
            for b in range(B):
                for s in (feat_done, xnT_done, qk_done, qksq_done, v_done, qn_done):
                    act.sem_inc(s[b], 1)
            act.wait_ge(packed, 2)
            for b in range(B):
                act.wait_ge(x_in[b], 32)

            def head(c, n):
                for b in range(B):
                    act.wait_ge(mixed[b], before(c))
                    act.wait_ge(silu_done[b], before(c))
                    for f in range(2):
                        last = nc.scalar.activation(feat[:, b, f, 0:n], x2[:, b, bass.ds(c * CH, n)], ACT.Sigmoid,
                                                    scale=slope[:, f:f + 1])
                    last.then_inc(feat_done[b], 1)

            def tail(c):
                for b in range(B):
                    act.wait_ge(xnT_ps[b], after(c))
                    act.wait_ge(v_ps[b], before(c))
                    nc.scalar.copy(xnT[:, b], ps_t[0:C, 0:CH]).then_inc(xnT_done[b], 1)
                    act.wait_ge(qk_ps[b], after(c))
                    act.wait_ge(parts_done[b], before(c))
                    act.wait_ge(qksq_done[b], before(c))
                    nc.scalar.activation(qk[:, b], ps_qk[:, b, 0:CH], ACT.Copy, scale=qscale[:]).then_inc(qk_done[b], 1)
                    act.wait_ge(qk_done[b], after(c))
                    act.wait_ge(n_ps[b], before(c))
                    nc.scalar.activation(qksq[:, b], qk[:, b], ACT.Square).then_inc(qksq_done[b], 1)
                    act.wait_ge(v_ps[b], after(c))
                    act.wait_ge(v_out[b], 16 * before(c))
                    nc.scalar.copy(vout[0:TQ, b].rearrange("p i e -> p (i e)"), ps_v[0:TQ, 0:CT * C]).then_inc(v_done[b], 1)
                for b in range(B):
                    act.wait_ge(n_ps[b], after(c))
                    act.wait_ge(qn_out[b], 16 * before(c))
                    nc.scalar.copy(qn[:, b], ps_n[:, 0, 0:CH]).then_inc(qn_done[b], 1)

            def turn(c, n):
                head(c + 1, n)
                tail(c)
            nc.scalar.preload_act_table(ACT.Sigmoid)
            pipelined(act, head, turn, tail)

        @block.vector
        def _(dve):
            for b in range(B):
                for s in (silu_done, h_done, sum_done, mean_done, centre_done, square_done, var_done, norm_done, hi_done,
                          rest1_done, mid_done, rest2_done, parts_done, kn_done):
                    dve.sem_inc(s[b], 1)
            nc.vector.memset(zeros[:], 0.0).then_inc(zeroed, 1)
            for b in range(B):
                last = nc.vector.memset(h[96:TQ, b * NT + NT - 1, :], 0.0)
            last.then_inc(padded, 1)
            for u in range(SLOTS):
                for p in range(2):
                    nc.vector.memset(k_stack[u][p][C:STACK, 0:NP].bitcast(F32), TWO_ONES)
                    nc.vector.memset(k_stack[u][p][:, NP:KP], 0.0)
            for u in range(SLOTS):
                for p in range(2):
                    nc.vector.memset(v_head[u][p][:], 0.0).then_inc(ones_set, 1)
                    nc.vector.memset(win_head[u][p][:], 0.0).then_inc(ones_set, 1)
            dve.wait_ge(ones_set, 8)
            for u in range(SLOTS):
                for p in range(2):
                    ones = slice(p * HEAD_AT + HD, p * HEAD_AT + HD + 1)
                    nc.vector.memset(v_head[u][p][:, 0:KB - 1, ones], 1.0).then_inc(attn_set, 1)
                    nc.vector.memset(v_head[u][p][0:1, KB - 1, ones], 1.0).then_inc(attn_set, 1)
            nc.vector.memset(void[:], 0.0).then_inc(void_set, 1)
            dve.wait_ge(b2_loaded, 16)
            nc.vector.tensor_copy(b2_parts[:, 0], b2_in[:]).then_inc(b2_split, 1)
            dve.wait_ge(b2_split, 1)
            nc.vector.tensor_tensor(b2_rest[:], b2_in[:], b2_parts[:, 0], ALU.subtract).then_inc(b2_split, 1)
            dve.wait_ge(b2_split, 2)
            nc.vector.tensor_copy(b2_parts[:, 1], b2_rest[:]).then_inc(b2_split, 1)
            dve.wait_ge(b2_split, 3)
            nc.vector.tensor_tensor(b2_parts[:, 2], b2_rest[:], b2_parts[:, 1], ALU.subtract).then_inc(b2_split, 1)
            dve.wait_ge(w_in, 16 * LOADS)
            for f, half, src in ((0, 0, spl_raw[:, :, 0]), (0, 1, spl_raw[:, :, 1]), (1, 0, spl_raw[:, :, 2]),
                                 (1, 1, base_raw[:])):
                nc.vector.tensor_copy(mix_raw[:, f, half, :], src).then_inc(packed_raw, 1)
            nc.vector.tensor_copy(slope[0:C, 0:1], bases[0:C, 0:1])
            nc.vector.tensor_copy(slope[C:P, 0:1], bases[C:P, 1:2])
            nc.vector.tensor_copy(slope[0:C, 1:2], bases[0:C, 2:3])
            nc.vector.memset(slope[C:P, 1:2], 1.0).then_inc(packed, 1)
            nc.vector.memset(qscale[C:P, :], 1.0)
            nc.vector.memset(qscale[0:C, :], float(HD) ** -0.5).then_inc(packed, 1)
            nc.vector.tensor_tensor(bias_e[:], bias_spline[:], bias_base[:], ALU.add).then_inc(packed, 1)
            nc.vector.tensor_reduce(table_max[:], table[:], AX.X, ALU.max).then_inc(packed, 1)
            dve.wait_ge(consts, 4)
            nc.vector.tensor_copy(heads_of[:], heads_f[:]).then_inc(packed, 1)
            for n, (dst, src) in enumerate(((mixT[:, 0, :], ps_t[:, 0:C]), (mixT[:, 1, :], ps_t[:, C:2 * C]),
                                            (qkvT[:, 0:C], ps_t[0:C, 2 * C:3 * C]), (qkvT[:, C:2 * C], ps_t[0:C, 3 * C:4 * C]),
                                            (qkvT[:, 2 * C:], ps_t[0:C, 4 * C:5 * C]), (wprojT[0:C], ps_t[0:C, 5 * C:6 * C]))):
                dve.wait_ge(turned, 1)
                nc.vector.tensor_copy(dst, src).then_inc(turned_out, 1)
            dve.wait_ge(padded, 1)
            dve.wait_ge(packed, 5)

            def silu(c, n):
                for b in range(B):
                    dve.wait_ge(feat_done[b], after(c))
                    nc.vector.tensor_tensor(feat[C:P, b, 1, 0:n], feat[C:P, b, 1, 0:n], x2[C:P, b, bass.ds(c * CH, n)],
                                            ALU.mult).then_inc(silu_done[b], 1)

            def tokens(b, c, n):
                tile = b * NT + c * CT
                full = n // TQ
                dve.wait_ge(mixed[b], after(c))
                dst = h[0:TQ, bass.ds(tile, full), :]
                psv = ps_h[:, b, 0:CT * C].rearrange("p (i e) -> p i e", e=C)
                over = bias_e[0:TQ].unsqueeze(1).to_broadcast([TQ, full, C])
                last = nc.vector.tensor_tensor(dst, psv[0:TQ, 0:full], over, ALU.add)
                if full < CT:
                    rows = n - full * TQ
                    last = nc.vector.tensor_tensor(h[0:rows, tile + full, :], psv[0:rows, full], bias_e[0:rows], ALU.add)
                    dve.wait_ge(cls_in, 16 * B)
                last.then_inc(h_done[b], 1)
                tok = h[0:TQ, bass.ds(tile, CT), :]
                dve.wait_ge(h_done[b], after(c))
                dve.sem_inc(held, 1)
                nc.vector.tensor_reduce(total[0:TQ, b], tok, AX.X, ALU.add).then_inc(sum_done[b], 1)
                dve.wait_ge(sum_done[b], after(c))
                nc.vector.tensor_scalar(neg_mean[0:TQ, b], total[0:TQ, b], -1.0 / C, None, ALU.mult).then_inc(mean_done[b], 1)
                dve.wait_ge(mean_done[b], after(c))
                nc.vector.tensor_tensor(centred[0:TQ, b], tok, neg_mean[0:TQ, b].unsqueeze(2).to_broadcast([TQ, CT, C]),
                                        ALU.add).then_inc(centre_done[b], 1)
                dve.wait_ge(centre_done[b], after(c))
                nc.vector.tensor_tensor(square[0:TQ, b], centred[0:TQ, b], centred[0:TQ, b], ALU.mult).then_inc(square_done[b], 1)
                dve.wait_ge(square_done[b], after(c))
                nc.vector.tensor_reduce(variance[0:TQ, b], square[0:TQ, b], AX.X, ALU.add).then_inc(var_done[b], 1)

            def normalise(c):
                for b in range(B):
                    dve.wait_ge(rstd_done[b], after(c))
                    dve.wait_ge(xnT_ps[b], before(c))
                    nc.vector.tensor_tensor(xn[0:TQ, b], centred[0:TQ, b], rstd[0:TQ, b].unsqueeze(2).to_broadcast([TQ, CT, C]),
                                            ALU.mult).then_inc(norm_done[b], 1)

            def split(b, c):
                dve.wait_ge(qk_done[b], after(c))
                dve.wait_ge(parts_out[b], 16 * before(c))
                nc.vector.tensor_copy(qkp[:, b, 0], qk[:, b]).then_inc(hi_done[b], 1)
                dve.wait_ge(hi_done[b], after(c))
                nc.vector.tensor_tensor(rest1[:, b], qk[:, b], qkp[:, b, 0], ALU.subtract).then_inc(rest1_done[b], 1)
                dve.wait_ge(rest1_done[b], after(c))
                nc.vector.tensor_copy(qkp[:, b, 1], rest1[:, b]).then_inc(mid_done[b], 1)
                dve.wait_ge(mid_done[b], after(c))
                nc.vector.tensor_tensor(qkp[:, b, 2], rest1[:, b], qkp[:, b, 1], ALU.subtract).then_inc(parts_done[b], 1)

            def longest(c):
                for b in range(B):
                    dve.wait_ge(n_ps[b], after(c))
                    dve.sem_inc(held, 1)
                    nc.vector.tensor_reduce(kn[:, b, bass.ds(c, 1)], ps_n[:, 1, 0:CH], AX.X, ALU.max).then_inc(kn_done[b], 1)

            def head(c, n):
                silu(c, n)
                for b in range(B):
                    tokens(b, c, n)
                normalise(c)

            def turn(c, n):
                silu(c + 1, n)
                for b in range(B):
                    tokens(b, c + 1, n)
                    split(b, c)
                longest(c)
                normalise(c + 1)

            def tail(c):
                for b in range(B):
                    split(b, c)
                longest(c)
            pipelined(dve, head, turn, tail)
            for b in range(B):
                dve.wait_ge(kn_done[b], after(NCH - 1))
                nc.vector.tensor_reduce(kmax[:, b:b + 1], kn[:, b], AX.X, ALU.max).then_inc(kmax_done, 1)
            nc.vector.tensor_scalar(table_max[:], table_max[:], 0.0, None, ALU.max).then_inc(table_done, 1)
            dve.wait_ge(window_in, 16)
            nc.vector.tensor_copy(window[:], win_raw[:].rearrange("n m h -> n h m")).then_inc(table_done, 1)

        @block.tensor
        def _(pe):
            for b in range(B):
                for s in (mixed, xnT_ps, qk_ps, v_ps, n_ps):
                    pe.sem_inc(s[b], 1)
            pe.wait_ge(ident, 2)
            pe.wait_ge(w_in, 16 * LOADS)
            pe.wait_ge(packed_raw, 4)
            eye = identity[0:C, 0:C]
            for f in range(2):
                nc.tensor.transpose(ps_t[:, C * f:C * f + C], mix_raw[:, f].rearrange("e a c -> e (a c)"), eye)
            for s in range(3):
                nc.tensor.transpose(ps_t[0:C, C * (2 + s):C * (3 + s)], qkv_raw[:, s, :], eye)
            nc.tensor.transpose(ps_t[0:C, 5 * C:6 * C], proj_raw[:], eye).then_inc(turned, 1)
            pe.wait_ge(turned_out, TURNS)
            pe.wait_ge(packed, 5)

            def mix(b, c, n):
                pe.wait_ge(silu_done[b], after(c))
                pe.wait_ge(h_done[b], before(c))
                for i in range(CT):
                    rows = min(TQ, n - i * TQ)
                    for f in range(2):
                        last = nc.tensor.matmul(ps_h[0:rows, b, C * i:C * i + C], feat[:, b, f, TQ * i:TQ * i + rows],
                                                mixT[:, f, :], start=(f == 0), stop=(f == 1))
                last.then_inc(mixed[b], 1)

            def turn_rows(b, c):
                pe.wait_ge(norm_done[b], after(c))
                pe.wait_ge(xnT_done[1 - b], after(c) if b else before(c))
                pe.sem_inc(held, 1)
                for i in range(CT):
                    last = nc.tensor.transpose(ps_t[0:C, TQ * i:TQ * i + TQ], xn[0:TQ, b, i, :], identity[0:TQ, 0:TQ])
                last.then_inc(xnT_ps[b], 1)

            def project(b, c):
                pe.wait_ge(xnT_done[b], after(c))
                pe.wait_ge(qk_done[b], before(c))
                nc.tensor.matmul(ps_qk[:, b, 0:CH], qkvT[:, 0:2 * C], xnT[:, b], start=True, stop=True).then_inc(qk_ps[b], 1)
                pe.wait_ge(v_done[1 - b], after(c) if b else before(c))
                for i in range(CT):
                    last = nc.tensor.matmul(ps_v[0:TQ, C * i:C * i + C], xnT[:, b, TQ * i:TQ * i + TQ], qkvT[:, 2 * C:],
                                            start=True, stop=True)
                last.then_inc(v_ps[b], 1)

            def squares(c):
                for b in range(B):
                    pe.wait_ge(qksq_done[b], after(c))
                    pe.wait_ge(qn_done[1 - b], after(c) if b else before(c))
                    pe.wait_ge(kn_done[1 - b], after(c) if b else before(c))
                    for w in range(2):
                        last = nc.tensor.matmul(ps_n[:, w, 0:CH], heads_of[:, w, :], qksq[:, b], start=True, stop=True)
                    last.then_inc(n_ps[b], 1)

            def head(c, n):
                for b in range(B):
                    mix(b, c, n)

            def turn(c, n):
                for b in range(B):
                    turn_rows(b, c)
                    mix(b, c + 1, n)
                    project(b, c)
                squares(c)

            def tail(c):
                for b in range(B):
                    turn_rows(b, c)
                    project(b, c)
                squares(c)
            pipelined(pe, head, turn, tail)


def load_stack(sp, t, b, head, q_stack, k_stack, with_shift, done):
    parts = t["qk_parts"][b] if isinstance(b, int) else t["qk_parts"][bass.ds(b, 1)].rearrange("a s r n -> (a s) r n")
    for j in range(PARTS):
        rows = slice(j * PARTS * HD, (j + 1) * PARTS * HD)
        of_q = parts[j:j + 1, bass.ds(head * HD, HD), :].to_broadcast([PARTS, HD, NP])
        sp.dma_start(q_stack[rows, 0:NP], of_q).then_inc(done, 16)
        of_k = parts[:, bass.ds(head * HD + C, HD), :]
        sp.dma_start(k_stack[rows, 0:NP], of_k).then_inc(done, 16)
    if with_shift:
        of_shift = t["shift_parts"][bass.ds(b * H + head, 1)].rearrange("a s n -> (a s) n")
        sp.dma_start(q_stack[SROWS:STACK, 0:NP], of_shift).then_inc(done, 16)


def settle_shifts(nc, ins, t):
    ctx = ExitStack()
    with ctx:
        ctx.enter_context(nc.cleanup_on_exit())
        def sb(name, shape, dt=F32):
            return ctx.enter_context(nc.sbuf_tensor(name, shape, dt))

        def sem(name):
            return nc.alloc_semaphore(name)

        COLS = B * H * NP // P
        shift = sb("shift", [P, COLS])
        k_top = sb("k_top", [P, 1])
        k_scale = sb("k_scale", [P, 1])
        bias_top = sb("bias_top", [P, 1])
        top = sb("top", [P, 1])
        top_all = sb("top_all", [P, 1])
        wide = sb("wide", [1, 1])
        general = sb("general", [1, 1], I32)
        rest1 = sb("s_rest1", [P, COLS])
        parts = sb("s_parts", [P, PARTS, COLS], BF16)
        q_stack = sb("m_q_stack", [SROWS, KP], BF16)
        k_stack = sb("m_k_stack", [SROWS, NP], BF16)
        row_top = sb("row_top", [P, NCH])
        row_tops = sb("row_tops", [P, KB])
        place = sb("place", [WS2, P])
        ps_s = ctx.enter_context(nc.psum_tensor("ps_s", [P, PARTS, 512], F32))

        loaded, scaled, rooted, raised, top_done, top_shared, wide_done, flagged = (sem(n) for n in (
            "loaded", "scaled", "rooted", "raised", "top_done", "top_shared", "wide_done", "flagged"))
        split, parts_out = sem("split"), sem("s_parts_out")
        prepared, placed, stack_in, piece_done, piece_read, tile_done, head_out, max_in = (sem(n) for n in (
            "prepared", "placed", "m_stack_in", "piece_done", "piece_read", "tile_done", "head_out", "max_in"))
        held = sem("s_held")
        PIECES = NCH
        BANKS = 3
        PER_HEAD = KB * PIECES
        WINDOW_TILE = (WIN0 + WS2) // P - 1

        block = ctx.enter_context(nc.Block())

        @block.sync
        def _(sp):
            sp.dma_start(shift[:], t["q_squares"].rearrange("g (s n) -> (g s) n", n=COLS)).then_inc(loaded, 16)
            per = P // (B * H)
            for n, dst in enumerate((k_top, bias_top)):
                sp.dma_start(dst[:], t["head_tops"][n].unsqueeze(1).unsqueeze(2).to_broadcast([B * H, per, 1])).then_inc(loaded, 16)
            sp.wait_ge(flagged, 1)
            wide_bound = sp.value_load(general[0:1, 0:1], min_val=0, max_val=1)
            with sp.If(wide_bound > 0):
                sp.sem_inc(head_out, 16)
                sp.wait_ge(prepared, 1)
                with sp.Fori(0, B) as b:
                    with sp.Fori(0, H) as n:
                        sp.wait_ge(tile_done, (b * H + n) * KB + 1)
                        sp.sem_inc(held, 1)
                        load_stack(sp, t, b, n, q_stack, k_stack, False, stack_in)
                        sp.wait_ge(tile_done, (b * H + n) * KB + KB + 1)
                        sp.sem_inc(held, 1)
                        with nc.allow_non_contiguous_dma(reason="4097 maxima of a head"):
                            sp.dma_start(t["row_max"][bass.ds(b * H + n, 1), :].rearrange("a (i p) -> p (a i)", p=P),
                                         row_tops[:]).then_inc(head_out, 16)
                sp.wait_ge(head_out, 16 * B * H + 16)
                sp.dma_start(shift[:], t["row_max"][:, 0:NP].rearrange("g (s n) -> g s n", n=COLS)).then_inc(max_in, 16)
            with sp.Else():
                sp.sem_inc(held, 1)
            sp.wait_ge(split, 4)
            for j in range(PARTS):
                sp.dma_start(t["shift_parts"][:, j, :].rearrange("g (s n) -> g s n", n=COLS), parts[:, j, :]).then_inc(parts_out, 16)
            sp.wait_ge(parts_out, 16 * PARTS)

        @block.gpsimd
        def _(pool):
            nc.gpsimd.memset(place[:], 0.0).then_inc(placed, 1)
            pool.wait_ge(placed, 1)
            nc.gpsimd.affine_select(out=place[:], in_=place[:], compare_op=ALU.not_equal, fill=1.0, base=P - WS2,
                                    pattern=[[-1, P]], channel_multiplier=1).then_inc(placed, 1)
            pool.wait_ge(placed, 2)
            pool.wait_ge(top_done, 1)
            nc.gpsimd.partition_all_reduce(top_all[:], top[:], P, RMAX).then_inc(top_shared, 1)

        @block.scalar
        def _(act):
            act.wait_ge(scaled, 1)
            nc.scalar.activation(shift[:], shift[:], ACT.Sqrt, scale=k_scale[:]).then_inc(rooted, 1)

        @block.vector
        def _(dve):
            dve.wait_ge(loaded, 48)
            nc.vector.tensor_scalar(k_scale[:], k_top[:], 1.03, None, ALU.mult).then_inc(scaled, 1)
            dve.wait_ge(rooted, 1)
            nc.vector.tensor_scalar(shift[:], shift[:], bias_top[:], None, ALU.add).then_inc(raised, 1)
            dve.wait_ge(raised, 1)
            nc.vector.tensor_reduce(top[:], shift[:], AX.X, ALU.max).then_inc(top_done, 1)
            dve.wait_ge(top_shared, 1)
            nc.vector.tensor_scalar(wide[:], top_all[0:1, :], SAFE, None, ALU.is_gt).then_inc(wide_done, 1)
            dve.wait_ge(wide_done, 1)
            nc.vector.tensor_copy(general[:], wide[:]).then_inc(flagged, 1)
            dve.wait_ge(flagged, 1)
            wide_bound = dve.value_load(general[0:1, 0:1], min_val=0, max_val=1)
            with dve.If(wide_bound > 0):
                dve.sem_inc(tile_done, 1)
                dve.sem_inc(piece_read, BANKS)
                nc.vector.memset(q_stack[:, NP:KP], 0.0).then_inc(prepared, 1)
                with dve.Fori(0, B * H) as n:
                    with dve.Fori(0, KB) as i:
                        dve.wait_ge(tile_done, n * KB + i + 1)
                        for k in range(PIECES):
                            keys = CH if k < PIECES - 1 else N - (PIECES - 1) * CH
                            dve.wait_ge(piece_done, (n * KB + i) * PIECES + k + 1)
                            nc.vector.tensor_reduce(row_top[:, k:k + 1], ps_s[:, k % BANKS, 0:keys], AX.X, ALU.max).then_inc(piece_read, 1)
                        dve.wait_ge(piece_read, (n * KB + i) * PIECES + PIECES + BANKS)
                        dve.wait_ge(head_out, 16 * n + 16)
                        dve.sem_inc(held, 1)
                        nc.vector.tensor_reduce(row_tops[:, bass.ds(i, 1)], row_top[:], AX.X, ALU.max).then_inc(tile_done, 1)
                dve.wait_ge(max_in, 16)
                dve.sem_inc(held, 1)
            with dve.Else():
                dve.sem_inc(held, 1)
            nc.vector.tensor_scalar(parts[:, 0, :], shift[:], -1.0, None, ALU.mult).then_inc(split, 1)
            dve.wait_ge(split, 1)
            nc.vector.scalar_tensor_tensor(out=rest1[:], in0=shift[:], scalar=-1.0, in1=parts[:, 0, :], op0=ALU.mult,
                                           op1=ALU.subtract).then_inc(split, 1)
            dve.wait_ge(split, 2)
            nc.vector.tensor_copy(parts[:, 1, :], rest1[:]).then_inc(split, 1)
            dve.wait_ge(split, 3)
            nc.vector.tensor_tensor(parts[:, 2, :], rest1[:], parts[:, 1, :], ALU.subtract).then_inc(split, 1)

        @block.tensor
        def _(pe):
            pe.wait_ge(flagged, 1)
            wide_bound = pe.value_load(general[0:1, 0:1], min_val=0, max_val=1)
            with pe.If(wide_bound > 0):
                pe.wait_ge(prepared, 1)
                pe.wait_ge(placed, 2)
                pe.sem_inc(held, 1)

                def tile(n, i, windowed):
                    for k in range(PIECES):
                        keys = CH if k < PIECES - 1 else N - (PIECES - 1) * CH
                        pe.wait_ge(piece_read, (n * KB + i) * PIECES + k + 1)
                        pe.sem_inc(held, 1)
                        over = windowed and k == PIECES - 1
                        last = nc.tensor.matmul(ps_s[:, k % BANKS, 0:keys], q_stack[:, bass.ds(i * P, P)],
                                                k_stack[:, k * CH:k * CH + keys], start=True, stop=not over)
                        if over:
                            at = WIN0 - k * CH
                            last = nc.tensor.matmul(ps_s[:, k % BANKS, at:at + WS2], place[:],
                                                    windowed[0], start=False, stop=True)
                        last.then_inc(piece_done, 1)

                with pe.Fori(0, B) as b:
                    with pe.Fori(0, H) as hd:
                        n = pe.snap(b * H + hd)
                        pe.wait_ge(stack_in, n * (16 * 2 * PARTS) + 16 * 2 * PARTS)
                        pe.sem_inc(held, 1)
                        with pe.Fori(0, WINDOW_TILE) as i:
                            tile(n, i, None)
                        bias = t["window"][:, bass.ds(hd, 1), :].rearrange("n a m -> n (a m)")
                        tile(n, WINDOW_TILE, [bias])
                        tile(n, WINDOW_TILE + 1, None)
            with pe.Else():
                pe.sem_inc(held, 1)


def attend(nc, ins, t):
    ctx = ExitStack()
    with ctx:
        ctx.enter_context(nc.cleanup_on_exit())
        def sb(name, shape, dt=F32):
            return ctx.enter_context(nc.sbuf_tensor(name, shape, dt))

        def sem(name):
            return nc.alloc_semaphore(name)

        def pair(name):
            return [sem(f"{name}{n}") for n in range(2)]

        GROUPS = 2 * NG
        PAIRS = B * H // 2
        PER_IMAGE = H // 2 // SLOTS
        W = 32
        RING = 4
        ring_at = [g % 3 for g in range(GROUPS - RING)] + list(range(RING))
        back = [next(d for d in range(1, GROUPS + 1) if ring_at[(g - d) % GROUPS] == ring_at[g]) for g in range(GROUPS)]
        AHEAD = 2
        FINISH = 6

        q_stack, k_stack, v_head, win_head = (t[k] for k in ("q_stack", "k_stack", "v_head", "win_head"))
        v_all = sb("v_all", [P, B, KB, C])
        probs = sb("probs", [P, RING, KG, CH])
        o_rest = sb("o_rest", [P, 2, CH])
        o_parts = sb("o_parts", [P, 2, PARTS, CH], BF16)
        inverse = sb("inverse", [P, 2, CT, 2, 1])
        gather_f = sb("gather_f", [P, W])
        gather = sb("gather", [P, W], BF16)
        identity, attn = t["identity"], t["attn"]

        ps_s = ctx.enter_context(nc.psum_tensor("ps_scores", [P, 2, KG, 512], F32))
        ps_o = ctx.enter_context(nc.psum_tensor("ps_out", [P, 2, 512], F32))

        v_in, gather_set = sem("v_in"), sem("gather_set")
        stack_in, v_ready = pair("stack_in"), pair("v_ready")
        scored, exped, valued = sem("scored"), sem("exped"), sem("valued")
        parts_ready, turned, split, inverted, normed = (pair(n) for n in (
            "parts_ready", "o_turned", "o_split", "o_inverted", "normed"))
        cleared = sem("cleared")
        a_held = sem("a_held")
        LOADS = 16 * 2 * (2 * PARTS + 1)
        STAGED = 4
        PAIR_GROUPS = NCH * GROUPS
        TURNS = PAIRS // SLOTS
        START = PAIR_GROUPS + RING

        def bank_turn(turn_no, u, r, w):
            return turn_no * NCH + (u * NCH + w) // 2 + r

        block = ctx.enter_context(nc.Block())

        @block.sync
        def _(sp):
            with sp.Fori(0, B) as b:
                with sp.Fori(0, PER_IMAGE) as j:
                    for u in range(SLOTS):
                        sp.wait_ge(scored, (((b * PER_IMAGE + j) * SLOTS + u) - 1) * PAIR_GROUPS + START)
                        sp.sem_inc(a_held, 1)
                        for p in range(2):
                            load_stack(sp, t, b, j * 2 * SLOTS + 2 * u + p, q_stack[u][p], k_stack[u][p], True, stack_in[u])
            sp.wait_ge(t["voided"], 16 * 2 * (NCH - 1))
            sp.wait_ge(t["packed"], 16 * (2 * (NCH - 1) + 2))

        @block.gpsimd
        def _(pool):
            for b in range(B):
                pool.dma_start(v_all[:, b], t["v_rows"][b].rearrange("(k p) e -> p k e", p=P)).then_inc(v_in, 16)
            nc.gpsimd.memset(gather_f[:], 0.0).then_inc(gather_set, 1)
            for j in range(4):
                pool.wait_ge(gather_set, j + 1)
                nc.gpsimd.affine_select(out=gather_f[:], in_=gather_f[:], compare_op=ALU.not_equal, fill=1.0, base=-W * j,
                                        pattern=[[-1, W]], channel_multiplier=1).then_inc(gather_set, 1)
            pool.wait_ge(gather_set, 5)
            nc.gpsimd.tensor_copy(gather[:], gather_f[:]).then_inc(gather_set, 1)
            pool.wait_ge(v_in, 16 * B)
            pool.sem_inc(a_held, 1)
            with pool.Fori(0, B) as b:
                with pool.Fori(0, PER_IMAGE) as j:
                    for u in range(SLOTS):
                        pool.wait_ge(valued, (((b * PER_IMAGE + j) * SLOTS + u) - 1) * PAIR_GROUPS + START)
                        pool.sem_inc(a_held, 1)
                        for p in range(2):
                            head = j * 2 * SLOTS + 2 * u + p
                            nc.gpsimd.tensor_copy(v_head[u][p][:, :, p * HEAD_AT:p * HEAD_AT + HD],
                                                  v_all[:, bass.ds(b, 1), :, bass.ds(head * HD, HD)].rearrange("p a k e -> p (a k) e")
                                                  ).then_inc(v_ready[u], 1)
                            nc.gpsimd.tensor_copy(win_head[u][p][:, P - WS2:P],
                                                  t["window"][:, bass.ds(head, 1), :].rearrange("n a m -> n (a m)")
                                                  ).then_inc(v_ready[u], 1)

        @block.scalar
        def _(act):
            nc.scalar.preload_act_table(ACT.Exp)
            with act.Fori(0, PAIRS * NCH) as k:
                for g in range(GROUPS):
                    act.wait_ge(scored, k * GROUPS + g + 1 + START)
                    act.wait_ge(valued, k * GROUPS + g - back[g] + 1 + START)
                    nc.scalar.activation(probs[:, ring_at[g]], ps_s[:, g % 2, :, 0:CH], ACT.Exp).then_inc(exped, 1)

        @block.vector
        def _(dve):
            for p in range(2):
                dve.sem_inc(normed[p], 1)
            nc.vector.memset(ps_o[:], 0.0).then_inc(cleared, 1)
            nc.vector.memset(o_parts[:, 1], 0.0).then_inc(parts_ready[1], 1)

            def finish(b, j, u, r, w):
                bank = (u + w) % 2
                turn_no = b * PER_IMAGE + j
                m = dve.snap(bank_turn(turn_no, u, r, w))
                dve.wait_ge(valued, (turn_no * SLOTS * NCH + u * NCH + r * 2 + w + 1) * GROUPS + START)
                nc.vector.tensor_copy(o_parts[:, bank, 0], ps_o[:, bank, 0:CH]).then_inc(split[bank], 1)
                dve.wait_ge(split[bank], m * 3 + 1)
                nc.vector.tensor_tensor(o_rest[:, bank], ps_o[:, bank, 0:CH], o_parts[:, bank, 0], ALU.subtract).then_inc(split[bank], 1)
                dve.wait_ge(split[bank], m * 3 + 2)
                nc.vector.tensor_copy(o_parts[:, bank, 1], o_rest[:, bank]).then_inc(split[bank], 1)
                dve.wait_ge(split[bank], m * 3 + 3)
                nc.vector.tensor_tensor(o_parts[:, bank, 2], o_rest[:, bank], o_parts[:, bank, 1], ALU.subtract).then_inc(parts_ready[bank], 1)
                dve.wait_ge(turned[bank], m + 1 + bank)
                sums = ps_o[0:TQ, bank, 0:CT * W].rearrange("q (i p d) -> q i p d", p=2, d=HEAD_AT)
                dve.wait_ge(normed[bank], m + 1)
                nc.vector.reciprocal(inverse[0:TQ, bank], sums[:, :, :, HD:HD + 1]).then_inc(inverted[bank], 1)
                dve.wait_ge(inverted[bank], m + 1)
                dst = attn[0:TQ, bass.ds(b * NT + r * 2 * CT + w * CT, CT), bass.ds(j * (2 * SLOTS * HD) + 2 * u * HD, 2 * HD)]
                nc.vector.tensor_tensor(dst.rearrange("q i (p d) -> q i p d", p=2), sums[:, :, :, 0:HD],
                                        inverse[0:TQ, bank].to_broadcast([TQ, CT, 2, HD]), ALU.mult).then_inc(normed[bank], 1)

            with dve.Fori(0, B) as b:
                with dve.Fori(0, PER_IMAGE) as j:
                    for u in range(SLOTS):
                        with dve.Fori(0, NCH // 2) as r:
                            for w in range(2):
                                finish(b, j, u, r, w)
                        finish(b, j, u, NCH // 2, 0)

        @block.tensor
        def _(pe):
            pe.sem_inc(exped, AHEAD)
            pe.sem_inc(scored, START)
            pe.sem_inc(valued, START)

            def scores(u, c, g, windowed):
                p, first = g // NG, g % NG * KG
                for s in range(KG):
                    over = windowed and first + s == (WIN0 + WS2) // P - 1
                    last = nc.tensor.matmul(ps_s[:, g % 2, s, 0:CH], k_stack[u][p][:, (first + s) * P:(first + s + 1) * P],
                                            q_stack[u][p][:, bass.ds(c * CH, CH)], start=True, stop=not over)
                    if over:
                        at = WIN0 - (NCH - 1) * CH
                        last = nc.tensor.matmul(ps_s[:, g % 2, s, at:at + WS2], win_head[u][p][:], identity[0:WS2, 0:WS2],
                                                start=False, stop=True)
                last.then_inc(scored, 1)

            def values(u, bank, g):
                p, first = g // NG, g % NG * KG
                for s in range(KG):
                    kb = first + s
                    at = W * (kb % 4)
                    last = nc.tensor.matmul(ps_o[at:at + VW, bank, 0:CH], v_head[u][p][:, kb, :], probs[:, ring_at[g], s],
                                            start=p == 0 and kb < 4, stop=p == 1 and kb >= KB - 4)
                last.then_inc(valued, 1)

            def turn(bank):
                for i in range(CT):
                    for part in range(PARTS):
                        last = nc.tensor.matmul(ps_o[0:TQ, bank, W * i:W * i + W], o_parts[:, bank, part, TQ * i:TQ * i + TQ],
                                                gather[:], start=part == 0, stop=part == PARTS - 1)
                last.then_inc(turned[bank], 1)

            def body(turn_no, u, r, w, last_pair):
                k = (turn_no * SLOTS + u) * NCH + r * 2 + w
                bank, m = (u + w) % 2, bank_turn(turn_no, u, r, w)
                ends = isinstance(r, int)
                for g in range(AHEAD, GROUPS + AHEAD):
                    pe.wait_ge(exped, k * GROUPS + g + 1)
                    if g < GROUPS:
                        scores(u, r * 2 + w, g, ends)
                    elif not ends:
                        scores(u, r * 2 + (w + 1), g - GROUPS, False)
                    elif not last_pair:
                        if g == GROUPS:
                            pe.wait_ge(stack_in[1 - u], (turn_no + 1 + u) * LOADS)
                        scores(1 - u, 0, g - GROUPS, False)
                    if g == AHEAD:
                        pe.wait_ge(normed[bank], m + 1)
                    values(u, bank, g - AHEAD)
                    if g == FINISH:
                        pe.wait_ge(parts_ready[1 - bank], m + 1)
                        turn(1 - bank)

            def head_pair(turn_no, u, last_pair=False):
                pe.wait_ge(v_ready[u], (turn_no + 1) * STAGED)
                pe.sem_inc(a_held, 1)
                with pe.Fori(0, NCH // 2) as r:
                    for w in range(2):
                        body(turn_no, u, r, w, last_pair)
                body(turn_no, u, NCH // 2, 0, last_pair)

            pe.wait_ge(gather_set, 6)
            pe.wait_ge(cleared, 1)
            pe.wait_ge(stack_in[0], LOADS)
            for g in range(AHEAD):
                scores(0, 0, g, False)
            with pe.Fori(0, TURNS - 1) as turn_no:
                for u in range(SLOTS):
                    head_pair(turn_no, u)
            head_pair(TURNS - 1, 0)
            head_pair(TURNS - 1, 1, last_pair=True)
            pe.wait_ge(parts_ready[1], PAIRS * NCH // 2 + 1)
            turn(1)


def tile_sems(sem, names):
    return [[sem(f"{n}{s}") for s in range(2)] for n in names]


def route(nc, ins, t):
    ctx = ExitStack()
    with ctx:
        ctx.enter_context(nc.cleanup_on_exit())

        def sb(name, shape, dt=F32):
            return ctx.enter_context(nc.sbuf_tensor(name, shape, dt))

        def ps(name, shape, dt=F32):
            return ctx.enter_context(nc.psum_tensor(name, shape, dt))

        def sem(name):
            return nc.alloc_semaphore(name)

        h, attn, identity, wprojT, ids, moved, at_f = (t[k] for k in ("h", "attn", "identity", "wprojT", "ids", "moved", "at_f"))
        TILES = B * NT
        TURNS = TILES // CT // 2
        R = slice(0, TQ)
        SENDS = 16 * CT * TOP
        router = sb("router", [C + 1, EXPERTS])
        r_power = sb("r_power", [P, CT])
        attn_c = sb("attn_c", [P, 2, CT, C])
        aT = sb("aT", [C + 1, 2, CH])
        xT = sb("xT", [C + 1, 2, CH])
        total = sb("r_total", [P, 2, CT])
        neg_mean = sb("r_neg_mean", [P, 2, CT])
        centred = sb("r_centred", [P, 2, CT, C])
        square = sb("r_square", [P, 2, CT, C])
        variance = sb("r_variance", [P, 2, CT])
        var_eps = sb("r_var_eps", [P, 2, CT])
        rstd = sb("r_rstd", [P, 2, CT])
        xn_c = sb("xn_c", [P, 2, CT, C])
        sent = sb("sent", [P, 2, CT, C])
        logits = sb("logits", [P, 2, CT, EXPERTS])
        best_c = sb("best_c", [P, 2, CT, 8])
        best_at_c = sb("best_at_c", [P, 2, CT, 8], U32)
        at_c = sb("at_c", [P, 2, CT, TOP])
        best = sb("best", [P, TILES, TOP])
        chosen = sb("chosen", [P, 2, CT, TOP, EXPERTS], BF16)
        either = sb("either", [P, 2, CT, EXPERTS], BF16)
        start = sb("start", [P, EXPERTS])
        full = sb("full", [P, 2, CT, EXPERTS])
        product = sb("product", [P, 2, CT, TOP, EXPERTS])
        slot_f = sb("slot_f", [P, 2, CT, TOP])
        slot_i = sb("slot_i", [P, 2, CT, TOP], I32)
        first_slot = sb("first_slot", [P, EXPERTS])
        ones_f = sb("ones_f", [P, P])
        before_f = sb("before_f", [P, P])
        ones_b = sb("ones_b", [P, P], BF16)
        before_b = sb("before_b", [P, P], BF16)
        nothing = sb("nothing", [P, C])
        block_ids = sb("block_ids", [P, 2])
        count = sb("count", [P, EXPERTS])
        count_i = sb("count_i", [P, 2, EXPERTS], I32)
        ends_i = sb("ends_i", [1, EXPERTS], I32)
        ends = sb("ends", [P, 2, EXPERTS])
        n_blocks = sb("n_blocks", [P, EXPERTS])
        cap_blocks = sb("cap_blocks", [P, EXPERTS])
        over = sb("over", [P, 2, EXPERTS])
        passed = sb("passed", [P, 2, EXPERTS])
        block_f = sb("block_f", [P, 2, 2])
        over_f = sb("over_f", [P, 2])
        passed_f = sb("passed_f", [P, 2])
        block_i = sb("block_i", [P, 2, 2], I32)
        gap = sb("gap", [P, TILES])
        weight2 = sb("weight2", [P, TILES])
        weight_sum = sb("weight_sum", [P, TILES])

        ps_a = ps("ps_a", [C, 512])
        ps_x = ps("ps_x", [C, 512])
        ps_p = ps("ps_p", [P, 2, 512])
        ps_l = ps("ps_l", [P, 2, 512])
        ps_r = ps("ps_r", [P, 2, 512])
        TOTALS = slice(CT * EXPERTS, (CT + 1) * EXPERTS)

        w_in, consts, held, rows_set = sem("r_w_in"), sem("r_consts"), sem("r_held"), sem("rows_set")
        staged, aT_ps, aT_done, p_ps, h_done, sum_done, mean_done, centre_done, square_done, var_done = tile_sems(sem, (
            "staged", "aT_ps", "aT_done", "p_ps", "r_h_done", "r_sum_done", "r_mean_done", "r_centre_done", "r_square_done",
            "r_var_done"))
        eps_done, rstd_done, norm_done, xT_ps, xT_done, l_ps, logits_done, best_found, best_done = tile_sems(sem, (
            "r_eps_done", "r_rstd_done", "r_norm_done", "xT_ps", "xT_done", "l_ps", "logits_done", "best_found", "best_done"))
        at_done, chosen_done, either_done, kept, ranked, full_done, product_done, slot_found, slot_done, send_ready, slot_kept = tile_sems(
            sem, ("at_done", "chosen_done", "either_done", "kept", "ranked", "full_done", "product_done", "slot_found", "slot_done",
                  "send_ready", "slot_kept"))
        scattered = [sem(f"scattered{s}") for s in range(2)]
        start_done = sem("start_done")
        step, ends_done, gap_done, weight_done, blocks_out, nothing_set, tails_out = (
            sem(n) for n in ("step", "ends_done", "gap_done", "weight_done", "blocks_out", "nothing_set", "tails_out"))

        block = ctx.enter_context(nc.Block())

        def chunk(i, s):
            return bass.ds((i * 2 + s) * CT, CT) if not isinstance(i, int) else slice((i * 2 + s) * CT, (i * 2 + s + 1) * CT)

        def turns(eng, body):
            body(0)
            with eng.Fori(1, TURNS - 1) as i:
                body(i)
            body(TURNS - 1)

        def write_tails(eng, experts):
            eng.wait_ge(ends_done, 1)
            eng.wait_ge(nothing_set, 1)
            eng.sem_inc(held, 1)
            flat = t["slot_x"].rearrange("k p c -> (k p) c")
            for e in experts:
                end = eng.value_load(ends_i[0:1, e:e + 1], min_val=0, max_val=VOID * P - P)
                eng.dma_start(flat[bass.ds(end, P)], nothing[:]).then_inc(tails_out, 16)

        @block.sync
        def _(sp):
            sp.dma_start(wprojT[C:C + 1, :], ins["L0_attn_b_proj"].unsqueeze(0)).then_inc(w_in, 16)
            sp.dma_start(router[C:C + 1, :], ins["L0_ffn_br"].unsqueeze(0)).then_inc(w_in, 16)
            write_tails(sp, range(0, EXPERTS // 2))
            sp.wait_ge(step, BLOCK_STEPS)
            half = BLOCKS // 2
            with nc.allow_non_contiguous_dma(reason="an expert and a place for each block, once"):
                for w in range(2):
                    sp.dma_start(t["blocks"][w].rearrange("(a p) -> p a", p=half), block_i[0:half, :, w]).then_inc(blocks_out, 16)
            sp.wait_ge(blocks_out, 16 * 2)
            sp.wait_ge(tails_out, 16 * EXPERTS)

        @block.gpsimd
        def _(pool):
            for s in range(2):
                pool.sem_inc(eps_done[s], 1)
                pool.sem_inc(rstd_done[s], 1)
                pool.dma_start(router[C // 2 * s:C // 2 * s + C // 2, :], ins["L0_ffn_Wr"][C // 2 * s:C // 2 * s + C // 2, :]).then_inc(scattered[s], 16)
            nc.gpsimd.memset(r_power[:], -0.5).then_inc(consts, 1)
            nc.gpsimd.iota(ids[:], [[1, EXPERTS]], base=0, channel_multiplier=0, allow_small_or_imprecise_dtypes=True).then_inc(consts, 1)
            nc.gpsimd.iota(block_ids[:], [[BLOCKS // 2, 2]], base=0, channel_multiplier=1, allow_small_or_imprecise_dtypes=True).then_inc(consts, 1)
            nc.gpsimd.memset(ones_f[:], 1.0).then_inc(consts, 1)
            pool.wait_ge(consts, 4)
            nc.gpsimd.affine_select(out=before_f[:], in_=ones_f[:], compare_op=ALU.is_gt, fill=0.0, base=0,
                                    pattern=[[1, P]], channel_multiplier=-1).then_inc(consts, 1)
            flat = t["slot_x"].rearrange("k p c -> (k p) c")

            def send(i, s):
                pool.wait_ge(slot_done[s], after(i))
                pool.wait_ge(send_ready[s], after(i))
                pool.sem_inc(held, 1)
                for x in range(CT):
                    for k in range(TOP):
                        nc.gpsimd.indirect_dma_start(
                            out=flat, out_offset=bass.IndirectOffsetOnAxis(ap=slot_i[R, s, x, k:k + 1], axis=0),
                            in_=sent[R, s, x, :], in_offset=None).then_inc(scattered[s], 16)

            def body(i):
                for s in range(2):
                    pool.wait_ge(var_done[s], after(i))
                    pool.sem_inc(held, 1)
                    nc.gpsimd.tensor_scalar(var_eps[R, s], variance[R, s], 1.0 / C, EPS, ALU.mult, ALU.add).then_inc(eps_done[s], 1)
                    pool.wait_ge(eps_done[s], after(i))
                    nc.gpsimd.tensor_tensor(out=rstd[R, s], in0=var_eps[R, s], in1=r_power[R], op=ALU.pow).then_inc(rstd_done[s], 1)
                if not (isinstance(i, int) and i == 0):
                    for s in range(2):
                        send(i - 1, s)
            turns(pool, body)
            for s in range(2):
                send(TURNS - 1, s)
            for s in range(2):
                pool.wait_ge(scattered[s], 16 + SENDS * TURNS)

        @block.scalar
        def _(act):
            for s in range(2):
                for w in (staged, aT_done, square_done, xT_done, logits_done, kept, send_ready, slot_kept):
                    act.sem_inc(w[s], 1)
            nc.scalar.preload_act_table(ACT.Exp)

            def stage(i, s):
                act.wait_ge(aT_ps[s], before(i))
                nc.scalar.copy(attn_c[R, s], attn[R, chunk(i, s), :]).then_inc(staged[s], 1)

            def turned(i, s):
                act.wait_ge(aT_ps[s], after(i))
                act.wait_ge(p_ps[s], before(i))
                nc.scalar.copy(aT[0:C, s], ps_a[:, 0:CH]).then_inc(aT_done[s], 1)

            def to_send(i, s):
                act.wait_ge(norm_done[s], after(i))
                act.wait_ge(scattered[s], 16 + SENDS * i)
                nc.scalar.copy(sent[R, s], xn_c[R, s]).then_inc(send_ready[s], 1)
                act.wait_ge(slot_done[s], after(i))
                nc.scalar.copy(t["slots"][R, chunk(i, s), :], slot_i[R, s]).then_inc(slot_kept[s], 1)

            for s in range(2):
                stage(0, s)
            for s in range(2):
                turned(0, s)

            def body(i):
                first, last = (isinstance(i, int) and i == n for n in (0, TURNS - 1))
                if not last:
                    for s in range(2):
                        stage(i + 1, s)
                for s in range(2):
                    act.wait_ge(centre_done[s], after(i))
                    act.wait_ge(var_done[s], before(i))
                    nc.scalar.activation(square[R, s], centred[R, s], ACT.Square).then_inc(square_done[s], 1)
                if not first:
                    for s in range(2):
                        to_send(i - 1, s)
                for s in range(2):
                    act.wait_ge(xT_ps[s], after(i))
                    act.wait_ge(l_ps[s], before(i))
                    nc.scalar.copy(xT[0:C, s], ps_x[:, 0:CH]).then_inc(xT_done[s], 1)
                for s in range(2):
                    act.wait_ge(l_ps[s], after(i))
                    act.wait_ge(best_done[s], before(i))
                    nc.scalar.copy(logits[R, s].rearrange("p i e -> p (i e)"), ps_l[R, s, 0:CT * EXPERTS]).then_inc(logits_done[s], 1)
                if not last:
                    for s in range(2):
                        turned(i + 1, s)
                for s in range(2):
                    act.wait_ge(best_found[s], after(i))
                    nc.scalar.copy(best[R, chunk(i, s), :], best_c[R, s, :, 0:TOP])
                    act.wait_ge(at_done[s], after(i))
                    nc.scalar.copy(at_f[R, chunk(i, s), :], at_c[R, s]).then_inc(kept[s], 1)
            turns(act, body)
            for s in range(2):
                to_send(TURNS - 1, s)
            act.wait_ge(gap_done, 1)
            nc.scalar.activation(weight2[R], gap[R], ACT.Exp).then_inc(weight_done, 1)
            write_tails(act, range(EXPERTS // 2, EXPERTS))

        @block.vector
        def _(dve):
            for s in range(2):
                for w in (h_done, sum_done, mean_done, centre_done, var_done, norm_done, best_found, best_done, at_done, chosen_done,
                          either_done, full_done, product_done, slot_found, slot_done):
                    dve.sem_inc(w[s], 1)
            nc.vector.memset(nothing[:], 0.0).then_inc(nothing_set, 1)
            nc.vector.memset(aT[C:C + 1], 1.0).then_inc(rows_set, 1)
            nc.vector.memset(xT[C:C + 1], 1.0).then_inc(rows_set, 1)
            dve.wait_ge(consts, 5)
            nc.vector.tensor_copy(ones_b[:], ones_f[:]).then_inc(rows_set, 1)
            nc.vector.tensor_copy(before_b[:], before_f[:]).then_inc(rows_set, 1)
            nc.vector.tensor_scalar(cap_blocks[:], ids[:], float(CAP_BLOCKS), None, ALU.mult).then_inc(rows_set, 1)
            nc.vector.tensor_scalar(first_slot[:], ids[:], float(CAP_BLOCKS * P), None, ALU.mult).then_inc(rows_set, 1)
            nc.vector.tensor_scalar(start[:], ids[:], float(CAP_BLOCKS * P), None, ALU.mult).then_inc(start_done, 1)

            def wide(x):
                return x.unsqueeze(2).to_broadcast([TQ, CT, C])

            def place(i):
                for s in range(2):
                    dve.wait_ge(ranked[s], after(i))
                    dve.wait_ge(start_done, i * 2 + s + 1)
                    nc.vector.tensor_tensor(full[R, s], ps_r[R, s, 0:CT * EXPERTS].rearrange("p (i e) -> p i e", e=EXPERTS),
                                            start[R].unsqueeze(1).to_broadcast([TQ, CT, EXPERTS]), ALU.add).then_inc(full_done[s], 1)
                    dve.wait_ge(full_done[s], after(i))
                    nc.vector.tensor_tensor(start[R], start[R], ps_r[R, s, TOTALS], ALU.add).then_inc(start_done, 1)
                    nc.vector.tensor_tensor(product[R, s], chosen[R, s], full[R, s].unsqueeze(2).to_broadcast([TQ, CT, TOP, EXPERTS]),
                                            ALU.mult).then_inc(product_done[s], 1)
                for s in range(2):
                    dve.wait_ge(product_done[s], after(i))
                    nc.vector.tensor_reduce(slot_f[R, s], product[R, s], AX.X, ALU.add).then_inc(slot_found[s], 1)
                for s in range(2):
                    dve.wait_ge(slot_found[s], after(i))
                    dve.wait_ge(scattered[s], 16 + SENDS * i)
                    dve.wait_ge(slot_kept[s], before(i))
                    nc.vector.tensor_copy(slot_i[R, s], slot_f[R, s]).then_inc(slot_done[s], 1)

            def body(i):
                for s in range(2):
                    tok = h[R, chunk(i, s), :]
                    dve.wait_ge(p_ps[s], after(i))
                    nc.vector.tensor_tensor(tok, tok, ps_p[R, s, 0:CT * C].rearrange("p (i e) -> p i e", e=C), ALU.add).then_inc(h_done[s], 1)
                for s in range(2):
                    dve.wait_ge(h_done[s], after(i))
                    dve.sem_inc(held, 1)
                    nc.vector.tensor_reduce(total[R, s], h[R, chunk(i, s), :], AX.X, ALU.add).then_inc(sum_done[s], 1)
                for s in range(2):
                    dve.wait_ge(sum_done[s], after(i))
                    nc.vector.tensor_scalar(neg_mean[R, s], total[R, s], -1.0 / C, None, ALU.mult).then_inc(mean_done[s], 1)
                for s in range(2):
                    dve.wait_ge(mean_done[s], after(i))
                    nc.vector.tensor_tensor(centred[R, s], h[R, chunk(i, s), :], wide(neg_mean[R, s]), ALU.add).then_inc(centre_done[s], 1)
                for s in range(2):
                    dve.wait_ge(square_done[s], after(i))
                    dve.wait_ge(eps_done[s], before(i))
                    dve.sem_inc(held, 1)
                    nc.vector.tensor_reduce(variance[R, s], square[R, s], AX.X, ALU.add).then_inc(var_done[s], 1)
                if not (isinstance(i, int) and i == 0):
                    place(i - 1)
                for s in range(2):
                    dve.wait_ge(rstd_done[s], after(i))
                    dve.wait_ge(xT_ps[s], before(i))
                    dve.wait_ge(send_ready[s], before(i))
                    nc.vector.tensor_tensor(xn_c[R, s], centred[R, s], wide(rstd[R, s]), ALU.mult).then_inc(norm_done[s], 1)
                for s in range(2):
                    dve.wait_ge(logits_done[s], after(i))
                    dve.wait_ge(kept[s], before(i))
                    dve.sem_inc(held, 1)
                    for x in range(CT):
                        last = nc.vector.max(best_c[R, s, x, :], logits[R, s, x, :])
                    last.then_inc(best_found[s], 1)
                for s in range(2):
                    dve.wait_ge(best_found[s], after(i))
                    dve.sem_inc(held, 1)
                    for x in range(CT):
                        last = nc.vector.max_index(best_at_c[R, s, x, :], best_c[R, s, x, :], logits[R, s, x, :])
                    last.then_inc(best_done[s], 1)
                for s in range(2):
                    dve.wait_ge(best_done[s], after(i))
                    nc.vector.tensor_copy(at_c[R, s], best_at_c[R, s, :, 0:TOP]).then_inc(at_done[s], 1)
                for s in range(2):
                    whole = [TQ, CT * TOP, EXPERTS]
                    dve.wait_ge(at_done[s], after(i))
                    nc.vector.tensor_tensor(chosen[R, s].rearrange("p i k e -> p (i k) e"), ids[R].unsqueeze(1).to_broadcast(whole),
                                            at_c[R, s].rearrange("p i k -> p (i k)").unsqueeze(2).to_broadcast(whole), ALU.is_equal
                                            ).then_inc(chosen_done[s], 1)
                for s in range(2):
                    dve.wait_ge(chosen_done[s], after(i))
                    nc.vector.tensor_tensor(either[R, s], chosen[R, s, :, 0, :], chosen[R, s, :, 1, :], ALU.add).then_inc(either_done[s], 1)
            turns(dve, body)
            place(TURNS - 1)

            done = [0]

            def then(instruction):
                done[0] += 1
                instruction.then_inc(step, 1)
                dve.wait_ge(step, done[0])

            dve.wait_ge(start_done, 2 * TURNS + 1)
            dve.wait_ge(rows_set, 6)
            nc.vector.tensor_copy(ends_i[:], start[0:1]).then_inc(ends_done, 1)
            then(nc.vector.tensor_tensor(count[R], start[R], first_slot[R], ALU.subtract))
            then(nc.vector.tensor_scalar(count[R], count[R], float(P - 1), None, ALU.add))
            then(nc.vector.tensor_copy(count_i[R, 0], count[R]))
            then(nc.vector.tensor_scalar(count_i[R, 1], count_i[R, 0], 7, None, ALU.arith_shift_right))
            then(nc.vector.tensor_copy(n_blocks[R], count_i[R, 1]))
            then(nc.vector.tensor_copy(ends[R, 0], n_blocks[R]))
            src, width = 0, 1
            while width < EXPERTS:
                then(nc.vector.tensor_copy(ends[R, 1 - src, 0:width], ends[R, src, 0:width]))
                then(nc.vector.tensor_tensor(ends[R, 1 - src, width:], ends[R, src, width:], ends[R, src, 0:EXPERTS - width], ALU.add))
                src, width = 1 - src, 2 * width
            H2 = slice(0, BLOCKS // 2)
            for a in range(2):
                then(nc.vector.tensor_scalar(over[H2, a], ends[H2, src], block_ids[H2, a:a + 1], None, ALU.is_le))
            then(nc.vector.tensor_tensor(passed[H2], over[H2], n_blocks[H2].unsqueeze(1).to_broadcast([BLOCKS // 2, 2, EXPERTS]), ALU.mult))
            then(nc.vector.tensor_reduce(over_f[H2], over[H2], AX.X, ALU.add))
            then(nc.vector.tensor_reduce(passed_f[H2], passed[H2], AX.X, ALU.add))
            then(nc.vector.tensor_scalar(block_f[H2, :, 0], over_f[H2], float(EXPERTS - 1), None, ALU.min))
            then(nc.vector.scalar_tensor_tensor(out=block_f[H2, :, 1], in0=over_f[H2], scalar=float(CAP_BLOCKS), in1=block_ids[H2],
                                                op0=ALU.mult, op1=ALU.add))
            then(nc.vector.tensor_tensor(block_f[H2, :, 1], block_f[H2, :, 1], passed_f[H2], ALU.subtract))
            then(nc.vector.tensor_copy(block_i[H2], block_f[H2]))
            assert done[0] == BLOCK_STEPS, done[0]
            then(nc.vector.tensor_tensor(moved[R], ends[R, src], n_blocks[R], ALU.subtract))
            then(nc.vector.tensor_tensor(moved[R], moved[R], cap_blocks[R], ALU.subtract))
            gates = t["gates"]
            for s in range(2):
                dve.wait_ge(kept[s], after(TURNS - 1))
            nc.vector.tensor_tensor(gap[R], best[R, :, 1], best[R, :, 0], ALU.subtract).then_inc(gap_done, 1)
            dve.wait_ge(weight_done, 1)
            then(nc.vector.tensor_scalar(weight_sum[R], weight2[R], 1.0, None, ALU.add))
            then(nc.vector.reciprocal(gates[R, :, 0], weight_sum[R]))
            then(nc.vector.tensor_tensor(gates[R, :, 1], weight2[R], gates[R, :, 0], ALU.mult))

        @block.tensor
        def _(pe):
            for s in range(2):
                for w in (aT_ps, p_ps, xT_ps, l_ps, ranked):
                    pe.sem_inc(w[s], 1)
            pe.wait_ge(w_in, 32)
            pe.wait_ge(rows_set, 4)
            for s in range(2):
                pe.wait_ge(scattered[s], 16)

            def project(i):
                for s in range(2):
                    pe.wait_ge(staged[s], after(i))
                    pe.wait_ge(aT_done[1 - s], after(i) if s else before(i))
                    pe.sem_inc(held, 1)
                    for x in range(CT):
                        last = nc.tensor.transpose(ps_a[:, TQ * x:TQ * x + TQ], attn_c[R, s, x, :], identity[R, R])
                    last.then_inc(aT_ps[s], 1)
                for s in range(2):
                    pe.wait_ge(aT_done[s], after(i))
                    pe.wait_ge(h_done[s], before(i))
                    pe.sem_inc(held, 1)
                    for x in range(CT):
                        last = nc.tensor.matmul(ps_p[R, s, C * x:C * x + C], aT[:, s, TQ * x:TQ * x + TQ], wprojT[:],
                                                start=True, stop=True)
                    last.then_inc(p_ps[s], 1)

            project(0)

            def body(i):
                for s in range(2):
                    pe.wait_ge(norm_done[s], after(i))
                    pe.wait_ge(xT_done[1 - s], after(i) if s else before(i))
                    pe.sem_inc(held, 1)
                    for x in range(CT):
                        last = nc.tensor.transpose(ps_x[:, TQ * x:TQ * x + TQ], xn_c[R, s, x, :], identity[R, R])
                    last.then_inc(xT_ps[s], 1)
                for s in range(2):
                    pe.wait_ge(xT_done[s], after(i))
                    pe.wait_ge(logits_done[s], before(i))
                    pe.sem_inc(held, 1)
                    for x in range(CT):
                        last = nc.tensor.matmul(ps_l[R, s, EXPERTS * x:EXPERTS * x + EXPERTS], xT[:, s, TQ * x:TQ * x + TQ], router[:],
                                                start=True, stop=True)
                    last.then_inc(l_ps[s], 1)
                if not (isinstance(i, int) and i == TURNS - 1):
                    project(i + 1)
                for s in range(2):
                    pe.wait_ge(either_done[s], after(i))
                    if not (isinstance(i, int) and i == 0):
                        pe.wait_ge(start_done, i * 2 + s)
                    pe.wait_ge(full_done[s], before(i))
                    pe.sem_inc(held, 1)
                    for x in range(CT):
                        at = ps_r[R, s, EXPERTS * x:EXPERTS * x + EXPERTS]
                        nc.tensor.matmul(at, before_b[R, R], either[R, s, x, :], start=True, stop=x == 0)
                        for y in range(x):
                            nc.tensor.matmul(at, ones_b[R, R], either[R, s, y, :], start=False, stop=y == x - 1)
                    for x in range(CT):
                        last = nc.tensor.matmul(ps_r[R, s, TOTALS], ones_b[R, R], either[R, s, x, :], start=x == 0, stop=x == CT - 1)
                    last.then_inc(ranked[s], 1)
            turns(pe, body)


def run_experts(nc, ins, t):
    ctx = ExitStack()
    with ctx:
        ctx.enter_context(nc.cleanup_on_exit())
        def sb(name, shape, dt=F32):
            return ctx.enter_context(nc.sbuf_tensor(name, shape, dt))

        def ps(name, shape, dt=F32):
            return ctx.enter_context(nc.psum_tensor(name, shape, dt))

        def sem(name):
            return nc.alloc_semaphore(name)

        G = 4
        SLOTS = 4
        TURNS = BLOCKS // G // SLOTS
        block_row = sb("block_row", [1, 2, BLOCKS], I32)
        xs = sb("xs", [P, SLOTS, G, C])
        pack = sb("pack", [P, SLOTS, G, PACK])
        xsT = sb("xsT", [C + 1, 2, G * P])
        hidT = sb("hidT", [P, 2, G * P])
        ys = sb("ys", [P, 2, G, C])
        ones3 = sb("ones3", [P, P], BF16)
        identity = t["identity"]
        ps_x = ps("e_ps_x", [C, 2, 512])
        ps_h = ps("e_ps_h", [P, 2, 512])
        ps_y = ps("e_ps_y", [P, 2, 512])

        row_in, ones_done, held = (sem(n) for n in ("row_in", "ones_done", "e_held"))
        x_in = [sem(f"e_x_in{s}") for s in range(SLOTS)]
        pack_in = [sem(f"pack_in{s}") for s in range(SLOTS)]
        y_out = [sem(f"y_out{s}") for s in range(2)]
        xT_ps, xT_done, h_ps, h_done, y_ps, y_done = (sem(n) for n in ("e_xT_ps", "e_xT_done", "h_ps", "e_h_done", "y_ps", "y_done"))
        FIRST = SLOTS + 1
        PIECE = B * NT * TOP // (TURNS * SLOTS)
        assert PIECE * TURNS * SLOTS == B * NT * TOP
        is_its = sb("is_its", [P, PIECE, EXPERTS])
        its_move = sb("its_move", [P, PIECE, EXPERTS])
        moves = sb("moves", [P, B * NT * TOP])
        place_i = sb("place_i", [P, 2, B * NT * TOP], I32)
        place_f = sb("place_f", [P, 2, B * NT * TOP])
        matched, taken, moved = sem("matched"), sem("taken"), sem("moved_done")
        row_steps = sem("row_steps")

        block = ctx.enter_context(nc.Block())

        def made(i, g):
            return i * SLOTS + g + 1 + FIRST

        @block.gpsimd
        def _(pool):
            pool.wait_ge(row_in, 16)
            pool.sem_inc(held, 1)
            with pool.Fori(0, TURNS) as i:
                for s in range(SLOTS):
                    pool.wait_ge(y_ps, made(i, s - SLOTS))
                    pool.sem_inc(held, 1)
                    for x in range(G):
                        expert = pool.value_load(block_row[0:1, 0, bass.ds((i * SLOTS + s) * G + x, 1)], min_val=0, max_val=EXPERTS - 1)
                        pool.dma_start(pack[:, s, x], t["weights"][bass.ds(expert, 1)].rearrange("a p n -> p (a n)")).then_inc(pack_in[s], 16)

        @block.sync
        def _(sp):
            for s in range(2):
                sp.sem_inc(y_out[s], 16)
            sp.dma_start(block_row[:], t["blocks"].rearrange("(a w) k -> a w k", a=1)).then_inc(row_in, 16)
            sp.wait_ge(row_in, 16)
            sp.sem_inc(held, 1)
            with sp.Fori(0, TURNS) as i:
                for s in range(SLOTS):
                    sp.wait_ge(xT_ps, made(i, s - SLOTS))
                    sp.sem_inc(held, 1)
                    for x in range(G):
                        place = sp.value_load(block_row[0:1, 1, bass.ds((i * SLOTS + s) * G + x, 1)], min_val=0, max_val=VOID + BLOCKS - 1)
                        sp.dma_start(xs[:, s, x], t["slot_x"][bass.ds(place, 1)].rearrange("a p c -> p (a c)")).then_inc(x_in[s], 16)
            for s in range(2):
                sp.wait_ge(y_out[s], 16 * (2 * TURNS + 1))

        @block.scalar
        def _(act):
            act.sem_inc(xT_done, FIRST)
            act.sem_inc(y_done, FIRST)

            def rows(i, g):
                act.wait_ge(xT_ps, made(i, g))
                act.wait_ge(h_ps, made(i, g - 2))
                nc.scalar.copy(xsT[0:C, g % 2], ps_x[:, g % 2]).then_inc(xT_done, 1)

            def outputs(i, y):
                act.wait_ge(y_ps, made(i, y))
                act.wait_ge(y_out[y % 2], 16 * (i * 2 + y // 2 + 1))
                nc.scalar.copy(ys[:, y % 2].rearrange("p g c -> p (g c)"), ps_y[:, y % 2, 0:G * C]).then_inc(y_done, 1)
                act.wait_ge(y_done, made(i, y))
                act.dma_start(t["slot_y"][:, bass.ds((i * SLOTS + y) * G, G), :], ys[:, y % 2]).then_inc(y_out[y % 2], 16)

            def groups(i, last):
                for g in range(SLOTS):
                    if g + 1 < SLOTS:
                        rows(i, g + 1)
                    elif not last:
                        rows(i + 1, 0)
                    if g > 0:
                        outputs(i, g - 1)
                outputs(i, SLOTS - 1)

            rows(0, 0)
            with act.Fori(0, TURNS - 1) as i:
                groups(i, False)
            groups(TURNS - 1, True)

        @block.vector
        def _(dve):
            dve.sem_inc(h_done, FIRST)
            R = slice(0, TQ)
            at_flat = t["at_f"][R].rearrange("p i k -> p (i k)")
            nc.vector.memset(ones3[:], 1.0).then_inc(ones_done, 1)
            nc.vector.memset(xsT[B1_ROW:B1_ROW + 1], 1.0).then_inc(ones_done, 1)
            with dve.Fori(0, TURNS) as i:
                for g in range(SLOTS):
                    dve.wait_ge(h_ps, made(i, g))
                    dve.wait_ge(y_ps, made(i, g - 2))
                    nc.vector.tensor_scalar(hidT[:, g % 2], ps_h[:, g % 2], 0.0, None, ALU.max).then_inc(h_done, 1)
                    n = dve.snap(i * SLOTS + g)
                    whole = [TQ, PIECE, EXPERTS]
                    nc.vector.tensor_tensor(is_its[R], t["ids"][R].unsqueeze(1).to_broadcast(whole),
                                            at_flat[:, bass.ds(n * PIECE, PIECE)].unsqueeze(2).to_broadcast(whole), ALU.is_equal).then_inc(matched, 1)
                    dve.wait_ge(matched, n + 1)
                    nc.vector.tensor_tensor(its_move[R], is_its[R], t["moved"][R].unsqueeze(1).to_broadcast(whole), ALU.mult).then_inc(taken, 1)
                    dve.wait_ge(taken, n + 1)
                    dve.sem_inc(held, 1)
                    nc.vector.tensor_reduce(moves[R, bass.ds(n * PIECE, PIECE)], its_move[R], AX.X, ALU.add).then_inc(moved, 1)
            dve.wait_ge(moved, TURNS * SLOTS)
            slots = t["slots"][R].rearrange("p i k -> p (i k)")
            nc.vector.tensor_scalar(place_i[R, 0], slots, P - 1, None, ALU.bitwise_and).then_inc(row_steps, 1)
            nc.vector.tensor_scalar(place_i[R, 1], slots, 7, None, ALU.arith_shift_right).then_inc(row_steps, 1)
            dve.wait_ge(row_steps, 2)
            for k in range(2):
                nc.vector.tensor_copy(place_f[R, k], place_i[R, k]).then_inc(row_steps, 1)
            dve.wait_ge(row_steps, 4)
            nc.vector.tensor_tensor(place_f[R, 1], place_f[R, 1], moves[R], ALU.add).then_inc(row_steps, 1)
            dve.wait_ge(row_steps, 5)
            nc.vector.scalar_tensor_tensor(out=place_f[R, 0], in0=place_f[R, 0], scalar=float(BLOCKS), in1=place_f[R, 1],
                                           op0=ALU.mult, op1=ALU.add).then_inc(row_steps, 1)
            dve.wait_ge(row_steps, 6)
            nc.vector.tensor_copy(t["rows"][R].rearrange("p i k -> p (i k)"), place_f[R, 0]).then_inc(row_steps, 1)

        @block.tensor
        def _(pe):
            for w in (xT_ps, h_ps, y_ps):
                pe.sem_inc(w, FIRST)

            def turn(i, g):
                pe.wait_ge(x_in[g], 16 * G * i + 16 * G)
                pe.wait_ge(xT_done, made(i, g - 2))
                pe.sem_inc(held, 1)
                for x in range(G):
                    last = nc.tensor.transpose(ps_x[:, g % 2, P * x:P * x + P], xs[:, g, x, :], identity[:])
                last.then_inc(xT_ps, 1)

            def hidden(i, g):
                pe.wait_ge(pack_in[g], 16 * G * i + 16 * G)
                pe.wait_ge(xT_done, made(i, g))
                pe.wait_ge(h_done, made(i, g - 2))
                pe.sem_inc(held, 1)
                for x in range(G):
                    last = nc.tensor.matmul(ps_h[:, g % 2, P * x:P * x + P], pack[0:C + 1, g, x, 0:HID], xsT[:, g % 2, P * x:P * x + P],
                                            start=True, stop=True)
                last.then_inc(h_ps, 1)

            def outputs(i, g):
                pe.wait_ge(h_done, made(i, g))
                pe.wait_ge(y_done, made(i, g - 2))
                pe.sem_inc(held, 1)
                for x in range(G):
                    y = ps_y[:, g % 2, C * x:C * x + C]
                    nc.tensor.matmul(y, hidT[:, g % 2, P * x:P * x + P], pack[:, g, x, HID:PACK], start=True, stop=False)
                    b2 = pack[B2_ROW:B2_ROW + PARTS, g, x, 0:C // 2].bitcast(BF16)
                    last = nc.tensor.matmul(y, ones3[B2_ROW:B2_ROW + PARTS, :], b2, start=False, stop=True)
                last.then_inc(y_ps, 1)

            def groups(i, last):
                for g in range(SLOTS):
                    if g + 1 < SLOTS:
                        turn(i, g + 1)
                    elif not last:
                        turn(i + 1, 0)
                    hidden(i, g)
                    if g > 0:
                        outputs(i, g - 1)
                outputs(i, SLOTS - 1)

            pe.wait_ge(ones_done, 2)
            turn(0, 0)
            with pe.Fori(0, TURNS - 1) as i:
                groups(i, False)
            groups(TURNS - 1, True)


def combine(nc, t, out):
    ctx = ExitStack()
    with ctx:
        ctx.enter_context(nc.cleanup_on_exit())
        def sb(name, shape, dt=F32):
            return ctx.enter_context(nc.sbuf_tensor(name, shape, dt))

        def sem(name):
            return nc.alloc_semaphore(name)

        TILES = B * NT
        CHUNKS = TILES // CT
        got = sb("got", [P, TILES, TOP, C])
        part = sb("part", [P, CHUNKS, TOP, CT, C])
        h, gates = t["h"], t["gates"]
        got_in = [sem(f"got_in{n}") for n in range(CHUNKS)]
        scaled, summed, h_ready, stored = (sem(n) for n in ("c_scaled", "c_summed", "h_ready", "stored"))
        CLS_ROW = PATCHES - (NT - 1) * TQ

        block = ctx.enter_context(nc.Block())

        @block.gpsimd
        def _(pool):
            rows_y = t["slot_y"].rearrange("p k c -> (p k) c")
            for i in range(TILES):
                for k in range(TOP):
                    nc.gpsimd.indirect_dma_start(
                        out=got[0:TQ, i, k, :], out_offset=None, in_=rows_y,
                        in_offset=bass.IndirectOffsetOnAxis(ap=t["rows"][0:TQ, i, k:k + 1], axis=0)).then_inc(got_in[i // CT], 16)

        @block.vector
        def _(dve):
            for n in range(CHUNKS):
                dve.wait_ge(got_in[n], 16 * TOP * CT)
                for k in range(TOP):
                    nc.vector.tensor_tensor(part[0:TQ, n, k], got[0:TQ, n * CT:n * CT + CT, k, :],
                                            gates[0:TQ, n * CT:n * CT + CT, k:k + 1].to_broadcast([TQ, CT, C]), ALU.mult).then_inc(scaled, 1)
                dve.wait_ge(scaled, 2 * n + 2)
                nc.vector.tensor_tensor(part[0:TQ, n, 0], part[0:TQ, n, 0], part[0:TQ, n, 1], ALU.add).then_inc(summed, 1)
                dve.wait_ge(summed, n + 1)
                tok = h[0:TQ, n * CT:n * CT + CT, :]
                nc.vector.tensor_tensor(tok, tok, part[0:TQ, n, 0], ALU.add).then_inc(h_ready, 1)

        @block.sync
        def _(sp):
            stores = 0
            for n in range(CHUNKS):
                b, c = divmod(n, NCH)
                sp.wait_ge(h_ready, n + 1)
                full = CT if c < NCH - 1 else CT - 1
                at = 1 + c * CH
                sp.dma_start(out[b, at:at + full * TQ, :].rearrange("(i p) e -> p i e", p=TQ),
                             h[0:TQ, n * CT:n * CT + full, :]).then_inc(stored, 16)
                stores += 1
                if full < CT:
                    sp.dma_start(out[b, at + full * TQ:N, :], h[0:CLS_ROW, n * CT + full, :]).then_inc(stored, 16)
                    sp.dma_start(out[b, 0:1, :], h[CLS_ROW:CLS_ROW + 1, n * CT + full, :]).then_inc(stored, 16)
                    stores += 2
            sp.wait_ge(stored, 16 * stores)


_INS = ["x", "cls_tok", "L0_tok_bases", "L0_tok_W_spline", "L0_tok_b_spline", "L0_tok_W_base", "L0_tok_b_base",
        "L0_attn_w_qkv", "L0_attn_w_proj", "L0_attn_b_proj", "L0_attn_rel_table", "L0_attn_rel_index",
        "L0_ffn_Wr", "L0_ffn_br", "L0_ffn_W1", "L0_ffn_b1", "L0_ffn_W2", "L0_ffn_b2"]


def kernel(**inputs):
    import numpy as np
    import concourse.bacc as bacc
    from concourse.bass_utils import run_bass_kernel_spmd

    nc = bacc.Bacc("TRN2", target_bir_lowering=False, num_devices=1)
    arrays, aps = {}, {}
    for name in _INS:
        a = np.ascontiguousarray(inputs[name])
        arrays[f"in_{name}"] = a
        aps[name] = nc.dram_tensor(f"in_{name}", a.shape, mybir.dt.from_np(a.dtype), kind="ExternalInput").ap()
    out = nc.dram_tensor("out_tokens", (B, N, C), F32, kind="ExternalOutput").ap()
    vit_layer(nc, aps, out)
    r = run_bass_kernel_spmd(nc, [arrays], core_ids=[0])
    return r.results[0]["out_tokens"]
```

```python
import struct
from contextlib import ExitStack

import concourse.bass as bass
from concourse import mybir

ALU = mybir.AluOpType
ACT = mybir.ActivationFunctionType
AX = mybir.AxisListType
F32 = mybir.dt.float32
BF16 = mybir.dt.bfloat16
I32 = mybir.dt.int32
U32 = mybir.dt.uint32
RMAX = bass.bass_isa.ReduceOp.max

P = 128
C = 64
H = 8
HD = C // H
NB = 3
B = 2
PATCHES = 64 * 64
N = PATCHES + 1
TQ = 114
CT = 4
CH = TQ * CT
NCH = 9
NT = NCH * CT
NP = NCH * CH
LASTX = PATCHES - (NCH - 1) * CH
QT = 33
KB = PATCHES // P
KG = 3
NG = -(-KB // KG)
V_PARTS = 4
KEY0 = 8
CLS_COL = KEY0 + PATCHES
KW = KEY0 + CLS_COL
WS2 = 49
WIN0 = PATCHES - WS2
TABLE = 169
WIN_COLS = -(-WS2 * WS2 // P)
PARTS = 3
SROWS = PARTS * PARTS * HD
STACK = SROWS + PARTS
EPS = 1e-5
TWO_ONES = struct.unpack('<f', struct.pack('<I', 0x3F803F80))[0]
SLOTS = 2
COLUMN_GROUP = 32
HEAD_AT = 16
VW = HEAD_AT + HD + 1
EXPERTS = 64
TOP = 2
HID = 128
B1_ROW = C
B2_ROW = 96
PACK = HID + C
BLOCKS = (B * NT * TQ * TOP + EXPERTS * (P - 1)) // P + 1
BLOCKS += -BLOCKS % 8
SPARE = 16
CAP_BLOCKS = -(-(B * NT * TQ + P) // P)
VOID = EXPERTS * CAP_BLOCKS
BLOCK_STEPS = 27
SAFE = 30.0


def after(c):
    return c + 2


def before(c):
    return c + 1


def vit_layer(nc, ins, out):
    ctx = ExitStack()
    with ctx:
        def keep(name, shape, dt=F32):
            return ctx.enter_context(nc.sbuf_tensor(name, shape, dt))

        def dram(name, shape, dt=F32):
            return nc.dram_tensor(name, shape, dt).ap()

        t = {}
        t["h"] = keep("h", [P, B * NT, C])
        t["identity"] = keep("identity", [P, P])
        t["wprojT"] = keep("wprojT", [C + 1, C])
        t["window"] = keep("window", [WS2, H, WS2])
        t["qk_parts"] = dram("qk_parts", (B, PARTS, P, NP), BF16)
        t["v_rows"] = dram("v_rows", (B, NP, C))
        t["q_squares"] = dram("q_squares", (B * H, NP))
        t["head_tops"] = dram("head_tops", (2, B * H))
        t["window_rows"] = dram("window_rows", (P * WIN_COLS, H))
        t["shift_parts"] = dram("shift_parts", (B * H, PARTS, NP), BF16)
        t["row_max"] = dram("row_max", (B * H, QT * P))
        t["slot_x"] = dram("slot_x", (VOID + BLOCKS, P, C))
        t["slot_y"] = dram("slot_y", (P, BLOCKS, C))
        t["weights"] = dram("weights", (EXPERTS, P, PACK))
        t["attn"] = keep("attn", [P, B * NT, C])
        t["voided"] = nc.alloc_semaphore("voided")
        t["packed"] = nc.alloc_semaphore("packed_w")
        with ExitStack() as stacks:
            def pairs(name, shape, dt=F32):
                return [[stacks.enter_context(nc.sbuf_tensor(f"{name}{u}{p}", shape, dt)) for p in range(2)] for u in range(SLOTS)]

            t["q_stack"] = pairs("q_stack", [STACK, NP], BF16)
            t["k_stack"] = pairs("k_stack", [STACK, KW], BF16)
            t["v_head"] = pairs("v_head", [P, KB, VW])
            t["v_cls"] = [stacks.enter_context(nc.sbuf_tensor(f"v_cls{u}", [P, VW], F32)) for u in range(SLOTS)]
            t["win_head"] = pairs("win_head", [WS2, P])
            t["cls_all"] = stacks.enter_context(nc.sbuf_tensor("cls_all", [2, B, H // 2, VW], F32))
            t["gather"] = stacks.enter_context(nc.sbuf_tensor("gather", [P, COLUMN_GROUP], BF16))
            t["stack_in"] = [nc.alloc_semaphore(f"stack_in{u}") for u in range(SLOTS)]
            t["v_in"] = [nc.alloc_semaphore(f"v_in{b}") for b in range(B)]
            embed_and_project(nc, ins, t)
            t["v_all"] = stacks.enter_context(nc.sbuf_tensor("v_all", [P, B, KB, C], F32))
            settle_shifts(nc, ins, t)
            attend(nc, ins, t)
        t["at_f"] = keep("at_f", [P, B * NT, TOP])
        t["slots"] = keep("slots", [P, B * NT, TOP], I32)
        t["rows"] = keep("rows", [P, B * NT, TOP], I32)
        t["gates"] = keep("gates", [P, B * NT, TOP])
        t["ids"] = keep("ids", [P, EXPERTS])
        t["moved"] = keep("moved", [P, EXPERTS])
        t["blocks"] = dram("blocks", (2, BLOCKS), I32)
        route(nc, ins, t)
        run_experts(nc, ins, t)
        combine(nc, t, out)


def prepare_stack(nc, dve, t, n, zeros_set, count):
    u, p = divmod(n, 2)
    k_stack, v_head = t["k_stack"][u][p], t["v_head"][u][p]
    nc.vector.memset(k_stack[:, 0:KEY0], 0.0)
    nc.vector.memset(k_stack[:, CLS_COL:KW], 0.0)
    nc.vector.memset(v_head[:], 0.0).then_inc(zeros_set, 1)
    nc.vector.memset(k_stack[C:STACK, KEY0:CLS_COL].bitcast(F32), TWO_ONES)
    if p == 0:
        nc.vector.memset(t["v_cls"][u][:], 0.0)
    nc.vector.memset(t["win_head"][u][p][:], 0.0)
    dve.wait_ge(zeros_set, count)
    nc.vector.memset(k_stack[C:STACK, CLS_COL:CLS_COL + 1], 1.0)
    ones = slice(p * HEAD_AT + HD, p * HEAD_AT + HD + 1)
    nc.vector.memset(v_head[:, :, ones], 1.0)


def embed_and_project(nc, ins, t):
    ctx = ExitStack()
    with ctx:
        ctx.enter_context(nc.cleanup_on_exit())

        def sb(name, shape, dt=F32):
            return ctx.enter_context(nc.sbuf_tensor(name, shape, dt))

        def ps(name, shape, dt=F32):
            return ctx.enter_context(nc.psum_tensor(name, shape, dt))

        def sem(name):
            return nc.alloc_semaphore(name)

        def pair(name):
            return [sem(f"{name}{b}") for b in range(B)]

        h, identity, wprojT, window = (t[k] for k in ("h", "identity", "wprojT", "window"))

        spl_raw = sb("spl_raw", [C, C, NB])
        base_raw = sb("base_raw", [C, C])
        mix_raw = sb("mix_raw", [C, 2, 2, C])
        qkv_raw = sb("qkv_raw", [C, 3, C])
        proj_raw = sb("proj_raw", [C, C])
        mixT = sb("mixT", [P, 2, C])
        qkvT = sb("qkvT", [C, 3 * C])
        bases = sb("bases", [P, NB])
        slope = sb("slope", [P, 2])
        bias_spline = sb("bias_spline", [P, C])
        bias_base = sb("bias_base", [P, C])
        bias_e = sb("bias_e", [P, C])
        table = sb("table", [H, TABLE])
        table_max = sb("table_max", [H, 1])
        heads_f = sb("heads_f", [P, 2, H])
        heads_of = sb("heads_of", [P, 2, H], BF16)
        qscale = sb("qscale", [P, 1])
        power = sb("power", [P, CT])
        x2 = sb("x2", [P, B, PATCHES])
        feat = sb("feat", [P, B, 2, CH])
        total = sb("total", [P, B, CT])
        neg_mean = sb("neg_mean", [P, B, CT])
        centred = sb("centred", [P, B, CT, C])
        square = sb("square", [P, B, CT, C])
        variance = sb("variance", [P, B, CT])
        var_eps = sb("var_eps", [P, B, CT])
        rstd = sb("rstd", [P, B, CT])
        xn = sb("xn", [P, B, CT, C])
        xnT = sb("xnT", [C, B, CH])
        qk = sb("qk", [P, B, CH])
        rest1 = sb("rest1", [P, B, CH])
        qksq = sb("qksq", [P, B, CH], BF16)
        qkp = sb("qkp", [P, B, PARTS, CH], BF16)
        vout = sb("vout", [P, B, CT, C])
        kn = sb("kn", [H, B, NCH])
        kmax = sb("kmax", [H, B])
        qn = sb("qn", [H, B, CH])
        win_index = sb("win_index", [P, WIN_COLS], I32)
        win_bias = sb("win_bias", [P, WIN_COLS, H])
        win_raw = sb("win_raw", [WS2, WS2, H])
        VOIDS = BLOCKS // (NCH - 1)
        assert VOIDS * (NCH - 1) == BLOCKS and EXPERTS % (NCH - 1) == 0
        void = sb("void", [P, VOIDS * C])
        gather_f = sb("gather_f", [P, COLUMN_GROUP])
        cls_set, gather_set, table_in, heads_set = (sem(n) for n in ("cls_set", "gather_set", "table_in", "heads_set"))
        b2_in = sb("b2_in", [EXPERTS, C])
        b2_rest = sb("b2_rest", [EXPERTS, C])
        b2_parts = sb("b2_parts", [EXPERTS, PARTS, C], BF16)

        ps_h = ps("ps_h", [P, B, 512])
        ps_qk = ps("ps_qk", [P, B, 512])
        ps_n = ps("ps_n", [P, B, 512])
        K_ROW = 32
        ps_t = ps("ps_t", [P, 512])
        ps_v = ps("ps_v", [P, 512])

        w_in, ident, turned, turned_out, consts = (sem(n) for n in ("w_in", "ident", "turned", "turned_out", "consts"))
        packed = sem("packed")
        x_in = pair("x_in")
        feat_done, silu_done, mixed, h_done = pair("feat_done"), pair("silu_done"), pair("mixed"), pair("h_done")
        sum_done, mean_done, centre_done, square_done = (pair(n) for n in ("sum_done", "mean_done", "centre_done", "square_done"))
        var_done, eps_done, rstd_done, norm_done = (pair(n) for n in ("var_done", "eps_done", "rstd_done", "norm_done"))
        xnT_ps, xnT_done, qk_ps, v_ps, n_ps = (pair(n) for n in ("xnT_ps", "xnT_done", "qk_ps", "v_ps", "n_ps"))
        qk_done, qksq_done, v_done, qn_done, kn_done = (pair(n) for n in ("qk_done", "qksq_done", "v_done", "qn_done", "kn_done"))
        hi_done, rest1_done, mid_done, rest2_done, parts_done = (pair(n) for n in ("hi_done", "rest1_done", "mid_done", "rest2_done", "parts_done"))
        parts_out, v_out = pair("parts_out"), pair("v_out")
        padded, cls_in, held, packed_raw = (
            sem(n) for n in ("padded", "cls_in", "held", "packed_raw"))
        kmax_done, table_done, tops_out = (sem(n) for n in ("kmax_done", "table_done", "tops_out"))
        qn_out = pair("qn_out")
        zeros_set, void_set, b2_loaded, b2_split = (sem(n) for n in ("zeros_set", "void_set", "b2_loaded", "b2_split"))
        index_clear, index_in, gathered, rows_out, window_in = (
            sem(n) for n in ("index_clear", "index_in", "gathered", "rows_out", "window_in"))

        xflat = ins["x"].rearrange("b c a w -> b c (a w)")
        cls_row = ins["cls_tok"].rearrange("a b c -> (a b) c")
        LOADS = 8
        TURNED = 6
        CLS_ROW = PATCHES - (NT - 1) * TQ

        block = ctx.enter_context(nc.Block())

        def patches(c):
            return LASTX if isinstance(c, int) and c == NCH - 1 else CH

        def pipelined(eng, start, turn, tail):
            start()
            turn(0)
            with eng.Fori(1, NCH - 3) as c:
                turn(c)
            turn(NCH - 3)
            turn(NCH - 2)
            tail()

        def is_first(c):
            return isinstance(c, int) and c == 0

        def has_features(c):
            return not isinstance(c, int) or c + 2 < NCH

        @block.sync
        def _(sp):
            def load(dst, src):
                sp.dma_start(dst, src).then_inc(w_in, 16)

            for b in range(B):
                for s in (parts_out, v_out, qn_out):
                    sp.sem_inc(s[b], 16)
            load(spl_raw[:], ins["L0_tok_W_spline"].rearrange("e (c k) -> e c k", k=NB))
            load(base_raw[:], ins["L0_tok_W_base"])
            for half in range(2):
                load(bases[C * half:C * half + C, :], ins["L0_tok_bases"])
            def load_x(b, columns):
                for half in range(2):
                    sp.dma_start(x2[C * half:C * half + C, b, columns], xflat[b][:, columns]).then_inc(x_in[b], 16)

            for b in range(B):
                load_x(b, slice(0, 2 * CH))
            load(qkv_raw[:], ins["L0_attn_w_qkv"].rearrange("(s e) c -> e s c", s=3))
            load(proj_raw[:], ins["L0_attn_w_proj"])
            load(bias_spline[:], ins["L0_tok_b_spline"].partition_broadcast(P))
            load(bias_base[:], ins["L0_tok_b_base"].partition_broadcast(P))
            for b in range(B):
                load_x(b, slice(2 * CH, PATCHES))
            with nc.allow_non_contiguous_dma(reason="a table of 169 x 8, once"):
                sp.dma_start(table[:], ins["L0_attn_rel_table"].rearrange("r h -> h r")).then_inc(table_in, 16)
            sp.dma_start(b2_in[:], ins["L0_ffn_b2"]).then_inc(b2_loaded, 16)
            sp.wait_ge(padded, 1)
            for b in range(B):
                sp.dma_start(h[CLS_ROW:CLS_ROW + 1, b * NT + NT - 1, :], cls_row).then_inc(cls_in, 16)

            def store(c, n):
                for b in range(B):
                    sp.wait_ge(parts_done[b], after(c))
                    sp.sem_inc(held, 1)
                    sp.dma_start(t["qk_parts"][b][:, :, bass.ds(c * CH, CH)].rearrange("s p n -> p s n"),
                                 qkp[:, b]).then_inc(parts_out[b], 16)
                    sp.wait_ge(v_done[b], after(c))
                    sp.sem_inc(held, 1)
                    sp.dma_start(t["v_rows"][b][bass.ds(c * CH, CH), :].rearrange("(i p) e -> p i e", p=TQ),
                                 vout[0:TQ, b]).then_inc(v_out[b], 16)
                    sp.wait_ge(qn_done[b], after(c))
                    sp.sem_inc(held, 1)
                    sp.dma_start(t["q_squares"][b * H:b * H + H, bass.ds(c * CH, CH)], qn[:, b]).then_inc(qn_out[b], 16)
            with sp.Fori(0, NCH - 2) as c:
                store(c, CH)
            sp.wait_ge(gathered, 16 * WIN_COLS)
            sp.dma_start(t["window_rows"].rearrange("(p r) h -> p (r h)", p=P),
                         win_bias[:].rearrange("p r h -> p (r h)")).then_inc(rows_out, 16)
            sp.wait_ge(rows_out, 16)
            sp.dma_start(win_raw[:].rearrange("n m h -> n (m h)"),
                         t["window_rows"][0:WS2 * WS2, :].rearrange("(n m) h -> n (m h)", m=WS2)).then_inc(window_in, 16)
            store(NCH - 2, CH)
            store(NCH - 1, LASTX)
            sp.wait_ge(kmax_done, B)
            for b in range(B):
                sp.dma_start(t["head_tops"][0:1, b * H:b * H + H].rearrange("a h -> h a"), kmax[:, b:b + 1]).then_inc(tops_out, 16)
            sp.wait_ge(table_done, 2)
            for b in range(B):
                sp.dma_start(t["head_tops"][1:2, b * H:b * H + H].rearrange("a h -> h a"), table_max[:]).then_inc(tops_out, 16)
            for b in range(B):
                sp.wait_ge(parts_out[b], 16 * (NCH + 1))
                sp.wait_ge(v_out[b], 16 * (NCH + 1))
                sp.wait_ge(qn_out[b], 16 * (NCH + 1))
            sp.wait_ge(tops_out, 16 * 2 * B)
            sp.wait_ge(cls_set, 2)
            sp.wait_ge(gather_set, 6)

        @block.gpsimd
        def _(pool):
            for b in range(B):
                for s in (eps_done, rstd_done):
                    pool.sem_inc(s[b], 1)
            nc.gpsimd.memset(identity[:], 0.0).then_inc(ident, 1)
            pool.wait_ge(ident, 1)
            nc.gpsimd.affine_select(out=identity[:], in_=identity[:], compare_op=ALU.not_equal, fill=1.0, base=0,
                                    pattern=[[-1, P]], channel_multiplier=1).then_inc(ident, 1)
            nc.gpsimd.memset(power[:], -0.5).then_inc(consts, 1)
            nc.gpsimd.memset(win_index[:], 0).then_inc(index_clear, 1)
            pool.wait_ge(index_clear, 1)
            whole = WS2 * WS2 // WIN_COLS
            index = ins["L0_attn_rel_index"]
            pool.dma_start(win_index[0:whole, :], index[0:whole * WIN_COLS].rearrange("(p r) -> p r", r=WIN_COLS)).then_inc(index_in, 16)
            pool.dma_start(win_index[whole:whole + 1, 0:WS2 * WS2 - whole * WIN_COLS],
                           index[whole * WIN_COLS:WS2 * WS2].rearrange("(p r) -> p r", p=1)).then_inc(index_in, 16)
            def step(c, n):
                for b in range(B):
                    pool.wait_ge(var_done[b], after(c))
                    pool.sem_inc(held, 1)
                    nc.gpsimd.tensor_scalar(var_eps[0:TQ, b], variance[0:TQ, b], 1.0 / C, EPS, ALU.mult,
                                            ALU.add).then_inc(eps_done[b], 1)
                    pool.wait_ge(eps_done[b], after(c))
                    nc.gpsimd.tensor_tensor(out=rstd[0:TQ, b], in0=var_eps[0:TQ, b], in1=power[0:TQ],
                                            op=ALU.pow).then_inc(rstd_done[b], 1)

            packs, packed_w, voided = t["weights"], t["packed"], t["voided"]
            each = EXPERTS // (NCH - 1)

            def prepare(c):
                blocks = t["slot_x"][bass.ds(c * VOIDS + VOID, VOIDS)]
                pool.dma_start(blocks.rearrange("k p c -> p k c"), void[:].rearrange("p (k c) -> p k c", c=C)).then_inc(voided, 16)
                pool.dma_start(packs[bass.ds(c * each, each), B1_ROW:P, 0:HID].rearrange("e r c -> r e c"),
                               void[0:P - B1_ROW, 0:each * HID].rearrange("r (e c) -> r e c", c=HID)).then_inc(voided, 16)
                for columns, rows, name in ((slice(0, HID), slice(0, C), "L0_ffn_W1"), (slice(HID, PACK), slice(0, P), "L0_ffn_W2")):
                    pool.dma_start(packs[bass.ds(c * each, each), rows, columns], ins[name][bass.ds(c * each, each)]).then_inc(packed_w, 16)

            def set_constants():
                cls_all, gather = t["cls_all"], t["gather"]
                nc.gpsimd.memset(cls_all[:], 0.0).then_inc(cls_set, 1)
                pool.wait_ge(cls_set, 1)
                nc.gpsimd.affine_select(out=cls_all[:].rearrange("p b j w -> p (b j) w"), in_=cls_all[:].rearrange("p b j w -> p (b j) w"),
                                        compare_op=ALU.not_equal, fill=1.0, base=HD,
                                        pattern=[[0, B * H // 2], [-1, VW]], channel_multiplier=HEAD_AT).then_inc(cls_set, 1)
                nc.gpsimd.memset(gather_f[:], 0.0).then_inc(gather_set, 1)
                for j in range(4):
                    pool.wait_ge(gather_set, j + 1)
                    nc.gpsimd.affine_select(out=gather_f[:], in_=gather_f[:], compare_op=ALU.not_equal, fill=1.0, base=-COLUMN_GROUP * j,
                                            pattern=[[-1, COLUMN_GROUP]], channel_multiplier=1).then_inc(gather_set, 1)
                pool.wait_ge(gather_set, 5)
                nc.gpsimd.tensor_copy(gather[:], gather_f[:]).then_inc(gather_set, 1)
                nc.gpsimd.memset(heads_f[:], 1.0).then_inc(consts, 1)
                pool.wait_ge(consts, 2)
                nc.gpsimd.affine_select(out=heads_f[:], in_=heads_f[:], compare_op=ALU.is_ge, fill=0.0, base=0,
                                        pattern=[[-C, 2], [-HD, H]], channel_multiplier=1).then_inc(consts, 1)
                pool.wait_ge(consts, 3)
                nc.gpsimd.affine_select(out=heads_f[:], in_=heads_f[:], compare_op=ALU.is_ge, fill=0.0, base=HD - 1,
                                        pattern=[[C, 2], [HD, H]], channel_multiplier=-1).then_inc(consts, 1)

            def gather_window(columns):
                for r in columns:
                    nc.gpsimd.indirect_dma_start(out=win_bias[:, r, :], out_offset=None, in_=ins["L0_attn_rel_table"],
                                                 in_offset=bass.IndirectOffsetOnAxis(ap=win_index[:, r:r + 1], axis=0)).then_inc(gathered, 16)

            pool.wait_ge(void_set, 1)
            step(0, CH)
            set_constants()
            prepare(0)
            pool.wait_ge(index_in, 32)
            EACH = 5
            GATHERS = -(-WIN_COLS // EACH)
            for c in range(1, GATHERS + 1):
                step(c, CH)
                gather_window(range((c - 1) * EACH, min(c * EACH, WIN_COLS)))
                prepare(c)
            with pool.Fori(GATHERS + 1, NCH - 1) as c:
                step(c, CH)
                prepare(c)
            step(NCH - 1, LASTX)
            pool.dma_start(t["slot_y"][:, BLOCKS - SPARE:BLOCKS, :], void[:, 0:SPARE * C].rearrange("p (k c) -> p k c", c=C)).then_inc(voided, 16)
            pool.wait_ge(voided, 16 * (2 * (NCH - 1) + 1))
            pool.wait_ge(b2_split, 4)
            pool.dma_start(packs[:, B1_ROW:B1_ROW + 1, 0:HID], ins["L0_ffn_b1"].unsqueeze(1)).then_inc(packed_w, 16)
            pool.dma_start(packs[:, B2_ROW:B2_ROW + PARTS, 0:C // 2], b2_parts[:].bitcast(F32)).then_inc(packed_w, 16)

        @block.scalar
        def _(act):
            for b in range(B):
                for s in (feat_done, xnT_done, qk_done, qksq_done, v_done, qn_done):
                    act.sem_inc(s[b], 1)
            act.wait_ge(packed, 2)

            def features(c):
                n = patches(c)
                for b in range(B):
                    act.wait_ge(x_in[b], 32 if isinstance(c, int) and c < 2 else 64)
                    act.sem_inc(held, 1)
                    act.wait_ge(mixed[b], before(c))
                    act.wait_ge(silu_done[b], before(c))
                    for f in range(2):
                        last = nc.scalar.activation(feat[:, b, f, 0:n], x2[:, b, bass.ds(c * CH, n)], ACT.Sigmoid,
                                                    scale=slope[:, f:f + 1])
                    last.then_inc(feat_done[b], 1)

            def turned_rows(b, c):
                act.wait_ge(xnT_ps[b], after(c))
                act.wait_ge(v_ps[b], before(c))
                nc.scalar.copy(xnT[:, b], ps_t[0:C, 0:CH]).then_inc(xnT_done[b], 1)

            def project(b, c):
                act.wait_ge(qk_ps[b], after(c))
                act.wait_ge(parts_done[b], before(c))
                act.wait_ge(qksq_done[b], before(c))
                nc.scalar.activation(qk[:, b], ps_qk[:, b, 0:CH], ACT.Copy, scale=qscale[:]).then_inc(qk_done[b], 1)
                act.wait_ge(qk_done[b], after(c))
                act.wait_ge(n_ps[b], before(c))
                nc.scalar.activation(qksq[:, b], qk[:, b], ACT.Square).then_inc(qksq_done[b], 1)
                act.wait_ge(v_ps[b], after(c))
                act.wait_ge(v_out[b], 16 * before(c))
                nc.scalar.copy(vout[0:TQ, b].rearrange("p i e -> p (i e)"), ps_v[0:TQ, 0:CT * C]).then_inc(v_done[b], 1)

            def squares(c):
                for b in range(B):
                    act.wait_ge(n_ps[b], after(c))
                    act.wait_ge(qn_out[b], 16 * before(c))
                    nc.scalar.copy(qn[:, b], ps_n[0:H, b, 0:CH]).then_inc(qn_done[b], 1)

            def start():
                features(0)
                features(1)

            def turn(c):
                turned_rows(0, c)
                if not is_first(c):
                    squares(c - 1)
                turned_rows(1, c)
                project(0, c)
                if has_features(c):
                    features(c + 2)
                project(1, c)

            def tail():
                turned_rows(0, NCH - 1)
                squares(NCH - 2)
                turned_rows(1, NCH - 1)
                for b in range(B):
                    project(b, NCH - 1)
                squares(NCH - 1)
            nc.scalar.preload_act_table(ACT.Sigmoid)
            pipelined(act, start, turn, tail)

        @block.vector
        def _(dve):
            for b in range(B):
                for s in (silu_done, h_done, sum_done, mean_done, centre_done, square_done, var_done, norm_done, hi_done,
                          rest1_done, mid_done, rest2_done, parts_done, kn_done):
                    dve.sem_inc(s[b], 1)
            for b in range(B):
                last = nc.vector.memset(h[96:TQ, b * NT + NT - 1, :], 0.0)
            last.then_inc(padded, 1)
            nc.vector.memset(void[:], 0.0).then_inc(void_set, 1)
            dve.wait_ge(w_in, 16 * LOADS)
            for f, half, src in ((0, 0, spl_raw[:, :, 0]), (0, 1, spl_raw[:, :, 1]), (1, 0, spl_raw[:, :, 2]),
                                 (1, 1, base_raw[:])):
                nc.vector.tensor_copy(mix_raw[:, f, half, :], src).then_inc(packed_raw, 1)
            nc.vector.tensor_copy(slope[0:C, 0:1], bases[0:C, 0:1])
            nc.vector.tensor_copy(slope[C:P, 0:1], bases[C:P, 1:2])
            nc.vector.tensor_copy(slope[0:C, 1:2], bases[0:C, 2:3])
            nc.vector.memset(slope[C:P, 1:2], 1.0).then_inc(packed, 1)
            nc.vector.memset(qscale[C:P, :], 1.0)
            nc.vector.memset(qscale[0:C, :], float(HD) ** -0.5).then_inc(packed, 1)
            nc.vector.tensor_tensor(bias_e[:], bias_spline[:], bias_base[:], ALU.add).then_inc(packed, 1)
            for n, (dst, src) in enumerate(((mixT[:, 0, :], ps_t[:, 0:C]), (mixT[:, 1, :], ps_t[:, C:2 * C]),
                                            (qkvT[:, 0:C], ps_t[0:C, 2 * C:3 * C]), (qkvT[:, C:2 * C], ps_t[0:C, 3 * C:4 * C]),
                                            (qkvT[:, 2 * C:], ps_t[0:C, 4 * C:5 * C]), (wprojT[0:C], ps_t[0:C, 5 * C:6 * C]))):
                dve.wait_ge(turned, 1)
                nc.vector.tensor_copy(dst, src).then_inc(turned_out, 1)
            dve.wait_ge(padded, 1)
            dve.wait_ge(packed, 3)

            def silu(c):
                n = patches(c)
                for b in range(B):
                    dve.wait_ge(feat_done[b], after(c))
                    nc.vector.tensor_tensor(feat[C:P, b, 1, 0:n], feat[C:P, b, 1, 0:n], x2[C:P, b, bass.ds(c * CH, n)],
                                            ALU.mult).then_inc(silu_done[b], 1)

            def tokens(b, c):
                n = patches(c)
                tile = b * NT + c * CT
                full = n // TQ
                dve.wait_ge(mixed[b], after(c))
                dst = h[0:TQ, bass.ds(tile, full), :]
                psv = ps_h[:, b, 0:CT * C].rearrange("p (i e) -> p i e", e=C)
                over = bias_e[0:TQ].unsqueeze(1).to_broadcast([TQ, full, C])
                last = nc.vector.tensor_tensor(dst, psv[0:TQ, 0:full], over, ALU.add)
                if full < CT:
                    rows = n - full * TQ
                    last = nc.vector.tensor_tensor(h[0:rows, tile + full, :], psv[0:rows, full], bias_e[0:rows], ALU.add)
                    dve.wait_ge(cls_in, 16 * B)
                last.then_inc(h_done[b], 1)
                tok = h[0:TQ, bass.ds(tile, CT), :]
                dve.wait_ge(h_done[b], after(c))
                dve.sem_inc(held, 1)
                nc.vector.tensor_reduce(total[0:TQ, b], tok, AX.X, ALU.add).then_inc(sum_done[b], 1)
                dve.wait_ge(sum_done[b], after(c))
                nc.vector.tensor_scalar(neg_mean[0:TQ, b], total[0:TQ, b], -1.0 / C, None, ALU.mult).then_inc(mean_done[b], 1)
                dve.wait_ge(mean_done[b], after(c))
                nc.vector.tensor_tensor(centred[0:TQ, b], tok, neg_mean[0:TQ, b].unsqueeze(2).to_broadcast([TQ, CT, C]),
                                        ALU.add).then_inc(centre_done[b], 1)
                dve.wait_ge(centre_done[b], after(c))
                nc.vector.tensor_tensor(square[0:TQ, b], centred[0:TQ, b], centred[0:TQ, b], ALU.mult).then_inc(square_done[b], 1)
                dve.wait_ge(square_done[b], after(c))
                nc.vector.tensor_reduce(variance[0:TQ, b], square[0:TQ, b], AX.X, ALU.add).then_inc(var_done[b], 1)

            def normalise(b, c):
                dve.wait_ge(rstd_done[b], after(c))
                dve.wait_ge(xnT_ps[b], before(c))
                nc.vector.tensor_tensor(xn[0:TQ, b], centred[0:TQ, b], rstd[0:TQ, b].unsqueeze(2).to_broadcast([TQ, CT, C]),
                                        ALU.mult).then_inc(norm_done[b], 1)

            def split(b, c):
                dve.wait_ge(qk_done[b], after(c))
                dve.wait_ge(parts_out[b], 16 * before(c))
                nc.vector.tensor_copy(qkp[:, b, 0], qk[:, b]).then_inc(hi_done[b], 1)
                dve.wait_ge(hi_done[b], after(c))
                nc.vector.tensor_tensor(rest1[:, b], qk[:, b], qkp[:, b, 0], ALU.subtract).then_inc(rest1_done[b], 1)
                dve.wait_ge(rest1_done[b], after(c))
                nc.vector.tensor_copy(qkp[:, b, 1], rest1[:, b]).then_inc(mid_done[b], 1)
                dve.wait_ge(mid_done[b], after(c))
                nc.vector.tensor_tensor(qkp[:, b, 2], rest1[:, b], qkp[:, b, 1], ALU.subtract).then_inc(parts_done[b], 1)

            def longest(c):
                for b in range(B):
                    dve.wait_ge(n_ps[b], after(c))
                    dve.sem_inc(held, 1)
                    nc.vector.tensor_reduce(kn[:, b, bass.ds(c, 1)], ps_n[K_ROW:K_ROW + H, b, 0:CH], AX.X, ALU.max).then_inc(kn_done[b], 1)

            def split_b2():
                dve.wait_ge(b2_loaded, 16)
                nc.vector.tensor_copy(b2_parts[:, 0], b2_in[:]).then_inc(b2_split, 1)
                dve.wait_ge(b2_split, 1)
                nc.vector.tensor_tensor(b2_rest[:], b2_in[:], b2_parts[:, 0], ALU.subtract).then_inc(b2_split, 1)
                dve.wait_ge(b2_split, 2)
                nc.vector.tensor_copy(b2_parts[:, 1], b2_rest[:]).then_inc(b2_split, 1)
                dve.wait_ge(b2_split, 3)
                nc.vector.tensor_tensor(b2_parts[:, 2], b2_rest[:], b2_parts[:, 1], ALU.subtract).then_inc(b2_split, 1)

            def start():
                silu(0)
                for b in range(B):
                    tokens(b, 0)
                for b in range(B):
                    normalise(b, 0)
                silu(1)

            def turn(c):
                if not is_first(c):
                    longest(c - 1)
                for b in range(B):
                    tokens(b, c + 1)
                normalise(0, c + 1)
                split(0, c)
                normalise(1, c + 1)
                if has_features(c):
                    silu(c + 2)
                split(1, c)
                if isinstance(c, int) and c < NCH - 2:
                    prepare_stack(nc, dve, t, 0 if c == 0 else 1, zeros_set, c // (NCH - 3) + 1)
                if is_first(c):
                    split_b2()
                    dve.wait_ge(consts, 4)
                    nc.vector.tensor_copy(heads_of[:], heads_f[:]).then_inc(heads_set, 1)

            def tail():
                longest(NCH - 2)
                for b in range(B):
                    split(b, NCH - 1)
                longest(NCH - 1)
            pipelined(dve, start, turn, tail)
            for b in range(B):
                dve.wait_ge(kn_done[b], after(NCH - 1))
                nc.vector.tensor_reduce(kmax[:, b:b + 1], kn[:, b], AX.X, ALU.max).then_inc(kmax_done, 1)
            dve.wait_ge(table_in, 16)
            nc.vector.tensor_reduce(table_max[:], table[:], AX.X, ALU.max).then_inc(table_done, 1)
            dve.wait_ge(table_done, 1)
            nc.vector.tensor_scalar(table_max[:], table_max[:], 0.0, None, ALU.max).then_inc(table_done, 1)
            dve.wait_ge(window_in, 16)
            nc.vector.tensor_copy(window[:], win_raw[:].rearrange("n m h -> n h m")).then_inc(table_done, 1)

        @block.tensor
        def _(pe):
            for b in range(B):
                for s in (mixed, xnT_ps, qk_ps, v_ps, n_ps):
                    pe.sem_inc(s[b], 1)
            pe.wait_ge(ident, 2)
            pe.wait_ge(w_in, 16 * LOADS)
            pe.wait_ge(packed_raw, 4)
            eye = identity[0:C, 0:C]
            for f in range(2):
                nc.tensor.transpose(ps_t[:, C * f:C * f + C], mix_raw[:, f].rearrange("e a c -> e (a c)"), eye)
            for s in range(3):
                nc.tensor.transpose(ps_t[0:C, C * (2 + s):C * (3 + s)], qkv_raw[:, s, :], eye)
            nc.tensor.transpose(ps_t[0:C, 5 * C:6 * C], proj_raw[:], eye).then_inc(turned, 1)
            pe.wait_ge(turned_out, TURNED)

            def mix(b, c):
                n = patches(c)
                pe.wait_ge(silu_done[b], after(c))
                pe.wait_ge(h_done[b], before(c))
                for i in range(CT):
                    rows = min(TQ, n - i * TQ)
                    for f in range(2):
                        last = nc.tensor.matmul(ps_h[0:rows, b, C * i:C * i + C], feat[:, b, f, TQ * i:TQ * i + rows],
                                                mixT[:, f, :], start=(f == 0), stop=(f == 1))
                last.then_inc(mixed[b], 1)

            def turn_rows(b, c):
                pe.wait_ge(norm_done[b], after(c))
                pe.wait_ge(xnT_done[1 - b], after(c) if b else before(c))
                pe.sem_inc(held, 1)
                for i in range(CT):
                    last = nc.tensor.transpose(ps_t[0:C, TQ * i:TQ * i + TQ], xn[0:TQ, b, i, :], identity[0:TQ, 0:TQ])
                last.then_inc(xnT_ps[b], 1)

            def project(b, c):
                pe.wait_ge(xnT_done[b], after(c))
                pe.wait_ge(qk_done[b], before(c))
                nc.tensor.matmul(ps_qk[:, b, 0:CH], qkvT[:, 0:2 * C], xnT[:, b], start=True, stop=True).then_inc(qk_ps[b], 1)
                pe.wait_ge(v_done[1 - b], after(c) if b else before(c))
                for i in range(CT):
                    last = nc.tensor.matmul(ps_v[0:TQ, C * i:C * i + C], xnT[:, b, TQ * i:TQ * i + TQ], qkvT[:, 2 * C:],
                                            start=True, stop=True)
                last.then_inc(v_ps[b], 1)

            def squares(b, c):
                pe.wait_ge(qksq_done[b], after(c))
                pe.wait_ge(qn_done[b], before(c))
                pe.wait_ge(kn_done[b], before(c))
                for w in range(2):
                    last = nc.tensor.matmul(ps_n[K_ROW * w:K_ROW * w + H, b, 0:CH], heads_of[:, w, :], qksq[:, b], start=True, stop=True)
                last.then_inc(n_ps[b], 1)

            def start():
                for b in range(B):
                    mix(b, 0)

            def turn(c):
                turn_rows(0, c)
                if not is_first(c):
                    for b in range(B):
                        squares(b, c - 1)
                turn_rows(1, c)
                for b in range(B):
                    mix(b, c + 1)
                for b in range(B):
                    project(b, c)
                if is_first(c):
                    pe.wait_ge(heads_set, 1)

            def tail():
                turn_rows(0, NCH - 1)
                for b in range(B):
                    squares(b, NCH - 2)
                turn_rows(1, NCH - 1)
                for b in range(B):
                    project(b, NCH - 1)
                for b in range(B):
                    squares(b, NCH - 1)
            pipelined(pe, start, turn, tail)


def load_stack(sp, t, b, head, q_stack, k_stack, key0, done):
    parts = t["qk_parts"][b] if isinstance(b, int) else t["qk_parts"][bass.ds(b, 1)].rearrange("a s r n -> (a s) r n")
    for j in range(PARTS):
        rows = slice(j * PARTS * HD, (j + 1) * PARTS * HD)
        of_q = parts[j:j + 1, bass.ds(head * HD, HD), :].to_broadcast([PARTS, HD, NP])
        sp.dma_start(q_stack[rows, 0:NP], of_q).then_inc(done, 16)
        of_k = parts[:, bass.ds(head * HD + C, HD), :]
        sp.dma_start(k_stack[rows, key0:key0 + N], of_k[:, :, 0:N]).then_inc(done, 16)


def load_shift(sp, t, b, head, q_stack, done):
    of_shift = t["shift_parts"][bass.ds(b * H + head, 1)].rearrange("a s n -> (a s) n")
    sp.dma_start(q_stack[SROWS:STACK, 0:NP], of_shift).then_inc(done, 16)


def load_values(sp, t, b):
    v_rows = t["v_rows"][b]
    part = KB // V_PARTS
    for n in range(V_PARTS):
        sp.dma_start(t["v_all"][:, b, n * part:(n + 1) * part, :],
                     v_rows[n * part * P:(n + 1) * part * P].rearrange("(k p) e -> p k e", p=P)).then_inc(t["v_in"][b], 16)
    for p in range(2):
        sp.dma_start(t["cls_all"][p:p + 1, b, :, p * HEAD_AT:p * HEAD_AT + HD],
                     v_rows[PATCHES:N].rearrange("a (j s d) -> a j s d", s=2, d=HD)[:, :, p, :]).then_inc(t["v_in"][b], 16)


def settle_shifts(nc, ins, t):
    ctx = ExitStack()
    with ctx:
        ctx.enter_context(nc.cleanup_on_exit())

        def sb(name, shape, dt=F32):
            return ctx.enter_context(nc.sbuf_tensor(name, shape, dt))

        def sem(name):
            return nc.alloc_semaphore(name)

        COLS = B * H * NP // P
        shift = sb("shift", [P, COLS])
        k_top = sb("k_top", [P, 1])
        k_scale = sb("k_scale", [P, 1])
        bias_top = sb("bias_top", [P, 1])
        top = sb("top", [P, 1])
        top_all = sb("top_all", [P, 1])
        wide = sb("wide", [1, 1])
        general = sb("general", [1, 1], I32)
        rest1 = sb("s_rest1", [P, COLS])
        parts = sb("s_parts", [P, PARTS, COLS], BF16)
        q_stack = sb("m_q_stack", [SROWS, QT * P], BF16)
        k_stack = sb("m_k_stack", [SROWS, NP], BF16)
        row_top = sb("row_top", [P, NCH])
        row_tops = sb("row_tops", [P, QT])
        place = sb("place", [WS2, P])
        ps_s = ctx.enter_context(nc.psum_tensor("ps_s", [P, PARTS, 512], F32))

        loaded, scaled, rooted, raised, top_done, top_shared, wide_done, flagged = (sem(n) for n in (
            "loaded", "scaled", "rooted", "raised", "top_done", "top_shared", "wide_done", "flagged"))
        split, parts_out = sem("split"), sem("s_parts_out")
        prepared, placed, stack_in, piece_done, piece_read, tile_done, head_out, max_in = (sem(n) for n in (
            "prepared", "placed", "m_stack_in", "piece_done", "piece_read", "tile_done", "head_out", "max_in"))
        held, zeros_set = sem("s_held"), sem("s_zeros_set")
        PIECES = NCH
        BANKS = 3
        WINDOW_TILE = (WIN0 + WS2) // P - 1

        block = ctx.enter_context(nc.Block())

        @block.sync
        def _(sp):
            sp.dma_start(shift[:], t["q_squares"].rearrange("g (s n) -> (g s) n", n=COLS)).then_inc(loaded, 16)
            per = P // (B * H)
            for n, dst in enumerate((k_top, bias_top)):
                sp.dma_start(dst[:], t["head_tops"][n].unsqueeze(1).unsqueeze(2).to_broadcast([B * H, per, 1])).then_inc(loaded, 16)
            for p in range(2):
                load_stack(sp, t, 0, p, t["q_stack"][0][p], t["k_stack"][0][p], KEY0, t["stack_in"][0])
            load_values(sp, t, 0)
            sp.wait_ge(flagged, 1)
            wide_bound = sp.value_load(general[0:1, 0:1], min_val=0, max_val=1)
            with sp.If(wide_bound > 0):
                sp.sem_inc(head_out, 16)
                sp.wait_ge(prepared, 1)
                with sp.Fori(0, B) as b:
                    with sp.Fori(0, H) as n:
                        sp.wait_ge(tile_done, (b * H + n) * QT + 1)
                        sp.sem_inc(held, 1)
                        load_stack(sp, t, b, n, q_stack, k_stack, 0, stack_in)
                        sp.wait_ge(tile_done, (b * H + n) * QT + QT + 1)
                        sp.sem_inc(held, 1)
                        with nc.allow_non_contiguous_dma(reason="4097 maxima of a head"):
                            sp.dma_start(t["row_max"][bass.ds(b * H + n, 1), :].rearrange("a (i p) -> p (a i)", p=P),
                                         row_tops[:]).then_inc(head_out, 16)
                sp.wait_ge(head_out, 16 * B * H + 16)
                sp.dma_start(shift[:], t["row_max"][:, 0:NP].rearrange("g (s n) -> g s n", n=COLS)).then_inc(max_in, 16)
            with sp.Else():
                sp.sem_inc(held, 1)
            sp.wait_ge(split, 4)
            for j in range(PARTS):
                sp.dma_start(t["shift_parts"][:, j, :].rearrange("g (s n) -> g s n", n=COLS), parts[:, j, :]).then_inc(parts_out, 16)
            sp.wait_ge(parts_out, 16 * PARTS)

        @block.gpsimd
        def _(pool):
            nc.gpsimd.memset(place[:], 0.0).then_inc(placed, 1)
            pool.wait_ge(placed, 1)
            nc.gpsimd.affine_select(out=place[:], in_=place[:], compare_op=ALU.not_equal, fill=1.0, base=P - WS2,
                                    pattern=[[-1, P]], channel_multiplier=1).then_inc(placed, 1)
            pool.wait_ge(placed, 2)
            pool.wait_ge(top_done, 1)
            nc.gpsimd.partition_all_reduce(top_all[:], top[:], P, RMAX).then_inc(top_shared, 1)

        @block.scalar
        def _(act):
            act.wait_ge(scaled, 1)
            nc.scalar.activation(shift[:], shift[:], ACT.Sqrt, scale=k_scale[:]).then_inc(rooted, 1)

        @block.vector
        def _(dve):
            prepare_stack(nc, dve, t, 2, zeros_set, 1)
            dve.wait_ge(loaded, 48)
            nc.vector.tensor_scalar(k_scale[:], k_top[:], 1.03, None, ALU.mult).then_inc(scaled, 1)
            dve.wait_ge(rooted, 1)
            nc.vector.tensor_scalar(shift[:], shift[:], bias_top[:], None, ALU.add).then_inc(raised, 1)
            dve.wait_ge(raised, 1)
            nc.vector.tensor_reduce(top[:], shift[:], AX.X, ALU.max).then_inc(top_done, 1)
            dve.wait_ge(top_shared, 1)
            nc.vector.tensor_scalar(wide[:], top_all[0:1, :], SAFE, None, ALU.is_gt).then_inc(wide_done, 1)
            dve.wait_ge(wide_done, 1)
            nc.vector.tensor_copy(general[:], wide[:]).then_inc(flagged, 1)
            dve.wait_ge(flagged, 1)
            wide_bound = dve.value_load(general[0:1, 0:1], min_val=0, max_val=1)
            with dve.If(wide_bound > 0):
                dve.sem_inc(tile_done, 1)
                dve.sem_inc(piece_read, BANKS)
                nc.vector.memset(q_stack[:, NP:QT * P], 0.0).then_inc(prepared, 1)
                with dve.Fori(0, B * H) as n:
                    with dve.Fori(0, QT) as i:
                        dve.wait_ge(tile_done, n * QT + i + 1)
                        for k in range(PIECES):
                            keys = CH if k < PIECES - 1 else N - (PIECES - 1) * CH
                            dve.wait_ge(piece_done, (n * QT + i) * PIECES + k + 1)
                            nc.vector.tensor_reduce(row_top[:, k:k + 1], ps_s[:, k % BANKS, 0:keys], AX.X, ALU.max).then_inc(piece_read, 1)
                        dve.wait_ge(piece_read, (n * QT + i) * PIECES + PIECES + BANKS)
                        dve.wait_ge(head_out, 16 * n + 16)
                        dve.sem_inc(held, 1)
                        nc.vector.tensor_reduce(row_tops[:, bass.ds(i, 1)], row_top[:], AX.X, ALU.max).then_inc(tile_done, 1)
                dve.wait_ge(max_in, 16)
                dve.sem_inc(held, 1)
            with dve.Else():
                dve.sem_inc(held, 1)
            nc.vector.tensor_scalar(parts[:, 0, :], shift[:], -1.0, None, ALU.mult).then_inc(split, 1)
            dve.wait_ge(split, 1)
            nc.vector.scalar_tensor_tensor(out=rest1[:], in0=shift[:], scalar=-1.0, in1=parts[:, 0, :], op0=ALU.mult,
                                           op1=ALU.subtract).then_inc(split, 1)
            dve.wait_ge(split, 2)
            nc.vector.tensor_copy(parts[:, 1, :], rest1[:]).then_inc(split, 1)
            dve.wait_ge(split, 3)
            nc.vector.tensor_tensor(parts[:, 2, :], rest1[:], parts[:, 1, :], ALU.subtract).then_inc(split, 1)
            prepare_stack(nc, dve, t, 3, zeros_set, 2)

        @block.tensor
        def _(pe):
            pe.wait_ge(flagged, 1)
            wide_bound = pe.value_load(general[0:1, 0:1], min_val=0, max_val=1)
            with pe.If(wide_bound > 0):
                pe.wait_ge(prepared, 1)
                pe.wait_ge(placed, 2)
                pe.sem_inc(held, 1)

                def tile(n, i, windowed):
                    for k in range(PIECES):
                        keys = CH if k < PIECES - 1 else N - (PIECES - 1) * CH
                        pe.wait_ge(piece_read, (n * QT + i) * PIECES + k + 1)
                        pe.sem_inc(held, 1)
                        over = windowed and k == PIECES - 1
                        last = nc.tensor.matmul(ps_s[:, k % BANKS, 0:keys], q_stack[:, bass.ds(i * P, P)],
                                                k_stack[:, k * CH:k * CH + keys], start=True, stop=not over)
                        if over:
                            at = WIN0 - k * CH
                            last = nc.tensor.matmul(ps_s[:, k % BANKS, at:at + WS2], place[:],
                                                    windowed[0], start=False, stop=True)
                        last.then_inc(piece_done, 1)

                with pe.Fori(0, B) as b:
                    with pe.Fori(0, H) as hd:
                        n = pe.snap(b * H + hd)
                        pe.wait_ge(stack_in, n * (16 * 2 * PARTS) + 16 * 2 * PARTS)
                        pe.sem_inc(held, 1)
                        with pe.Fori(0, WINDOW_TILE) as i:
                            tile(n, i, None)
                        bias = t["window"][:, bass.ds(hd, 1), :].rearrange("n a m -> n (a m)")
                        tile(n, WINDOW_TILE, [bias])
                        tile(n, WINDOW_TILE + 1, None)
            with pe.Else():
                pe.sem_inc(held, 1)


def attend(nc, ins, t):
    ctx = ExitStack()
    with ctx:
        ctx.enter_context(nc.cleanup_on_exit())

        def sb(name, shape, dt=F32):
            return ctx.enter_context(nc.sbuf_tensor(name, shape, dt))

        def sem(name):
            return nc.alloc_semaphore(name)

        def pair(name):
            return [sem(f"{name}{n}") for n in range(2)]

        GROUPS = 2 * NG
        PAIRS = B * H // 2
        PER_IMAGE = H // 2 // SLOTS
        W = COLUMN_GROUP
        RING = 4
        ring_at = [g % 3 for g in range(GROUPS - RING)] + list(range(RING))
        back = [next(d for d in range(1, GROUPS + 1) if ring_at[(g - d) % GROUPS] == ring_at[g]) for g in range(GROUPS)]
        AHEAD = 2
        FINISH = 6

        q_stack, k_stack, v_head, v_cls, win_head = (t[k] for k in ("q_stack", "k_stack", "v_head", "v_cls", "win_head"))
        probs = sb("probs", [P, RING, KG, CH])
        o_rest = sb("o_rest", [P, 2, CH])
        o_parts = sb("o_parts", [P, 2, PARTS, CH], BF16)
        inverse = sb("inverse", [P, 2, CT, 2, 1])
        identity, attn, v_all, cls_all, gather = (t[k] for k in ("identity", "attn", "v_all", "cls_all", "gather"))

        ps_s = ctx.enter_context(nc.psum_tensor("ps_scores", [P, 2, KG, 512], F32))
        ps_o = ctx.enter_context(nc.psum_tensor("ps_out", [P, 2, 512], F32))

        v_in, stack_in, v_ready = t["v_in"], t["stack_in"], pair("v_ready")
        scored, exped, valued = sem("scored"), sem("exped"), sem("valued")
        parts_ready, turned, split, inverted, normed = (pair(n) for n in (
            "parts_ready", "o_turned", "o_split", "o_inverted", "normed"))
        cleared = sem("cleared")
        a_held = sem("a_held")
        LOADS = 16 * 2 * (2 * PARTS + 1)
        STAGED = 5
        PAIR_GROUPS = NCH * GROUPS
        TURNS = PAIRS // SLOTS
        START = PAIR_GROUPS + RING

        def bank_turn(turn_no, u, r, w):
            return turn_no * NCH + (u * NCH + w) // 2 + r

        block = ctx.enter_context(nc.Block())

        @block.sync
        def _(sp):
            def load_pair(b, j, u):
                sp.wait_ge(scored, (((b * PER_IMAGE + j) * SLOTS + u) - 1) * PAIR_GROUPS + START)
                sp.sem_inc(a_held, 1)
                for p in range(2):
                    load_stack(sp, t, b, j * 2 * SLOTS + 2 * u + p, q_stack[u][p], k_stack[u][p], KEY0, stack_in[u])
                for p in range(2):
                    load_shift(sp, t, b, j * 2 * SLOTS + 2 * u + p, q_stack[u][p], stack_in[u])

            for p in range(2):
                load_shift(sp, t, 0, p, q_stack[0][p], stack_in[0])
            for u in range(1, SLOTS):
                load_pair(0, 0, u)
            load_values(sp, t, 1)
            for b in range(B):
                with sp.Fori(1 if b == 0 else 0, PER_IMAGE) as j:
                    for u in range(SLOTS):
                        load_pair(b, j, u)
            sp.wait_ge(t["voided"], 16 * (2 * (NCH - 1) + 1))
            sp.wait_ge(t["packed"], 16 * (2 * (NCH - 1) + 2))

        @block.gpsimd
        def _(pool):
            def stage(b, j, u):
                pool.wait_ge(valued, (((b * PER_IMAGE + j) * SLOTS + u) - 1) * PAIR_GROUPS + START)
                pool.sem_inc(a_held, 1)
                nc.gpsimd.tensor_copy(v_cls[u][0:2], cls_all[:, b, bass.ds(j * SLOTS + u, 1), :].rearrange("p c w -> p (c w)")
                                      ).then_inc(v_ready[u], 1)
                for p in range(2):
                    head = j * 2 * SLOTS + 2 * u + p
                    nc.gpsimd.tensor_copy(v_head[u][p][:, :, p * HEAD_AT:p * HEAD_AT + HD],
                                          v_all[:, b, :, bass.ds(head * HD, HD)]
                                          ).then_inc(v_ready[u], 1)
                    nc.gpsimd.tensor_copy(win_head[u][p][:, P - WS2:P],
                                          t["window"][:, bass.ds(head, 1), :].rearrange("n a m -> n (a m)")
                                          ).then_inc(v_ready[u], 1)

            for b in range(B):
                pool.wait_ge(v_in[b], 16 * (V_PARTS + 2))
                pool.sem_inc(a_held, 1)
                with pool.Fori(0, PER_IMAGE) as j:
                    for u in range(SLOTS):
                        stage(b, j, u)

        @block.scalar
        def _(act):
            nc.scalar.preload_act_table(ACT.Exp)
            with act.Fori(0, PAIRS * NCH) as k:
                for g in range(GROUPS):
                    act.wait_ge(scored, k * GROUPS + g + 1 + START)
                    act.wait_ge(valued, k * GROUPS + g - back[g] + 1 + START)
                    banks = KG if g != NG - 1 else KB % KG
                    nc.scalar.activation(probs[:, ring_at[g], 0:banks], ps_s[:, g % 2, 0:banks, 0:CH], ACT.Exp).then_inc(exped, 1)

        @block.vector
        def _(dve):
            for p in range(2):
                dve.sem_inc(normed[p], 1)
            nc.vector.memset(ps_o[:], 0.0).then_inc(cleared, 1)
            nc.vector.memset(o_parts[:, 1], 0.0).then_inc(parts_ready[1], 1)

            def finish(b, j, u, r, w):
                bank = (u + w) % 2
                turn_no = b * PER_IMAGE + j
                m = dve.snap(bank_turn(turn_no, u, r, w))
                dve.wait_ge(valued, (turn_no * SLOTS * NCH + u * NCH + r * 2 + w + 1) * GROUPS + START)
                nc.vector.tensor_copy(o_parts[:, bank, 0], ps_o[:, bank, 0:CH]).then_inc(split[bank], 1)
                dve.wait_ge(split[bank], m * 3 + 1)
                nc.vector.tensor_tensor(o_rest[:, bank], ps_o[:, bank, 0:CH], o_parts[:, bank, 0], ALU.subtract).then_inc(split[bank], 1)
                dve.wait_ge(split[bank], m * 3 + 2)
                nc.vector.tensor_copy(o_parts[:, bank, 1], o_rest[:, bank]).then_inc(split[bank], 1)
                dve.wait_ge(split[bank], m * 3 + 3)
                nc.vector.tensor_tensor(o_parts[:, bank, 2], o_rest[:, bank], o_parts[:, bank, 1], ALU.subtract).then_inc(parts_ready[bank], 1)
                dve.wait_ge(turned[bank], m + 1 + bank)
                sums = ps_o[0:TQ, bank, 0:CT * W].rearrange("q (i p d) -> q i p d", p=2, d=HEAD_AT)
                dve.wait_ge(normed[bank], m + 1)
                nc.vector.reciprocal(inverse[0:TQ, bank], sums[:, :, :, HD:HD + 1]).then_inc(inverted[bank], 1)
                dve.wait_ge(inverted[bank], m + 1)
                dst = attn[0:TQ, bass.ds(b * NT + r * 2 * CT + w * CT, CT), bass.ds(j * (2 * SLOTS * HD) + 2 * u * HD, 2 * HD)]
                nc.vector.tensor_tensor(dst.rearrange("q i (p d) -> q i p d", p=2), sums[:, :, :, 0:HD],
                                        inverse[0:TQ, bank].to_broadcast([TQ, CT, 2, HD]), ALU.mult).then_inc(normed[bank], 1)

            with dve.Fori(0, B) as b:
                with dve.Fori(0, PER_IMAGE) as j:
                    for u in range(SLOTS):
                        with dve.Fori(0, NCH // 2) as r:
                            for w in range(2):
                                finish(b, j, u, r, w)
                        finish(b, j, u, NCH // 2, 0)

        @block.tensor
        def _(pe):
            pe.sem_inc(exped, AHEAD)
            pe.sem_inc(scored, START)
            pe.sem_inc(valued, START)

            def scores(u, c, g, windowed):
                p, first = g // NG, g % NG * KG
                for s in range(min(KG, KB - first)):
                    over = windowed and first + s == (WIN0 + WS2) // P - 1
                    last = nc.tensor.matmul(ps_s[:, g % 2, s, 0:CH], k_stack[u][p][:, KEY0 + (first + s) * P:KEY0 + (first + s + 1) * P],
                                            q_stack[u][p][:, bass.ds(c * CH, CH)], start=True, stop=not over)
                    if over:
                        at = WIN0 - (NCH - 1) * CH
                        last = nc.tensor.matmul(ps_s[:, g % 2, s, at:at + WS2], win_head[u][p][:], identity[0:WS2, 0:WS2],
                                                start=False, stop=True)
                if g == GROUPS - 1:
                    for head, columns in enumerate((slice(CLS_COL, CLS_COL + 2), slice(0, CLS_COL + 1, CLS_COL))):
                        last = nc.tensor.matmul(ps_s[0:2, g % 2, KB % KG, 0:CH], k_stack[u][head][:, columns],
                                                q_stack[u][head][:, bass.ds(c * CH, CH)], start=head == 0, stop=head == 1)
                last.then_inc(scored, 1)

            def values(u, bank, g):
                p, first = g // NG, g % NG * KG
                for s in range(min(KG, KB - first)):
                    kb = first + s
                    at = W * (kb % 4)
                    last = nc.tensor.matmul(ps_o[at:at + VW, bank, 0:CH], v_head[u][p][:, kb, :], probs[:, ring_at[g], s],
                                            start=p == 0 and kb < 4, stop=p == 1 and kb > KB - 4)
                if g == GROUPS - 1:
                    last = nc.tensor.matmul(ps_o[0:VW, bank, 0:CH], v_cls[u][:], probs[:, ring_at[g], KB % KG], start=False, stop=True)
                last.then_inc(valued, 1)

            def turn(bank):
                for i in range(CT):
                    for part in range(PARTS):
                        last = nc.tensor.matmul(ps_o[0:TQ, bank, W * i:W * i + W], o_parts[:, bank, part, TQ * i:TQ * i + TQ],
                                                gather[:], start=part == 0, stop=part == PARTS - 1)
                last.then_inc(turned[bank], 1)

            def body(turn_no, u, r, w, last_pair):
                k = (turn_no * SLOTS + u) * NCH + r * 2 + w
                bank, m = (u + w) % 2, bank_turn(turn_no, u, r, w)
                ends = isinstance(r, int)
                for g in range(AHEAD, GROUPS + AHEAD):
                    pe.wait_ge(exped, k * GROUPS + g + 1)
                    if g < GROUPS:
                        scores(u, r * 2 + w, g, ends)
                    elif not ends:
                        scores(u, r * 2 + (w + 1), g - GROUPS, False)
                    elif not last_pair:
                        if g == GROUPS:
                            pe.wait_ge(stack_in[1 - u], (turn_no + 1 + u) * LOADS)
                        scores(1 - u, 0, g - GROUPS, False)
                    if g == AHEAD:
                        pe.wait_ge(normed[bank], m + 1)
                    values(u, bank, g - AHEAD)
                    if g == FINISH:
                        pe.wait_ge(parts_ready[1 - bank], m + 1)
                        turn(1 - bank)

            def head_pair(turn_no, u, last_pair=False):
                pe.wait_ge(v_ready[u], (turn_no + 1) * STAGED)
                pe.sem_inc(a_held, 1)
                with pe.Fori(0, NCH // 2) as r:
                    for w in range(2):
                        body(turn_no, u, r, w, last_pair)
                body(turn_no, u, NCH // 2, 0, last_pair)

            pe.wait_ge(stack_in[0], LOADS)
            for g in range(AHEAD):
                scores(0, 0, g, False)
            pe.wait_ge(cleared, 1)
            with pe.Fori(0, TURNS - 1) as turn_no:
                for u in range(SLOTS):
                    head_pair(turn_no, u)
            head_pair(TURNS - 1, 0)
            head_pair(TURNS - 1, 1, last_pair=True)
            pe.wait_ge(parts_ready[1], PAIRS * NCH // 2 + 1)
            turn(1)


def tile_sems(sem, names):
    return [[sem(f"{n}{s}") for s in range(2)] for n in names]


def route(nc, ins, t):
    ctx = ExitStack()
    with ctx:
        ctx.enter_context(nc.cleanup_on_exit())

        def sb(name, shape, dt=F32):
            return ctx.enter_context(nc.sbuf_tensor(name, shape, dt))

        def ps(name, shape, dt=F32):
            return ctx.enter_context(nc.psum_tensor(name, shape, dt))

        def sem(name):
            return nc.alloc_semaphore(name)

        h, attn, identity, wprojT, ids, moved, at_f = (t[k] for k in ("h", "attn", "identity", "wprojT", "ids", "moved", "at_f"))
        TILES = B * NT
        TURNS = TILES // CT // 2
        R = slice(0, TQ)
        SENDS = 16 * CT * TOP
        router = sb("router", [C + 1, EXPERTS])
        r_power = sb("r_power", [P, 2, CT])
        attn_c = sb("attn_c", [P, 2, CT, C])
        aT = sb("aT", [C + 1, 2, CH])
        xT = sb("xT", [C + 1, 2, CH])
        total = sb("r_total", [P, 2, CT])
        neg_mean = sb("r_neg_mean", [P, 2, CT])
        centred = sb("r_centred", [P, 2, CT, C])
        square = sb("r_square", [P, 2, CT, C])
        variance = sb("r_variance", [P, 2, CT])
        var_eps = sb("r_var_eps", [P, 2, CT])
        rstd = sb("r_rstd", [P, 2, CT])
        xn_c = sb("xn_c", [P, 2, CT, C])
        sent = sb("sent", [P, 2, CT, C])
        logits = sb("logits", [P, 2, CT, EXPERTS])
        best_c = sb("best_c", [P, 2, CT, 8])
        best_at_c = sb("best_at_c", [P, 2, CT, 8], U32)
        at_c = sb("at_c", [P, 2, CT, TOP])
        best = sb("best", [P, TILES, TOP])
        chosen = sb("chosen", [P, 2, CT, TOP, EXPERTS], BF16)
        either = sb("either", [P, 2, CT, EXPERTS], BF16)
        start = sb("start", [P, EXPERTS])
        full = sb("full", [P, 2, CT, EXPERTS])
        product = sb("product", [P, 2, CT, TOP, EXPERTS])
        slot_f = sb("slot_f", [P, 2, CT, TOP])
        slot_i = sb("slot_i", [P, 2, CT, TOP], I32)
        first_slot = sb("first_slot", [P, EXPERTS])
        ones_f = sb("ones_f", [P, P])
        before_f = sb("before_f", [P, P])
        ones_b = sb("ones_b", [P, P], BF16)
        before_b = sb("before_b", [P, P], BF16)
        nothing = sb("nothing", [P, C])
        block_ids = sb("block_ids", [P, 2])
        count = sb("count", [P, EXPERTS])
        count_i = sb("count_i", [P, 2, EXPERTS], I32)
        ends_i = sb("ends_i", [1, EXPERTS], I32)
        ends = sb("ends", [P, 2, EXPERTS])
        n_blocks = sb("n_blocks", [P, EXPERTS])
        cap_blocks = sb("cap_blocks", [P, EXPERTS])
        over = sb("over", [P, 2, EXPERTS])
        passed = sb("passed", [P, 2, EXPERTS])
        block_f = sb("block_f", [P, 2, 2])
        over_f = sb("over_f", [P, 2])
        passed_f = sb("passed_f", [P, 2])
        block_i = sb("block_i", [P, 2, 2], I32)
        gap = sb("gap", [P, TILES])
        weight2 = sb("weight2", [P, TILES])
        weight_sum = sb("weight_sum", [P, TILES])

        ps_a = ps("ps_a", [C, 512])
        ps_x = ps("ps_x", [C, 512])
        ps_p = ps("ps_p", [P, 2, 512])
        ps_l = ps("ps_l", [P, 2, 512])
        ps_r = ps("ps_r", [P, 2, 512])
        TOTALS = slice(CT * EXPERTS, (CT + 1) * EXPERTS)

        w_in, consts, held, rows_set = sem("r_w_in"), sem("r_consts"), sem("r_held"), sem("rows_set")
        staged, aT_ps, aT_done, p_ps, h_done, sum_done, mean_done, centre_done, square_done, var_done = tile_sems(sem, (
            "staged", "aT_ps", "aT_done", "p_ps", "r_h_done", "r_sum_done", "r_mean_done", "r_centre_done", "r_square_done",
            "r_var_done"))
        norm_done, xT_ps, xT_done, l_ps, logits_done, best_found, best_done = tile_sems(sem, (
            "r_norm_done", "xT_ps", "xT_done", "l_ps", "logits_done", "best_found", "best_done"))
        at_done, chosen_done, either_done, kept, ranked, full_done, product_done, slot_found, slot_done, send_ready, slot_kept = tile_sems(
            sem, ("at_done", "chosen_done", "either_done", "kept", "ranked", "full_done", "product_done", "slot_found", "slot_done",
                  "send_ready", "slot_kept"))
        scattered = [sem(f"scattered{s}") for s in range(2)]
        start_done = sem("start_done")
        eps_done, rstd_done = sem("r_eps_done"), sem("r_rstd_done")
        step, ends_done, gap_done, weight_done, blocks_out, nothing_set, tails_out, pool_tails = (
            sem(n) for n in ("step", "ends_done", "gap_done", "weight_done", "blocks_out", "nothing_set", "tails_out", "pool_tails"))

        block = ctx.enter_context(nc.Block())

        def chunk(i, s):
            return bass.ds((i * 2 + s) * CT, CT) if not isinstance(i, int) else slice((i * 2 + s) * CT, (i * 2 + s + 1) * CT)

        def turns(eng, body):
            body(0)
            with eng.Fori(1, TURNS - 1) as i:
                body(i)
            body(TURNS - 1)

        POOL_TAILS = 14
        SYNC_TAILS = (EXPERTS - POOL_TAILS) // 2

        def write_tails(eng, experts, written):
            eng.wait_ge(ends_done, 1)
            eng.wait_ge(nothing_set, 1)
            eng.sem_inc(held, 1)
            flat = t["slot_x"].rearrange("k p c -> (k p) c")
            for e in experts:
                end = eng.value_load(ends_i[0:1, e:e + 1], min_val=0, max_val=VOID * P - P)
                eng.dma_start(flat[bass.ds(end, P)], nothing[:]).then_inc(written, 16)

        @block.sync
        def _(sp):
            sp.dma_start(wprojT[C:C + 1, :], ins["L0_attn_b_proj"].unsqueeze(0)).then_inc(w_in, 16)
            sp.dma_start(router[C:C + 1, :], ins["L0_ffn_br"].unsqueeze(0)).then_inc(w_in, 16)
            write_tails(sp, range(0, SYNC_TAILS), tails_out)
            sp.wait_ge(step, BLOCK_STEPS)
            half = BLOCKS // 2
            with nc.allow_non_contiguous_dma(reason="an expert and a place for each block, once"):
                for w in range(2):
                    sp.dma_start(t["blocks"][w].rearrange("(a p) -> p a", p=half), block_i[0:half, :, w]).then_inc(blocks_out, 16)
            sp.wait_ge(blocks_out, 16 * 2)
            sp.wait_ge(tails_out, 16 * (EXPERTS - POOL_TAILS))

        @block.gpsimd
        def _(pool):
            pool.sem_inc(rstd_done, 1)
            for s in range(2):
                pool.dma_start(router[C // 2 * s:C // 2 * s + C // 2, :], ins["L0_ffn_Wr"][C // 2 * s:C // 2 * s + C // 2, :]).then_inc(scattered[s], 16)
            nc.gpsimd.memset(r_power[:], -0.5).then_inc(consts, 1)
            nc.gpsimd.iota(ids[:], [[1, EXPERTS]], base=0, channel_multiplier=0, allow_small_or_imprecise_dtypes=True).then_inc(consts, 1)
            nc.gpsimd.iota(block_ids[:], [[BLOCKS // 2, 2]], base=0, channel_multiplier=1, allow_small_or_imprecise_dtypes=True).then_inc(consts, 1)
            nc.gpsimd.memset(ones_f[:], 1.0).then_inc(consts, 1)
            pool.wait_ge(consts, 4)
            nc.gpsimd.affine_select(out=before_f[:], in_=ones_f[:], compare_op=ALU.is_gt, fill=0.0, base=0,
                                    pattern=[[1, P]], channel_multiplier=-1).then_inc(consts, 1)
            flat = t["slot_x"].rearrange("k p c -> (k p) c")

            def send(i, s):
                pool.wait_ge(slot_done[s], after(i))
                pool.wait_ge(send_ready[s], after(i))
                pool.sem_inc(held, 1)
                for x in range(CT):
                    for k in range(TOP):
                        nc.gpsimd.indirect_dma_start(
                            out=flat, out_offset=bass.IndirectOffsetOnAxis(ap=slot_i[R, s, x, k:k + 1], axis=0),
                            in_=sent[R, s, x, :], in_offset=None).then_inc(scattered[s], 16)

            def body(i):
                pool.wait_ge(eps_done, after(i))
                pool.sem_inc(held, 1)
                nc.gpsimd.tensor_tensor(out=rstd[R], in0=var_eps[R], in1=r_power[R], op=ALU.pow).then_inc(rstd_done, 1)
                if not (isinstance(i, int) and i == 0):
                    for s in range(2):
                        send(i - 1, s)
            turns(pool, body)
            for s in range(2):
                send(TURNS - 1, s)
            write_tails(pool, range(EXPERTS - POOL_TAILS, EXPERTS), pool_tails)
            for s in range(2):
                pool.wait_ge(scattered[s], 16 + SENDS * TURNS)
            pool.wait_ge(pool_tails, 16 * POOL_TAILS)

        @block.scalar
        def _(act):
            for s in range(2):
                for w in (staged, aT_done, square_done, xT_done, logits_done, kept, send_ready, slot_kept):
                    act.sem_inc(w[s], 1)
            nc.scalar.preload_act_table(ACT.Exp)

            def stage(i, s):
                act.wait_ge(aT_ps[s], before(i))
                nc.scalar.copy(attn_c[R, s], attn[R, chunk(i, s), :]).then_inc(staged[s], 1)

            def turned(i, s):
                act.wait_ge(aT_ps[s], after(i))
                act.wait_ge(p_ps[s], before(i))
                nc.scalar.copy(aT[0:C, s], ps_a[:, 0:CH]).then_inc(aT_done[s], 1)

            def to_send(i, s):
                act.wait_ge(norm_done[s], after(i))
                act.wait_ge(scattered[s], 16 + SENDS * i)
                nc.scalar.copy(sent[R, s], xn_c[R, s]).then_inc(send_ready[s], 1)
                act.wait_ge(slot_done[s], after(i))
                nc.scalar.copy(t["slots"][R, chunk(i, s), :], slot_i[R, s]).then_inc(slot_kept[s], 1)

            for s in range(2):
                stage(0, s)
            for s in range(2):
                turned(0, s)

            def body(i):
                first, last = (isinstance(i, int) and i == n for n in (0, TURNS - 1))
                if not last:
                    for s in range(2):
                        stage(i + 1, s)
                for s in range(2):
                    act.wait_ge(centre_done[s], after(i))
                    act.wait_ge(var_done[s], before(i))
                    nc.scalar.activation(square[R, s], centred[R, s], ACT.Square).then_inc(square_done[s], 1)
                if not first:
                    for s in range(2):
                        to_send(i - 1, s)
                for s in range(2):
                    act.wait_ge(xT_ps[s], after(i))
                    act.wait_ge(l_ps[s], before(i))
                    nc.scalar.copy(xT[0:C, s], ps_x[:, 0:CH]).then_inc(xT_done[s], 1)
                for s in range(2):
                    act.wait_ge(l_ps[s], after(i))
                    act.wait_ge(best_done[s], before(i))
                    nc.scalar.copy(logits[R, s].rearrange("p i e -> p (i e)"), ps_l[R, s, 0:CT * EXPERTS]).then_inc(logits_done[s], 1)
                if not last:
                    for s in range(2):
                        turned(i + 1, s)
                for s in range(2):
                    act.wait_ge(best_found[s], after(i))
                    nc.scalar.copy(best[R, chunk(i, s), :], best_c[R, s, :, 0:TOP])
                    act.wait_ge(at_done[s], after(i))
                    nc.scalar.copy(at_f[R, chunk(i, s), :], at_c[R, s]).then_inc(kept[s], 1)
            turns(act, body)
            for s in range(2):
                to_send(TURNS - 1, s)
            write_tails(act, range(SYNC_TAILS, EXPERTS - POOL_TAILS), tails_out)
            act.wait_ge(gap_done, 1)
            nc.scalar.activation(weight2[R], gap[R], ACT.Exp).then_inc(weight_done, 1)

        @block.vector
        def _(dve):
            for s in range(2):
                for w in (h_done, sum_done, mean_done, centre_done, var_done, norm_done, best_found, best_done, at_done, chosen_done,
                          either_done, full_done, product_done, slot_found, slot_done):
                    dve.sem_inc(w[s], 1)
            dve.sem_inc(eps_done, 1)
            nc.vector.memset(nothing[:], 0.0).then_inc(nothing_set, 1)
            nc.vector.memset(aT[C:C + 1], 1.0).then_inc(rows_set, 1)
            nc.vector.memset(xT[C:C + 1], 1.0).then_inc(rows_set, 1)
            dve.wait_ge(consts, 5)
            nc.vector.tensor_copy(ones_b[:], ones_f[:]).then_inc(rows_set, 1)
            nc.vector.tensor_copy(before_b[:], before_f[:]).then_inc(rows_set, 1)
            nc.vector.tensor_scalar(cap_blocks[:], ids[:], float(CAP_BLOCKS), None, ALU.mult).then_inc(rows_set, 1)
            nc.vector.tensor_scalar(first_slot[:], ids[:], float(CAP_BLOCKS * P), None, ALU.mult).then_inc(rows_set, 1)
            nc.vector.tensor_scalar(start[:], ids[:], float(CAP_BLOCKS * P), None, ALU.mult).then_inc(start_done, 1)

            def wide(x):
                return x.unsqueeze(2).to_broadcast([TQ, CT, C])

            def place(i):
                for s in range(2):
                    dve.wait_ge(ranked[s], after(i))
                    dve.wait_ge(start_done, i * 2 + s + 1)
                    nc.vector.tensor_tensor(full[R, s], ps_r[R, s, 0:CT * EXPERTS].rearrange("p (i e) -> p i e", e=EXPERTS),
                                            start[R].unsqueeze(1).to_broadcast([TQ, CT, EXPERTS]), ALU.add).then_inc(full_done[s], 1)
                    dve.wait_ge(full_done[s], after(i))
                    nc.vector.tensor_tensor(start[R], start[R], ps_r[R, s, TOTALS], ALU.add).then_inc(start_done, 1)
                    nc.vector.tensor_tensor(product[R, s], chosen[R, s], full[R, s].unsqueeze(2).to_broadcast([TQ, CT, TOP, EXPERTS]),
                                            ALU.mult).then_inc(product_done[s], 1)
                for s in range(2):
                    dve.wait_ge(product_done[s], after(i))
                    nc.vector.tensor_reduce(slot_f[R, s], product[R, s], AX.X, ALU.add).then_inc(slot_found[s], 1)
                for s in range(2):
                    dve.wait_ge(slot_found[s], after(i))
                    dve.wait_ge(scattered[s], 16 + SENDS * i)
                    dve.wait_ge(slot_kept[s], before(i))
                    nc.vector.tensor_copy(slot_i[R, s], slot_f[R, s]).then_inc(slot_done[s], 1)

            def body(i):
                for s in range(2):
                    tok = h[R, chunk(i, s), :]
                    dve.wait_ge(p_ps[s], after(i))
                    nc.vector.tensor_tensor(tok, tok, ps_p[R, s, 0:CT * C].rearrange("p (i e) -> p i e", e=C), ALU.add).then_inc(h_done[s], 1)
                for s in range(2):
                    dve.wait_ge(h_done[s], after(i))
                    dve.sem_inc(held, 1)
                    nc.vector.tensor_reduce(total[R, s], h[R, chunk(i, s), :], AX.X, ALU.add).then_inc(sum_done[s], 1)
                for s in range(2):
                    dve.wait_ge(sum_done[s], after(i))
                    nc.vector.tensor_scalar(neg_mean[R, s], total[R, s], -1.0 / C, None, ALU.mult).then_inc(mean_done[s], 1)
                for s in range(2):
                    dve.wait_ge(mean_done[s], after(i))
                    nc.vector.tensor_tensor(centred[R, s], h[R, chunk(i, s), :], wide(neg_mean[R, s]), ALU.add).then_inc(centre_done[s], 1)
                for s in range(2):
                    dve.wait_ge(square_done[s], after(i))
                    dve.sem_inc(held, 1)
                    nc.vector.tensor_reduce(variance[R, s], square[R, s], AX.X, ALU.add).then_inc(var_done[s], 1)
                for s in range(2):
                    dve.wait_ge(var_done[s], after(i))
                dve.wait_ge(rstd_done, before(i))
                nc.vector.tensor_scalar(var_eps[R], variance[R], 1.0 / C, EPS, ALU.mult, ALU.add).then_inc(eps_done, 1)
                if not (isinstance(i, int) and i == 0):
                    place(i - 1)
                dve.wait_ge(rstd_done, after(i))
                for s in range(2):
                    dve.wait_ge(xT_ps[s], before(i))
                    dve.wait_ge(send_ready[s], before(i))
                    nc.vector.tensor_tensor(xn_c[R, s], centred[R, s], wide(rstd[R, s]), ALU.mult).then_inc(norm_done[s], 1)
                for s in range(2):
                    dve.wait_ge(logits_done[s], after(i))
                    dve.wait_ge(kept[s], before(i))
                    dve.sem_inc(held, 1)
                    for x in range(CT):
                        last = nc.vector.max(best_c[R, s, x, :], logits[R, s, x, :])
                    last.then_inc(best_found[s], 1)
                for s in range(2):
                    dve.wait_ge(best_found[s], after(i))
                    dve.sem_inc(held, 1)
                    for x in range(CT):
                        last = nc.vector.max_index(best_at_c[R, s, x, :], best_c[R, s, x, :], logits[R, s, x, :])
                    last.then_inc(best_done[s], 1)
                for s in range(2):
                    dve.wait_ge(best_done[s], after(i))
                    nc.vector.tensor_copy(at_c[R, s], best_at_c[R, s, :, 0:TOP]).then_inc(at_done[s], 1)
                for s in range(2):
                    whole = [TQ, CT * TOP, EXPERTS]
                    dve.wait_ge(at_done[s], after(i))
                    nc.vector.tensor_tensor(chosen[R, s].rearrange("p i k e -> p (i k) e"), ids[R].unsqueeze(1).to_broadcast(whole),
                                            at_c[R, s].rearrange("p i k -> p (i k)").unsqueeze(2).to_broadcast(whole), ALU.is_equal
                                            ).then_inc(chosen_done[s], 1)
                for s in range(2):
                    dve.wait_ge(chosen_done[s], after(i))
                    nc.vector.tensor_tensor(either[R, s], chosen[R, s, :, 0, :], chosen[R, s, :, 1, :], ALU.add).then_inc(either_done[s], 1)
            turns(dve, body)
            place(TURNS - 1)

            done = [0]

            def then(instruction):
                done[0] += 1
                instruction.then_inc(step, 1)
                dve.wait_ge(step, done[0])

            dve.wait_ge(start_done, 2 * TURNS + 1)
            dve.wait_ge(rows_set, 6)
            nc.vector.tensor_copy(ends_i[:], start[0:1]).then_inc(ends_done, 1)
            then(nc.vector.tensor_tensor(count[R], start[R], first_slot[R], ALU.subtract))
            then(nc.vector.tensor_scalar(count[R], count[R], float(P - 1), None, ALU.add))
            then(nc.vector.tensor_copy(count_i[R, 0], count[R]))
            then(nc.vector.tensor_scalar(count_i[R, 1], count_i[R, 0], 7, None, ALU.arith_shift_right))
            then(nc.vector.tensor_copy(n_blocks[R], count_i[R, 1]))
            then(nc.vector.tensor_copy(ends[R, 0], n_blocks[R]))
            src, width = 0, 1
            while width < EXPERTS:
                then(nc.vector.tensor_copy(ends[R, 1 - src, 0:width], ends[R, src, 0:width]))
                then(nc.vector.tensor_tensor(ends[R, 1 - src, width:], ends[R, src, width:], ends[R, src, 0:EXPERTS - width], ALU.add))
                src, width = 1 - src, 2 * width
            H2 = slice(0, BLOCKS // 2)
            for a in range(2):
                then(nc.vector.tensor_scalar(over[H2, a], ends[H2, src], block_ids[H2, a:a + 1], None, ALU.is_le))
            then(nc.vector.tensor_tensor(passed[H2], over[H2], n_blocks[H2].unsqueeze(1).to_broadcast([BLOCKS // 2, 2, EXPERTS]), ALU.mult))
            then(nc.vector.tensor_reduce(over_f[H2], over[H2], AX.X, ALU.add))
            then(nc.vector.tensor_reduce(passed_f[H2], passed[H2], AX.X, ALU.add))
            then(nc.vector.tensor_scalar(block_f[H2, :, 0], over_f[H2], float(EXPERTS - 1), None, ALU.min))
            then(nc.vector.scalar_tensor_tensor(out=block_f[H2, :, 1], in0=over_f[H2], scalar=float(CAP_BLOCKS), in1=block_ids[H2],
                                                op0=ALU.mult, op1=ALU.add))
            then(nc.vector.tensor_tensor(block_f[H2, :, 1], block_f[H2, :, 1], passed_f[H2], ALU.subtract))
            then(nc.vector.tensor_copy(block_i[H2], block_f[H2]))
            assert done[0] == BLOCK_STEPS, done[0]
            then(nc.vector.tensor_tensor(moved[R], ends[R, src], n_blocks[R], ALU.subtract))
            then(nc.vector.tensor_tensor(moved[R], moved[R], cap_blocks[R], ALU.subtract))
            gates = t["gates"]
            for s in range(2):
                dve.wait_ge(kept[s], after(TURNS - 1))
            nc.vector.tensor_tensor(gap[R], best[R, :, 1], best[R, :, 0], ALU.subtract).then_inc(gap_done, 1)
            dve.wait_ge(weight_done, 1)
            then(nc.vector.tensor_scalar(weight_sum[R], weight2[R], 1.0, None, ALU.add))
            then(nc.vector.reciprocal(gates[R, :, 0], weight_sum[R]))
            then(nc.vector.tensor_tensor(gates[R, :, 1], weight2[R], gates[R, :, 0], ALU.mult))

        @block.tensor
        def _(pe):
            for s in range(2):
                for w in (aT_ps, p_ps, xT_ps, l_ps, ranked):
                    pe.sem_inc(w[s], 1)
            pe.wait_ge(w_in, 32)
            pe.wait_ge(rows_set, 4)
            for s in range(2):
                pe.wait_ge(scattered[s], 16)

            def project(i):
                for s in range(2):
                    pe.wait_ge(staged[s], after(i))
                    pe.wait_ge(aT_done[1 - s], after(i) if s else before(i))
                    pe.sem_inc(held, 1)
                    for x in range(CT):
                        last = nc.tensor.transpose(ps_a[:, TQ * x:TQ * x + TQ], attn_c[R, s, x, :], identity[R, R])
                    last.then_inc(aT_ps[s], 1)
                for s in range(2):
                    pe.wait_ge(aT_done[s], after(i))
                    pe.wait_ge(h_done[s], before(i))
                    pe.sem_inc(held, 1)
                    for x in range(CT):
                        last = nc.tensor.matmul(ps_p[R, s, C * x:C * x + C], aT[:, s, TQ * x:TQ * x + TQ], wprojT[:],
                                                start=True, stop=True)
                    last.then_inc(p_ps[s], 1)

            project(0)

            def body(i):
                for s in range(2):
                    pe.wait_ge(norm_done[s], after(i))
                    pe.wait_ge(xT_done[1 - s], after(i) if s else before(i))
                    pe.sem_inc(held, 1)
                    for x in range(CT):
                        last = nc.tensor.transpose(ps_x[:, TQ * x:TQ * x + TQ], xn_c[R, s, x, :], identity[R, R])
                    last.then_inc(xT_ps[s], 1)
                for s in range(2):
                    pe.wait_ge(xT_done[s], after(i))
                    pe.wait_ge(logits_done[s], before(i))
                    pe.sem_inc(held, 1)
                    for x in range(CT):
                        last = nc.tensor.matmul(ps_l[R, s, EXPERTS * x:EXPERTS * x + EXPERTS], xT[:, s, TQ * x:TQ * x + TQ], router[:],
                                                start=True, stop=True)
                    last.then_inc(l_ps[s], 1)
                if not (isinstance(i, int) and i == TURNS - 1):
                    project(i + 1)
                for s in range(2):
                    pe.wait_ge(either_done[s], after(i))
                    if not (isinstance(i, int) and i == 0):
                        pe.wait_ge(start_done, i * 2 + s)
                    pe.wait_ge(full_done[s], before(i))
                    pe.sem_inc(held, 1)
                    for x in range(CT):
                        at = ps_r[R, s, EXPERTS * x:EXPERTS * x + EXPERTS]
                        nc.tensor.matmul(at, before_b[R, R], either[R, s, x, :], start=True, stop=x == 0)
                        for y in range(x):
                            nc.tensor.matmul(at, ones_b[R, R], either[R, s, y, :], start=False, stop=y == x - 1)
                    for x in range(CT):
                        last = nc.tensor.matmul(ps_r[R, s, TOTALS], ones_b[R, R], either[R, s, x, :], start=x == 0, stop=x == CT - 1)
                    last.then_inc(ranked[s], 1)
            turns(pe, body)


def run_experts(nc, ins, t):
    ctx = ExitStack()
    with ctx:
        ctx.enter_context(nc.cleanup_on_exit())

        def sb(name, shape, dt=F32):
            return ctx.enter_context(nc.sbuf_tensor(name, shape, dt))

        def ps(name, shape, dt=F32):
            return ctx.enter_context(nc.psum_tensor(name, shape, dt))

        def sem(name):
            return nc.alloc_semaphore(name)

        G = 4
        SLOTS = 4
        assert G * SLOTS == SPARE
        TURNS = BLOCKS // G // SLOTS
        block_row = sb("block_row", [1, 2, BLOCKS], I32)
        xs = sb("xs", [P, SLOTS, G, C])
        pack = sb("pack", [P, SLOTS, G, PACK])
        xsT = sb("xsT", [C + 1, 2, G * P])
        hidT = sb("hidT", [P, 2, G * P])
        ys = sb("ys", [P, 2, G, C])
        ones3 = sb("ones3", [P, P], BF16)
        identity = t["identity"]
        ps_x = ps("e_ps_x", [C, 2, 512])
        ps_h = ps("e_ps_h", [P, 2, 512])
        ps_y = ps("e_ps_y", [P, 2, 512])

        row_in, ones_done, held = (sem(n) for n in ("row_in", "ones_done", "e_held"))
        x_in = [sem(f"e_x_in{s}") for s in range(SLOTS)]
        pack_in = [sem(f"pack_in{s}") for s in range(SLOTS)]
        pack_in_act = [sem(f"pack_in_act{s}") for s in range(SLOTS)]
        POOL_SHARE = G - 1
        y_out = [sem(f"y_out{s}") for s in range(2)]
        xT_ps, xT_done, h_ps, h_done, y_ps, y_done = (sem(n) for n in ("e_xT_ps", "e_xT_done", "h_ps", "e_h_done", "y_ps", "y_done"))
        FIRST = SLOTS + 1
        MOVE_TURNS = TURNS * 3 // 4
        PIECE = B * NT * TOP // (MOVE_TURNS * SLOTS)
        assert PIECE * MOVE_TURNS * SLOTS == B * NT * TOP
        is_its = sb("is_its", [P, PIECE, EXPERTS])
        its_move = sb("its_move", [P, PIECE, EXPERTS])
        moves = sb("moves", [P, B * NT * TOP])
        place_i = sb("place_i", [P, 2, B * NT * TOP], I32)
        place_f = sb("place_f", [P, 2, B * NT * TOP])
        matched, taken, moved = sem("matched"), sem("taken"), sem("moved_done")
        row_steps = sem("row_steps")

        block = ctx.enter_context(nc.Block())

        def any_left(eng):
            eng.wait_ge(row_in, 16)
            eng.sem_inc(held, 1)
            first = (TURNS - 1) * SLOTS * G
            return eng.value_load(block_row[0:1, 1, first:first + 1], min_val=0, max_val=VOID + BLOCKS - 1) < VOID

        def made(i, g):
            return i * SLOTS + g + 1 + FIRST

        def load_weights(eng, i, s, blocks, loaded):
            eng.wait_ge(y_ps, made(i, s - SLOTS))
            eng.sem_inc(held, 1)
            for x in blocks:
                expert = eng.value_load(block_row[0:1, 0, bass.ds((i * SLOTS + s) * G + x, 1)], min_val=0, max_val=EXPERTS - 1)
                eng.dma_start(pack[:, s, x], t["weights"][bass.ds(expert, 1)].rearrange("a p n -> p (a n)")).then_inc(loaded[s], 16)

        @block.gpsimd
        def _(pool):
            pool.wait_ge(row_in, 16)
            pool.sem_inc(held, 1)

            def weights(i):
                for s in range(SLOTS):
                    load_weights(pool, i, s, range(POOL_SHARE), pack_in)

            with pool.Fori(0, TURNS - 1) as i:
                weights(i)
            with pool.If(any_left(pool)):
                weights(TURNS - 1)

        @block.sync
        def _(sp):
            for s in range(2):
                sp.sem_inc(y_out[s], 16)
            sp.dma_start(block_row[:], t["blocks"].rearrange("(a w) k -> a w k", a=1)).then_inc(row_in, 16)
            sp.wait_ge(row_in, 16)
            sp.sem_inc(held, 1)

            def rows(i):
                for s in range(SLOTS):
                    sp.wait_ge(xT_ps, made(i, s - SLOTS))
                    sp.sem_inc(held, 1)
                    for x in range(G):
                        place = sp.value_load(block_row[0:1, 1, bass.ds((i * SLOTS + s) * G + x, 1)], min_val=0, max_val=VOID + BLOCKS - 1)
                        sp.dma_start(xs[:, s, x], t["slot_x"][bass.ds(place, 1)].rearrange("a p c -> p (a c)")).then_inc(x_in[s], 16)

            with sp.Fori(0, TURNS - 1) as i:
                rows(i)
            for s in range(2):
                sp.wait_ge(y_out[s], 16 * (2 * (TURNS - 1) + 1))
            with sp.If(any_left(sp)):
                rows(TURNS - 1)
                for s in range(2):
                    sp.wait_ge(y_out[s], 16 * (2 * TURNS + 1))

        @block.scalar
        def _(act):
            act.sem_inc(xT_done, FIRST)
            act.sem_inc(y_done, FIRST)

            def rows(i, g):
                act.wait_ge(xT_ps, made(i, g))
                act.wait_ge(h_ps, made(i, g - 2))
                nc.scalar.copy(xsT[0:C, g % 2], ps_x[:, g % 2]).then_inc(xT_done, 1)

            def outputs(i, y):
                act.wait_ge(y_ps, made(i, y))
                act.wait_ge(y_out[y % 2], 16 * (i * 2 + y // 2 + 1))
                nc.scalar.copy(ys[:, y % 2].rearrange("p g c -> p (g c)"), ps_y[:, y % 2, 0:G * C]).then_inc(y_done, 1)
                act.wait_ge(y_done, made(i, y))
                act.dma_start(t["slot_y"][:, bass.ds((i * SLOTS + y) * G, G), :], ys[:, y % 2]).then_inc(y_out[y % 2], 16)

            def groups(i, last):
                for g in range(SLOTS):
                    if g + 1 < SLOTS:
                        rows(i, g + 1)
                    elif not last:
                        rows(i + 1, 0)
                    if g > 0:
                        outputs(i, g - 1)
                        if not last:
                            weights(i + 1, g - 1)
                outputs(i, SLOTS - 1)
                if not last:
                    weights(i + 1, SLOTS - 1)

            def weights(i, g):
                load_weights(act, i, g, range(POOL_SHARE, G), pack_in_act)

            act.wait_ge(row_in, 16)
            act.sem_inc(held, 1)
            for g in range(SLOTS):
                weights(0, g)
            rows(0, 0)
            with act.Fori(0, TURNS - 2) as i:
                groups(i, False)
            groups(TURNS - 2, True)
            with act.If(any_left(act)):
                for g in range(SLOTS):
                    weights(TURNS - 1, g)
                rows(TURNS - 1, 0)
                groups(TURNS - 1, True)

        @block.vector
        def _(dve):
            dve.sem_inc(h_done, FIRST)
            R = slice(0, TQ)
            at_flat = t["at_f"][R].rearrange("p i k -> p (i k)")
            nc.vector.memset(ones3[:], 1.0).then_inc(ones_done, 1)
            nc.vector.memset(xsT[B1_ROW:B1_ROW + 1], 1.0).then_inc(ones_done, 1)

            def hidden(i, g):
                dve.wait_ge(h_ps, made(i, g))
                dve.wait_ge(y_ps, made(i, g - 2))
                nc.vector.tensor_scalar(hidT[:, g % 2], ps_h[:, g % 2], 0.0, None, ALU.max).then_inc(h_done, 1)

            with dve.Fori(0, MOVE_TURNS) as i:
                for g in range(SLOTS):
                    hidden(i, g)
                    n = dve.snap(i * SLOTS + g)
                    whole = [TQ, PIECE, EXPERTS]
                    nc.vector.tensor_tensor(is_its[R], t["ids"][R].unsqueeze(1).to_broadcast(whole),
                                            at_flat[:, bass.ds(n * PIECE, PIECE)].unsqueeze(2).to_broadcast(whole), ALU.is_equal).then_inc(matched, 1)
                    dve.wait_ge(matched, n + 1)
                    nc.vector.tensor_tensor(its_move[R], is_its[R], t["moved"][R].unsqueeze(1).to_broadcast(whole), ALU.mult).then_inc(taken, 1)
                    dve.wait_ge(taken, n + 1)
                    dve.sem_inc(held, 1)
                    nc.vector.tensor_reduce(moves[R, bass.ds(n * PIECE, PIECE)], its_move[R], AX.X, ALU.add).then_inc(moved, 1)
            with dve.Fori(MOVE_TURNS, TURNS - 1) as i:
                for g in range(SLOTS):
                    hidden(i, g)
            with dve.If(any_left(dve)):
                for g in range(SLOTS):
                    hidden(TURNS - 1, g)
            dve.wait_ge(moved, MOVE_TURNS * SLOTS)
            slots = t["slots"][R].rearrange("p i k -> p (i k)")
            nc.vector.tensor_scalar(place_i[R, 0], slots, P - 1, None, ALU.bitwise_and).then_inc(row_steps, 1)
            nc.vector.tensor_scalar(place_i[R, 1], slots, 7, None, ALU.arith_shift_right).then_inc(row_steps, 1)
            dve.wait_ge(row_steps, 2)
            for k in range(2):
                nc.vector.tensor_copy(place_f[R, k], place_i[R, k]).then_inc(row_steps, 1)
            dve.wait_ge(row_steps, 4)
            nc.vector.tensor_tensor(place_f[R, 1], place_f[R, 1], moves[R], ALU.add).then_inc(row_steps, 1)
            dve.wait_ge(row_steps, 5)
            nc.vector.scalar_tensor_tensor(out=place_f[R, 0], in0=place_f[R, 0], scalar=float(BLOCKS), in1=place_f[R, 1],
                                           op0=ALU.mult, op1=ALU.add).then_inc(row_steps, 1)
            dve.wait_ge(row_steps, 6)
            nc.vector.tensor_copy(t["rows"][R].rearrange("p i k -> p (i k)"), place_f[R, 0]).then_inc(row_steps, 1)

        @block.tensor
        def _(pe):
            for w in (xT_ps, h_ps, y_ps):
                pe.sem_inc(w, FIRST)

            def turn(i, g):
                pe.wait_ge(x_in[g], 16 * G * i + 16 * G)
                pe.wait_ge(xT_done, made(i, g - 2))
                pe.sem_inc(held, 1)
                for x in range(G):
                    last = nc.tensor.transpose(ps_x[:, g % 2, P * x:P * x + P], xs[:, g, x, :], identity[:])
                last.then_inc(xT_ps, 1)

            def hidden(i, g):
                pe.wait_ge(pack_in[g], 16 * POOL_SHARE * i + 16 * POOL_SHARE)
                pe.wait_ge(pack_in_act[g], 16 * (G - POOL_SHARE) * i + 16 * (G - POOL_SHARE))
                pe.wait_ge(xT_done, made(i, g))
                pe.wait_ge(h_done, made(i, g - 2))
                pe.sem_inc(held, 1)
                for x in range(G):
                    last = nc.tensor.matmul(ps_h[:, g % 2, P * x:P * x + P], pack[0:C + 1, g, x, 0:HID], xsT[:, g % 2, P * x:P * x + P],
                                            start=True, stop=True)
                last.then_inc(h_ps, 1)

            def outputs(i, g):
                pe.wait_ge(h_done, made(i, g))
                pe.wait_ge(y_done, made(i, g - 2))
                pe.sem_inc(held, 1)
                for x in range(G):
                    y = ps_y[:, g % 2, C * x:C * x + C]
                    nc.tensor.matmul(y, hidT[:, g % 2, P * x:P * x + P], pack[:, g, x, HID:PACK], start=True, stop=False)
                    b2 = pack[B2_ROW:B2_ROW + PARTS, g, x, 0:C // 2].bitcast(BF16)
                    last = nc.tensor.matmul(y, ones3[B2_ROW:B2_ROW + PARTS, :], b2, start=False, stop=True)
                last.then_inc(y_ps, 1)

            def groups(i, last):
                for g in range(SLOTS):
                    if g + 1 < SLOTS:
                        turn(i, g + 1)
                    elif not last:
                        turn(i + 1, 0)
                    hidden(i, g)
                    if g > 0:
                        outputs(i, g - 1)
                outputs(i, SLOTS - 1)

            pe.wait_ge(ones_done, 2)
            turn(0, 0)
            with pe.Fori(0, TURNS - 2) as i:
                groups(i, False)
            groups(TURNS - 2, True)
            with pe.If(any_left(pe)):
                turn(TURNS - 1, 0)
                groups(TURNS - 1, True)


def combine(nc, t, out):
    ctx = ExitStack()
    with ctx:
        ctx.enter_context(nc.cleanup_on_exit())

        def sb(name, shape, dt=F32):
            return ctx.enter_context(nc.sbuf_tensor(name, shape, dt))

        def sem(name):
            return nc.alloc_semaphore(name)

        TILES = B * NT
        CHUNKS = TILES // CT
        got = sb("got", [P, TILES, TOP, C])
        part = sb("part", [P, CHUNKS, TOP, CT, C])
        h, gates = t["h"], t["gates"]
        got_in = [sem(f"got_in{n}") for n in range(CHUNKS)]
        scaled, summed, h_ready, stored = (sem(n) for n in ("c_scaled", "c_summed", "h_ready", "stored"))
        CLS_ROW = PATCHES - (NT - 1) * TQ

        block = ctx.enter_context(nc.Block())

        @block.gpsimd
        def _(pool):
            rows_y = t["slot_y"].rearrange("p k c -> (p k) c")
            for i in range(TILES):
                for k in range(TOP):
                    nc.gpsimd.indirect_dma_start(
                        out=got[0:TQ, i, k, :], out_offset=None, in_=rows_y,
                        in_offset=bass.IndirectOffsetOnAxis(ap=t["rows"][0:TQ, i, k:k + 1], axis=0)).then_inc(got_in[i // CT], 16)

        @block.vector
        def _(dve):
            for n in range(CHUNKS):
                dve.wait_ge(got_in[n], 16 * TOP * CT)
                for k in range(TOP):
                    nc.vector.tensor_tensor(part[0:TQ, n, k], got[0:TQ, n * CT:n * CT + CT, k, :],
                                            gates[0:TQ, n * CT:n * CT + CT, k:k + 1].to_broadcast([TQ, CT, C]), ALU.mult).then_inc(scaled, 1)
                dve.wait_ge(scaled, 2 * n + 2)
                nc.vector.tensor_tensor(part[0:TQ, n, 0], part[0:TQ, n, 0], part[0:TQ, n, 1], ALU.add).then_inc(summed, 1)
                dve.wait_ge(summed, n + 1)
                tok = h[0:TQ, n * CT:n * CT + CT, :]
                nc.vector.tensor_tensor(tok, tok, part[0:TQ, n, 0], ALU.add).then_inc(h_ready, 1)

        @block.sync
        def _(sp):
            stores = 0
            for n in range(CHUNKS):
                b, c = divmod(n, NCH)
                sp.wait_ge(h_ready, n + 1)
                full = CT if c < NCH - 1 else CT - 1
                at = 1 + c * CH
                sp.dma_start(out[b, at:at + full * TQ, :].rearrange("(i p) e -> p i e", p=TQ),
                             h[0:TQ, n * CT:n * CT + full, :]).then_inc(stored, 16)
                stores += 1
                if full < CT:
                    sp.dma_start(out[b, at + full * TQ:N, :], h[0:CLS_ROW, n * CT + full, :]).then_inc(stored, 16)
                    sp.dma_start(out[b, 0:1, :], h[CLS_ROW:CLS_ROW + 1, n * CT + full, :]).then_inc(stored, 16)
                    stores += 2
            sp.wait_ge(stored, 16 * stores)


_INS = ["x", "cls_tok", "L0_tok_bases", "L0_tok_W_spline", "L0_tok_b_spline", "L0_tok_W_base", "L0_tok_b_base",
        "L0_attn_w_qkv", "L0_attn_w_proj", "L0_attn_b_proj", "L0_attn_rel_table", "L0_attn_rel_index",
        "L0_ffn_Wr", "L0_ffn_br", "L0_ffn_W1", "L0_ffn_b1", "L0_ffn_W2", "L0_ffn_b2"]


def kernel(**inputs):
    import numpy as np
    import concourse.bacc as bacc
    from concourse.bass_utils import run_bass_kernel_spmd

    nc = bacc.Bacc("TRN2", target_bir_lowering=False, num_devices=1)
    arrays, aps = {}, {}
    for name in _INS:
        a = np.ascontiguousarray(inputs[name])
        arrays[f"in_{name}"] = a
        aps[name] = nc.dram_tensor(f"in_{name}", a.shape, mybir.dt.from_np(a.dtype), kind="ExternalInput").ap()
    out = nc.dram_tensor("out_tokens", (B, N, C), F32, kind="ExternalOutput").ap()
    vit_layer(nc, aps, out)
    r = run_bass_kernel_spmd(nc, [arrays], core_ids=[0])
    return r.results[0]["out_tokens"]
```
